# Optimizing a Trainium2 kernel written in Bass

```python
import numpy as np
import jax
import jax.numpy as jnp

def _softmax(x, axis=-1):
    return jax.nn.softmax(x, axis=axis)
def _gelu(x):
    return jax.nn.gelu(x, approximate=True)
def _silu(x):
    return jax.nn.silu(x)
def _sigmoid(x):
    return jax.nn.sigmoid(x)
def _layernorm(x, axis=-1, eps=1e-5):
    m = jnp.mean(x, axis=axis, keepdims=True)
    v = jnp.var(x, axis=axis, keepdims=True)
    return (x - m) / jnp.sqrt(v + eps)
def _scatter_add(tgt, idx, src, axis=0):
    return tgt.at[idx].add(src)
def _segment_sum(src, seg, n):
    return jax.ops.segment_sum(src, seg, n)

kernel_name = 'mk_metaformer_d1_conv_nchw256_577589'

def setup_inputs(seed: int = 0):
    np.random.seed(seed)
    _w = jnp.asarray
    def _rec_inputs():
        import jax
        import jax.numpy as jnp
        _gk = jax.random.key(seed)
        x = 7.22e-05 + 1 * jax.random.normal(jax.random.fold_in(_gk, 1), (8, 256, 64, 64), jnp.float32)
        return x
    x = _rec_inputs()
    def _L0_conv_setup():
        import jax, jax.numpy as jnp
        import numpy as np
        IN_CH = 256
        OUT_CH = 256
        DIM = 8
        HEADS = IN_CH // DIM
        TOTAL = HEADS * DIM
        SCALE = 5
        EPS = 1e-15
        BN_EPS = 1e-05

        def conv2d(x, w, padding=0, groups=1):
            return jax.lax.conv_general_dilated(x, w, window_strides=(1, 1), padding=[(padding, padding), (padding, padding)], feature_group_count=groups, dimension_numbers=('NCHW', 'OIHW', 'NCHW'))

        def relu_linear_att(qkv):
            B, C, H, W = qkv.shape
            N = H * W
            G = C // (3 * DIM)
            qkv = qkv.astype(jnp.float32).reshape(B, G, 3 * DIM, N)
            q = jax.nn.relu(qkv[:, :, :DIM])
            k = jax.nn.relu(qkv[:, :, DIM:2 * DIM])
            v = qkv[:, :, 2 * DIM:]
            ones = jnp.ones((B, G, 1, N), qkv.dtype)
            v = jnp.concatenate([v, ones], axis=2)
            vk = jnp.einsum('bgdn,bgen->bgde', v, k)
            out = jnp.einsum('bgde,bgen->bgdn', vk, q)
            out = out[:, :, :DIM] / (out[:, :, DIM:] + EPS)
            return out.reshape(B, G * DIM, H, W)
        key = jax.random.key(seed)
        ks = jax.random.split(key, 8)
        B, H, W = (8, 64, 64)
        x = jax.random.normal(ks[0], (B, IN_CH, H, W), dtype=jnp.float32)
        w_qkv = jax.random.normal(ks[1], (3 * TOTAL, IN_CH, 1, 1), jnp.float32) * 0.05
        w_dw = jax.random.normal(ks[2], (3 * TOTAL, 1, SCALE, SCALE), jnp.float32) * 0.05
        w_pw = jax.random.normal(ks[3], (3 * TOTAL, DIM, 1, 1), jnp.float32) * 0.05
        w_proj = jax.random.normal(ks[4], (OUT_CH, 2 * TOTAL, 1, 1), jnp.float32) * 0.05
        bn_gamma = jnp.ones((OUT_CH,), jnp.float32)
        bn_beta = jnp.zeros((OUT_CH,), jnp.float32)
        bn_mean = jax.random.normal(ks[5], (OUT_CH,), jnp.float32) * 0.1
        bn_var = jax.random.uniform(ks[6], (OUT_CH,), jnp.float32, 0.5, 1.5)
        return {'x': x, 'w_qkv': w_qkv, 'w_dw': w_dw, 'w_pw': w_pw, 'w_proj': w_proj, 'bn_gamma': bn_gamma, 'bn_beta': bn_beta, 'bn_mean': bn_mean, 'bn_var': bn_var}
    _L0_conv_all = _L0_conv_setup()
    _L0_conv_in = {k: v for k, v in _L0_conv_all.items() if k in ('w_qkv', 'w_dw', 'w_pw', 'w_proj', 'bn_gamma', 'bn_beta', 'bn_mean', 'bn_var', )}
    del _L0_conv_all

    def _L0_ffn_setup():
        import math
        import jax, jax.numpy as jnp
        import numpy as np
        CAPACITY_FACTOR = 1.25
        key = jax.random.key(seed)
        ks = jax.random.split(key, 5)
        B, L, D, F, E = (8, 8192, 256, 1024, 8)
        h = jax.random.normal(ks[0], (B, L, D), dtype=jnp.float32)
        gate_w = jax.random.normal(ks[1], (D, E), dtype=jnp.float32) * 0.02
        gate_b = jnp.zeros((E,), dtype=jnp.float32)
        w1 = jax.random.normal(ks[2], (E, D, F), dtype=jnp.float32) * (1.0 / math.sqrt(D))
        b1 = jnp.zeros((E, F), dtype=jnp.float32)
        w2 = jax.random.normal(ks[3], (E, F, D), dtype=jnp.float32) * (1.0 / math.sqrt(F))
        b2 = jnp.zeros((E, D), dtype=jnp.float32)
        return {'h': h, 'gate_w': gate_w, 'gate_b': gate_b, 'w1': w1, 'b1': b1, 'w2': w2, 'b2': b2}
    _L0_ffn_all = _L0_ffn_setup()
    _L0_ffn_in = {k: v for k, v in _L0_ffn_all.items() if k in ('gate_w', 'gate_b', 'w1', 'b1', 'w2', 'b2', )}
    del _L0_ffn_all

    return {
        "x": x,
        "L0_conv_w_qkv": _L0_conv_in["w_qkv"],
        "L0_conv_w_dw": _L0_conv_in["w_dw"],
        "L0_conv_w_pw": _L0_conv_in["w_pw"],
        "L0_conv_w_proj": _L0_conv_in["w_proj"],
        "L0_conv_bn_gamma": _L0_conv_in["bn_gamma"],
        "L0_conv_bn_beta": _L0_conv_in["bn_beta"],
        "L0_conv_bn_mean": _L0_conv_in["bn_mean"],
        "L0_conv_bn_var": _L0_conv_in["bn_var"],
        "L0_ffn_gate_w": _L0_ffn_in["gate_w"],
        "L0_ffn_gate_b": _L0_ffn_in["gate_b"],
        "L0_ffn_w1": _L0_ffn_in["w1"],
        "L0_ffn_b1": _L0_ffn_in["b1"],
        "L0_ffn_w2": _L0_ffn_in["w2"],
        "L0_ffn_b2": _L0_ffn_in["b2"],
    }

def reference(x, L0_conv_w_qkv, L0_conv_w_dw, L0_conv_w_pw, L0_conv_w_proj, L0_conv_bn_gamma, L0_conv_bn_beta, L0_conv_bn_mean, L0_conv_bn_var, L0_ffn_gate_w, L0_ffn_gate_b, L0_ffn_w1, L0_ffn_b1, L0_ffn_w2, L0_ffn_b2):
    import jax
    import jax.numpy as jnp
    def _L0_conv_ref(x, w_qkv, w_dw, w_pw, w_proj, bn_gamma, bn_beta, bn_mean, bn_var):
        import jax, jax.numpy as jnp
        import numpy as np
        IN_CH = 256
        OUT_CH = 256
        DIM = 8
        HEADS = IN_CH // DIM
        TOTAL = HEADS * DIM
        SCALE = 5
        EPS = 1e-15
        BN_EPS = 1e-05

        def conv2d(x, w, padding=0, groups=1):
            return jax.lax.conv_general_dilated(x, w, window_strides=(1, 1), padding=[(padding, padding), (padding, padding)], feature_group_count=groups, dimension_numbers=('NCHW', 'OIHW', 'NCHW'))

        def relu_linear_att(qkv):
            B, C, H, W = qkv.shape
            N = H * W
            G = C // (3 * DIM)
            qkv = qkv.astype(jnp.float32).reshape(B, G, 3 * DIM, N)
            q = jax.nn.relu(qkv[:, :, :DIM])
            k = jax.nn.relu(qkv[:, :, DIM:2 * DIM])
            v = qkv[:, :, 2 * DIM:]
            ones = jnp.ones((B, G, 1, N), qkv.dtype)
            v = jnp.concatenate([v, ones], axis=2)
            vk = jnp.einsum('bgdn,bgen->bgde', v, k)
            out = jnp.einsum('bgde,bgen->bgdn', vk, q)
            out = out[:, :, :DIM] / (out[:, :, DIM:] + EPS)
            return out.reshape(B, G * DIM, H, W)
        qkv = conv2d(x, w_qkv)
        agg = conv2d(qkv, w_dw, padding=SCALE // 2, groups=3 * TOTAL)
        agg = conv2d(agg, w_pw, groups=3 * HEADS)
        qkv_ms = jnp.concatenate([qkv, agg], axis=1)
        out = relu_linear_att(qkv_ms)
        out = conv2d(out, w_proj)
        inv = bn_gamma / jnp.sqrt(bn_var + BN_EPS)
        out = out * inv[None, :, None, None] + (bn_beta - bn_mean * inv)[None, :, None, None]
        return out

    def _L0_ffn_ref(h, gate_w, gate_b, w1, b1, w2, b2):
        import math
        import jax, jax.numpy as jnp
        import numpy as np
        CAPACITY_FACTOR = 1.25
        B, L, D = h.shape
        E = gate_w.shape[1]
        T = B * L
        C = max(1, math.ceil(CAPACITY_FACTOR * T / E))
        x = h.reshape(T, D)
        logits = x @ gate_w + gate_b
        probs = jax.nn.softmax(logits, axis=-1)
        idx = jnp.argmax(probs, axis=-1)
        prb = jnp.take_along_axis(probs, idx[:, None], axis=1)[:, 0]
        one_hot = jax.nn.one_hot(idx, E, dtype=jnp.float32)
        pos = (jnp.cumsum(one_hot, axis=0) * one_hot).sum(-1).astype(jnp.int32) - 1
        kept = pos < C
        pos_safe = jnp.where(kept, pos, C)
        buf = jnp.zeros((E, C, D), dtype=h.dtype).at[idx, pos_safe].set(x, mode='drop')
        hmid = jax.nn.relu(jnp.einsum('ecd,edf->ecf', buf, w1) + b1[:, None, :])
        ybuf = jnp.einsum('ecf,efd->ecd', hmid, w2) + b2[:, None, :]
        pos_g = jnp.minimum(pos, C - 1)
        y_tok = ybuf[idx, pos_g] * (prb * kept)[:, None]
        y = y_tok.reshape(B, L, D)
        y = jnp.nan_to_num(y, nan=0.0, posinf=10000.0, neginf=-10000.0)
        return y

    def _gn(v, G=32, eps=1e-5):
        B_, C_, H_, W_ = v.shape
        g = v.reshape(B_, G, C_ // G, H_, W_)
        m = jnp.mean(g, axis=(2, 3, 4), keepdims=True)
        s = jnp.var(g, axis=(2, 3, 4), keepdims=True)
        return ((g - m) / jnp.sqrt(s + eps)).reshape(v.shape)

    def _ln_c(v, eps=1e-6):
        m = jnp.mean(v, axis=1, keepdims=True)
        s = jnp.var(v, axis=1, keepdims=True)
        return (v - m) / jnp.sqrt(s + eps)

    def _ln_t(v, eps=1e-5):
        m = jnp.mean(v, axis=-1, keepdims=True)
        s = jnp.var(v, axis=-1, keepdims=True)
        return (v - m) / jnp.sqrt(s + eps)

    def _to_tokens(v):
        B_, C_, H_, W_ = v.shape
        return v.reshape(B_, C_, H_ * W_).transpose(0, 2, 1)
    def _from_tokens(t, like):
        B_, C_, H_, W_ = like.shape
        return t.transpose(0, 2, 1).reshape(B_, C_, H_, W_)

    x = x + _L0_conv_ref(_ln_c(x), L0_conv_w_qkv, L0_conv_w_dw, L0_conv_w_pw, L0_conv_w_proj, L0_conv_bn_gamma, L0_conv_bn_beta, L0_conv_bn_mean, L0_conv_bn_var)
    t = _to_tokens(x)
    t = t + _L0_ffn_ref(_ln_t(t), L0_ffn_gate_w, L0_ffn_gate_b, L0_ffn_w1, L0_ffn_b1, L0_ffn_w2, L0_ffn_b2)
    x = _from_tokens(t, x)
    return x


_drawn_inputs = setup_inputs


def setup_inputs(seed=0):
    import zlib

    import numpy as np

    out = dict(_drawn_inputs(seed))
    spreads = {'L0_conv_bn_gamma': (1.0, 0.2),
     'L0_conv_bn_beta': (0.0, 0.1),
     'L0_ffn_gate_b': (0.0, 0.1),
     'L0_ffn_b1': (0.0, 0.62),
     'L0_ffn_b2': (0.0, 0.438)}
    factors = {'L0_conv_w_dw': 8.0, 'L0_conv_w_pw': 8.0}
    for name, (base, spread) in spreads.items():
        noise = np.random.default_rng([zlib.crc32(name.encode()), seed]).standard_normal(out[name].shape)
        drawn = base * np.exp(spread * noise) if base else spread * noise
        out[name] = jnp.asarray(drawn.astype(out[name].dtype))
    for name, factor in factors.items():
        out[name] = (out[name] * factor).astype(out[name].dtype)
    return out
```

```python
import concourse.bass as bass
from concourse import mybir
from contextlib import ExitStack

B, CH, HW = 8, 256, 64
NTOK = HW * HW
KC = CH // 128
TILE = 512
NT = NTOK // TILE
BLK = 4
POS = BLK * BLK
NB = HW // BLK
GRID = NB + 1
GG = GRID * GRID
NGRID = POS * GG
NTRT = -(-NGRID // 128)
NTR = -(-NTRT // 4)
NCHUNK = 6
NG = 16
CHUNKS = [("k", 0), ("v", 0), ("k", 1), ("v", 1), ("q", 0), ("q", 1)]
NE, CAP, FF = 8, 5120, 1024
FT = FF // 128
NSLOT = NE * CAP
TOKENS = B * NTOK
QUADS = TOKENS // TILE
NSB = CAP // TILE
FMAX = 3.4028234663852886e38

CON = {}
_at = 0
for _name, _n in (("ident", 128), ("gmask", 128), ("tri", 128), ("gm16", 16), ("spread", 4 * 128),
                  ("carry0", NE), ("rev", NE)):
    CON[_name] = (_at, _at + _n)
    _at += _n
NCON = _at


class Ring:

    def __init__(self, size, keys):
        self.size, self.at = size, {k: (n % size, n // size) for n, k in enumerate(keys)}
        assert len(keys) % size == 0
        self.per = len(keys) // size

    def __getitem__(self, key):
        return self.at[key]


def nothing(*_):
    pass


def hold(eng, sem, value):
    eng.wait_ge(sem, value)
    eng.nop(nofuse=True)


def image(ph):
    ph["ln"]()
    ph["qkv"](0)
    ph["tr"](0)
    for t in range(NCHUNK):
        ph["conv"](t, 0)
        if t + 1 < NCHUNK:
            ph["qkv"](t + 1)
        ph["conv"](t, 1)
        if CHUNKS[t][0] == "k":
            ph["tr"](t + 1)
            ph["flush"](t)
        if CHUNKS[t][0] == "v":
            ph["flush"](t)
            ph["vka"](CHUNKS[t][1])
            if CHUNKS[t + 1][0] == "k":
                ph["tr"](t + 1)
    ph["out"]()
    ph["den"](0)
    for s in range(NT + 3):
        if s >= 3:
            ph["rank"](s - 3)
        if s + 1 < NT:
            ph["den"](s + 1)
        if s < NT:
            ph["attend"](s)
        if 1 <= s <= NT:
            ph["proj"](s - 1)
        if 2 <= s <= NT + 1:
            ph["logit"](s - 2)


def psum_rings():
    main, turn = [], []
    for u in range(NT + 1):
        main += [("mu", u)] if u < NT else []
        main += [("var", u - 1)] if u else []
    image(dict(ln=nothing, out=nothing, vka=nothing,
               qkv=lambda t: main.extend(("qkv", t, w) for w in range(NT)),
               tr=lambda t: turn.extend(("tr", t, m) for m in range(NTR)),
               conv=lambda t, half: turn.extend(("ct", t, p - 1) for p in range(4 * half, 4 * half + 4)
                                                if p and CHUNKS[t][0] != "q"),
               flush=lambda t: turn.append(("ct", t, 7)),
               den=lambda s: main.append(("den", s)),
               attend=lambda s: main.extend((k, s, c) for c in range(4) for k in ("num", "inv")),
               proj=lambda s: main.extend(("proj", s, i) for i in range(2)),
               logit=lambda s: (main.append(("logit", s)), turn.extend(("tn", s, k) for k in range(2))),
               rank=lambda s: main.append(("rank", s))))
    return Ring(3, main), Ring(2, turn)


def mixer_and_dispatch(nc, keep, D):
    f32, u32 = mybir.dt.float32, mybir.dt.uint32
    ALU, ACT, AX = mybir.AluOpType, mybir.ActivationFunctionType, mybir.AxisListType
    G, T = psum_rings()
    with ExitStack() as ctx:
        def sb(name, shape, dt=f32):
            return ctx.enter_context(nc.sbuf_tensor(name, shape, dt))

        def sem(name):
            return ctx.enter_context(nc.semaphore(name))

        xt = [sb(f"xt{i}", [128, KC, TILE]) for i in range(2)]
        xn = sb("xn", [128, KC, NTOK])
        grid = sb("grid", [128, BLK, BLK, GRID, GRID])
        conv_in = sb("conv_in", [128, NG, GRID, GRID])
        toep = sb("toep", [128, 4, 4, 128])
        dwt = sb("dwt", [128, 2, NG, 64])
        pwt = sb("pwt", [128, NCHUNK, NG, 8])
        kt = sb("kt", [128, NTRT * 128])
        kta = sb("kta", [128, 2, POS, 128])
        vt = sb("vt", [128, 2, 4, 129])
        qe = sb("qe", [128, 4, 256])
        q0 = sb("q0", [128, 2, NTOK])
        wq = sb("wq", [128, KC, NCHUNK, 128])
        wp = sb("wp", [128, 4, CH])
        vk = sb("vk", [128, 4, 128])
        dn = sb("dn", [128, 4, 64])
        ones = sb("ones", [128, 128])
        mean_w = sb("mean_w", [128, 128])
        eps = sb("eps", [128, 3])
        bias = sb("bias", [128, CH])
        bnr = sb("bnr", [128, 4, CH])
        gate = sb("gate", [128, KC, NE])
        gate_b = sb("gate_b", [128, NE])
        carry = sb("carry", [128, NE])
        small = sb("small", [128, 2, 4, 24])
        stat = sb("stat", [128, 2, 4, 16])
        sidx = sb("sidx", [128, 4, 4], u32)
        con = sb("con", [128, NCON])
        dlog, kept, gidx = keep
        c_ = {k: con[:, a:b] for k, (a, b) in CON.items()}
        ident = c_["ident"]
        ktn = kt[:, :].rearrange("p (m c) -> p m c", m=NTRT)
        vta = kt[:, 0:32 * 129].rearrange("p (h s c) -> p h s c", h=2, s=POS)
        ktf = kta[:, :, :, :].rearrange("p h s c -> p (h s c)")
        sq = [ktf[:, i * 1024:(i + 1) * 1024].rearrange("p (k n) -> p k n", k=KC) for i in range(2)]
        std = [ktf[:, 2048 + i * 512:2048 + (i + 1) * 512] for i in range(2)]
        den = [kt[0:64, i * 512:(i + 1) * 512] for i in range(2)]
        tnt = kt[:, 1024:2048].rearrange("p (k n) -> p k n", k=KC)
        cif = conv_in[:, :, :, :].rearrange("p g i j -> p (g i j)")
        y1 = [cif[:, i * 1024:(i + 1) * 1024].rearrange("p (j d) -> p j d", j=4) for i in range(2)]
        ao = [a.rearrange("p (c n) -> p c n", c=4) for a in (cif[:, 2048:4096], kt[:, 2048:4096])]
        num = [cif[:, 4096:4608], kt[:, 4096:4608]]
        tn = [ktf[:, i * 1024:(i + 1) * 1024].rearrange("p (j d) -> p j d", j=4) for i in range(4)]
        qr = [q0[:, 0, :], xn[:, 0, :], q0[:, 1, :], xn[:, 1, :]]
        zero = q0[:, 0, 0:1024]

        Gb = [ctx.enter_context(nc.psum_tensor(f"G{i}", [128, 512], f32)) for i in range(3)]
        Vb = [ctx.enter_context(nc.psum_tensor(f"V{i}", [128, 512], f32)) for i in range(2)]
        Tb = [ctx.enter_context(nc.psum_tensor(f"T{i}", [128, 512], f32)) for i in range(2)]
        Kb = ctx.enter_context(nc.psum_tensor("K0", [128, 512], f32))

        g_full = [sem(f"g_full{i}") for i in range(3)]
        g_out = [sem(f"g_out{i}") for i in range(3)]
        t_full = [sem(f"t_full{i}") for i in range(2)]
        t_out = [sem(f"t_out{i}") for i in range(2)]
        v_out = [sem(f"v_out{i}") for i in range(2)]
        conv_done = sem("conv_done")
        k_full, k_out = sem("k_full"), sem("k_out")
        w_in = sem("w_in")
        setup = sem("setup")
        zset, zfill = sem("zset"), sem("zfill")
        begin_at_1 = [*g_out, *t_out, *v_out]
        prime = sb("prime", [128, 10, NE])
        xt_in = [sem(f"xt_in{i}") for i in range(2)]
        sq_done, xn_done = sem("sq_done"), sem("xn_done")
        ci_in = [sem(f"ci_in{g}") for g in range(NG)]
        dwt_in = [sem(f"dwt_in{i}") for i in range(2)]
        toep_done = sem("toep_done")
        qe_out = [sem(f"qe_out{i}") for i in range(4)]
        rec_done = sem("rec_done")
        y1_out = [sem(f"y1_out{i}") for i in range(2)]
        var_done, sd_done, tn_done = sem("var_done"), sem("sd_done"), sem("tn_done")
        oh_done, sidx_done = sem("oh_done"), sem("sidx_done")
        sc_out = [sem(f"sc_out{i}") for i in range(4)]
        carried = sem("carried")
        bn_eps, bn_sd = sem("bn_eps"), sem("bn_sd")
        chain0 = sem("chain0")
        chain = sem("chain")

        XT = Ring(2, [("ln", u) for u in range(NT)] + [("proj", u) for u in range(NT)])

        def full(eng, b, key):
            bank, n = G[key]
            eng.wait_ge(g_full[bank], b * G.per + n + 1)
            return Gb[bank], g_out[bank]

        def tfull(eng, b, key):
            bank, n = T[key]
            eng.wait_ge(t_full[bank], b * T.per + n + 1)
            return Tb[bank], t_out[bank]

        def emptied(eng, b, key):
            bank, n = G[key]
            hold(eng, g_out[bank], b * G.per + n + 2)

        def grid_ready(eng, b, t_):
            for w in (NT - 3, NT - 2, NT - 1):
                emptied(eng, b, ("qkv", t_, w))

        def tiles_of(m4):
            return [(j, 4 * m4 + j, min(128, NGRID - 128 * (4 * m4 + j))) for j in range(4) if 4 * m4 + j < NTRT]

        def grid_view(w):
            qy, pair = w // 2, w % 2
            py, i0 = (qy + 2) % BLK, (qy + 2) // BLK
            px, j0 = (2, 0) if pair == 0 else (0, 1)
            return grid[:, py, px:px + 2, i0:i0 + NB, j0:j0 + NB]

        block = ctx.enter_context(nc.Block())

        @block.sync
        def _(sp):
            loads = [(con[:, :], D["con"]), (wq[:, :, :, :], D["wq"]), (wp[:, :, :], D["wp"]), (pwt[:, :, :, :], D["pw"]),
                     (gate[:, :, :], D["gate_w"]), (gate_b[:, :], D["gate_b"].to_broadcast([128, NE]))]
            loads += [(bnr[:, i, :], D[k].to_broadcast([128, CH])) for i, k in
                      enumerate(("bn_gamma", "bn_beta", "bn_mean", "bn_var"))]
            for dst, src in loads:
                sp.dma_start(dst, src).then_inc(w_in, 16)
            assert len(loads) == 10
            for i, first in enumerate([*qe_out, *y1_out]):
                sp.dma_start(prime[:, i, :], D["gate_b"].to_broadcast([128, NE])).then_inc(first, 16)
            hold(sp, zset, 1)
            for i in range(NSLOT * CH // (128 * 1024)):
                sp.dma_start(D["slots"][i * 512:(i + 1) * 512, :].rearrange("(p r) d -> p (r d)", p=128),
                             zero).then_inc(zfill, 16)

            with sp.Fori(0, B) as b:
                def load_x(key):
                    s, n = XT[key]
                    if key[0] == "ln" and key[1] >= 2:
                        hold(sp, xn_done, b * NT + key[1] - 1)
                    if key[0] == "proj" and key[1] < 2:
                        hold(sp, xn_done, b * NT + NT)
                    sp.dma_start(xt[s][:, :, :], D["x"][bass.ds(b, 1), :, key[1] * TILE:(key[1] + 1) * TILE]
                                 .rearrange("o (k p) n -> p (o k) n", p=128)).then_inc(xt_in[s], 16)

                def load_dwt(t_):
                    if t_ < 2:
                        hold(sp, toep_done, b * 96 + 1)
                    else:
                        hold(sp, toep_done, b * 96 + 16 * (t_ - 1) + 1)
                    sp.dma_start(dwt[:, t_ % 2, :, :], D["dw"][t_, :, :, :]).then_inc(dwt_in[t_ % 2], 16)

                def regroup(t_, half):
                    if half == 0:
                        grid_ready(sp, b, t_)
                        if t_ == 0:
                            for i in range(2):
                                hold(sp, y1_out[i], b * 64 + 16)
                    for g in range(8 * half, 8 * half + 8):
                        hold(sp, conv_done, b * 96 + 16 * t_ + g + 1)
                        sp.dma_start(conv_in[:, g, :, :].rearrange("p i j -> p (i j)"),
                                     grid[8 * g:8 * g + 8, :, :, :, :].rearrange("p y x i j -> p (y x) (i j)"))\
                            .then_inc(ci_in[g], 16)

                def q_back(t_, half):
                    h = CHUNKS[t_][1]
                    for g in range(8 * half, 8 * half + 8):
                        n = NG * t_ + g
                        hold(sp, v_out[(n // 2) % 2], b * 24 + n // 4 + 2)
                        sp.dma_start(qr[2 + h][8 * g:8 * g + 8, :].rearrange("p (s n) -> p s n", s=POS),
                                     qe[:, g % 4, :]).then_inc(qe_out[g % 4], 16)

                load_x(("ln", 0))
                load_x(("ln", 1))
                load_dwt(0)
                load_dwt(1)
                for u in range(2, NT):
                    load_x(("ln", u))
                regroup(0, 0)
                regroup(0, 1)
                for t_ in range(1, NCHUNK):
                    if CHUNKS[t_ - 1][0] == "q":
                        q_back(t_ - 1, 0)
                    regroup(t_, 0)
                    if CHUNKS[t_ - 1][0] == "q":
                        q_back(t_ - 1, 1)
                    regroup(t_, 1)
                    if t_ + 1 < NCHUNK:
                        load_dwt(t_ + 1)
                q_back(5, 0)
                q_back(5, 1)
                load_x(("proj", 0))
                load_x(("proj", 1))
                for u in range(NT):
                    emptied(sp, b, ("proj", u, 0))
                    emptied(sp, b, ("proj", u, 1))
                    sp.dma_start(D["y1"][bass.ds(b * NTOK + u * TILE, TILE), :].rearrange("(j p) d -> p j d", p=128),
                                 y1[u % 2]).then_inc(y1_out[u % 2], 16)
                    if u + 2 < NT:
                        load_x(("proj", u + 2))
            for i in range(2):
                hold(sp, y1_out[i], B * 64 + 16)

        @block.gpsimd
        def _(pool):
            for first in [*begin_at_1, k_out, toep_done, carried]:
                pool.sem_inc(first, 1)
            for i, first in enumerate(sc_out):
                pool.dma_start(prime[:, 6 + i, :], D["gate_b"].to_broadcast([128, NE])).then_inc(first, 16)
            nc.gpsimd.memset(zero, 0.0).then_inc(zset, 1)
            nc.gpsimd.memset(grid[:, :, :, :, :], 0.0).then_inc(setup, 1)
            nc.gpsimd.memset(ones[:, :], 1.0).then_inc(setup, 1)
            nc.gpsimd.memset(mean_w[:, :], 1.0 / CH).then_inc(setup, 1)
            nc.gpsimd.memset(dn[:, :, :], 0.0).then_inc(setup, 1)
            nc.gpsimd.memset(vt[:, :, :, 128:129], 1.0).then_inc(setup, 1)
            nc.gpsimd.memset(eps[:, 0:1], 1e-6).then_inc(setup, 1)
            nc.gpsimd.memset(eps[:, 1:2], 1e-5).then_inc(setup, 1)
            nc.gpsimd.memset(eps[:, 2:3], 1e-15).then_inc(setup, 1)
            hold(pool, w_in, 160)
            hold(pool, zfill, 16 * (NSLOT // 512))
            with pool.Fori(0, B) as b:
                for t_ in range(NCHUNK):
                    hold(pool, dwt_in[t_ % 2], b * 48 + 16 * (t_ // 2) + 16)
                    for g in range(NG):
                        n = NG * t_ + g
                        hold(pool, conv_done, b * 96 + n + 13)
                        nc.gpsimd.tensor_tensor(
                            toep[:, n % 4, :, :].rearrange("p q (c s) -> p q c s", c=8),
                            dwt[:, t_ % 2, g, :].rearrange("p (q o s) -> p q o s", q=4, o=1).to_broadcast([128, 4, 8, POS]),
                            pwt[:, t_, g, :].rearrange("p (o c s) -> p o c s", o=1, s=1).to_broadcast([128, 4, 8, POS]),
                            ALU.mult).then_inc(toep_done, 1)
                for u in range(NT):
                    hold(pool, sidx_done, b * 8 + u + 1)
                    for j in range(4):
                        nc.gpsimd.indirect_dma_start(
                            out=D["slots"], out_offset=bass.IndirectOffsetOnAxis(ap=sidx[:, u % 4, j:j + 1], axis=0),
                            in_=tn[u % 4][:, j, :], in_offset=None,
                            bounds_check=NSLOT - 1, oob_is_err=False).then_inc(sc_out[u % 4], 16)
            for i in range(4):
                hold(pool, sc_out[i], B * 128 + 16)

        @block.tensor
        def _(pe):
            def bank(b, key):
                i, n = G[key]
                pe.wait_ge(g_out[i], b * G.per + n + 1)
                return Gb[i], g_full[i]

            def tbank(b, key):
                i, n = T[key]
                pe.wait_ge(t_out[i], b * T.per + n + 1)
                return Tb[i], t_full[i]

            mm = nc.tensor.matmul
            pe.sem_inc(conv_done, 16)
            pe.wait_ge(w_in, 160)
            pe.wait_ge(setup, 8 + 3)
            with pe.Fori(0, B) as b:
                def ln():
                    for u in range(NT + 1):
                        if u < NT:
                            s, n = XT[("ln", u)]
                            pe.wait_ge(xt_in[s], (b * XT.per + n) * 16 + 16)
                            o, done = bank(b, ("mu", u))
                            for k in range(KC):
                                last = mm(o[:, :], mean_w[:, :], xt[s][:, k, :], start=k == 0, stop=k == 1)
                            last.then_inc(done, 1)
                        if u:
                            pe.wait_ge(sq_done, b * NT + u)
                            o, done = bank(b, ("var", u - 1))
                            for k in range(KC):
                                last = mm(o[:, :], mean_w[:, :], sq[(u - 1) % 2][:, k, :], start=k == 0, stop=k == 1)
                            last.then_inc(done, 1)
                    pe.wait_ge(xn_done, b * NT + NT)

                def qkv(t_):
                    if t_:
                        for g in range(8, NG):
                            pe.wait_ge(ci_in[g], b * 96 + 16 * t_)
                    for w in range(NT):
                        o, done = bank(b, ("qkv", t_, w))
                        for k in range(KC):
                            last = mm(o[:, :], wq[:, k, t_, :], xn[:, k, w * TILE:(w + 1) * TILE],
                                      start=k == 0, stop=k == 1)
                        last.then_inc(done, 1)

                def tr(t_):
                    kind, h = CHUNKS[t_]
                    grid_ready(pe, b, t_)

                    def own_vk(m4):
                        i, n = T[("tr", t_, m4)]
                        pe.wait_ge(t_out[i], b * T.per + n + 2)
                        for j, m, n_ in tiles_of(m4):
                            last = mm(Kb[:, 0:129], ktn[0:n_, m, :], vt[0:n_, m4 % 2, j, :], start=m == 0, stop=m == NTRT - 1)
                        if m4 == NTR - 1:
                            last.then_inc(k_full, 1)

                    if kind == "v":
                        pe.wait_ge(k_out, b * 4 + 2 * h + 1)
                    flat = grid[:, :, :, :, :].rearrange("p y x i j -> p (y x i j)")
                    for m4 in range(NTR):
                        o, done = tbank(b, ("tr", t_, m4))
                        for j, m, n_ in tiles_of(m4):
                            last = nc.tensor.transpose(o[0:n_, 128 * j:128 * j + 128], flat[:, 128 * m:128 * m + n_], ident)
                        last.then_inc(done, 1)
                        if kind == "v" and m4:
                            own_vk(m4 - 1)
                    if kind == "v":
                        own_vk(NTR - 1)

                def conv(t_, half):
                    for g in range(8 * half, 8 * half + 8):
                        n = NG * t_ + g
                        pe.wait_ge(ci_in[g], b * 96 + 16 * (t_ + 1))
                        pe.wait_ge(toep_done, b * 96 + n + 2)
                        i = (n // 2) % 2
                        if g % 2 == 0:
                            pe.wait_ge(v_out[i], b * 24 + n // 4 + 1)
                        o = Vb[i]
                        at = 256 * (g % 2)
                        for q in range(4):
                            y, x = q // 2, q % 2
                            last = mm(o[:, at:at + 256], toep[:, n % 4, q, :], conv_in[:, g, y:y + NB, x:x + NB],
                                      start=q == 0, stop=q == 3)
                        last.then_inc(conv_done, 1)
                        if g % 2 and g > 1 and CHUNKS[t_][0] != "q":
                            turn_conv(t_, g // 2 - 1)

                def turn_conv(t_, p):
                    n = NG * t_ + 2 * p
                    pe.wait_ge(v_out[(n // 2) % 2], b * 24 + n // 4 + 2)
                    o, done = tbank(b, ("ct", t_, p))
                    for i in range(4):
                        last = nc.tensor.transpose(o[:, 128 * i:128 * i + 128],
                                                   qe[:, (2 * p + i // 2) % 4, 128 * (i % 2):128 * (i % 2) + 128], ident)
                    last.then_inc(done, 1)

                def vka(h):
                    pe.wait_ge(k_out, b * 4 + 2 * h + 2)
                    for p in (6, 7):
                        i, n = T[("ct", 2 * h + 1, p)]
                        pe.wait_ge(t_out[i], b * T.per + n + 2)
                    for m in range(32):
                        hf, s = m // POS, m % POS
                        last = mm(Kb[:, 0:129], kta[:, hf, s, :], vta[:, hf, s, :], start=m == 0, stop=m == 31)
                    last.then_inc(k_full, 1)

                def out():
                    for i in range(4):
                        pe.wait_ge(qe_out[i], b * 128 + 128 + 16)
                    pe.wait_ge(k_out, b * 4 + 5)


                def tile_of(c, s):
                    return qr[c].rearrange("p (s n) -> p s n", s=POS)[:, :, 32 * s:32 * s + 32]

                def dens(s):
                    o, done = bank(b, ("den", s))
                    for c in range(4):
                        last = mm(o[0:64, :], dn[:, c, :], tile_of(c, s), start=c == 0, stop=c == 3)
                    last.then_inc(done, 1)

                def attend(s):
                    spread = c_["spread"].rearrange("p (c m) -> p c m", c=4)
                    for c in range(4):
                        o, done = bank(b, ("num", s, c))
                        mm(o[:, :], vk[:, c, :], tile_of(c, s), start=True, stop=True).then_inc(done, 1)
                        if c == 0:
                            pe.wait_ge(rec_done, b * NT + s + 1)
                        o, done = bank(b, ("inv", s, c))
                        mm(o[:, :], spread[0:64, c, :], den[s % 2], start=True, stop=True).then_inc(done, 1)

                def proj(s):
                    emptied(pe, b, ("inv", s, 3))
                    sl, n = XT[("proj", s)]
                    pe.wait_ge(xt_in[sl], (b * XT.per + n) * 16 + 16)
                    for i in range(2):
                        o, done = bank(b, ("proj", s, i))
                        for j in range(2):
                            at = (2 * i + j) * 128
                            oo = o[:, 256 * j:256 * j + 256]
                            for c in range(4):
                                mm(oo, ao[s % 2][:, c, at:at + 128], wp[:, c, :], start=c == 0, stop=False)
                            for k in range(KC):
                                last = mm(oo[:, 128 * k:128 * k + 128], xt[sl][:, k, at:at + 128], ident,
                                          start=False, stop=k == 1)
                        last.then_inc(done, 1)

                def logit(s):
                    pe.wait_ge(tn_done, b * NT + s + 1)
                    for k in range(KC):
                        o, done = tbank(b, ("tn", s, k))
                        for j in range(4):
                            last = nc.tensor.transpose(o[:, 128 * j:128 * j + 128], tn[s % 4][:, j, 128 * k:128 * k + 128], ident)
                        last.then_inc(done, 1)
                    o, done = bank(b, ("logit", s))
                    for k in range(KC):
                        i, n = T[("tn", s, k)]
                        pe.wait_ge(t_out[i], b * T.per + n + 2)
                    for j in range(4):
                        for k in range(KC):
                            last = mm(o[:, NE * j:NE * j + NE], tnt[:, k, 128 * j:128 * j + 128], gate[:, k, :],
                                      start=k == 0, stop=k == 1)
                    last.then_inc(done, 1)

                def rank(s):
                    pe.wait_ge(oh_done, b * NT + s + 1)
                    oh = small[:, s % 2, :, 0:NE]
                    o, done = bank(b, ("rank", s))
                    mm(o[:, 0:32], c_["tri"], oh, start=True, stop=False)
                    for j in range(3):
                        for jj in range(j + 1, 4):
                            mm(o[:, NE * jj:NE * jj + NE], ones[:, :], oh[:, j, :], start=False, stop=(j == 2))
                    for j in range(4):
                        last = mm(o[:, 32:32 + NE], ones[:, :], oh[:, j, :], start=j == 0, stop=j == 3)
                    last.then_inc(done, 1)

                image(dict(ln=ln, qkv=qkv, tr=tr, conv=conv, flush=lambda t_: turn_conv(t_, 7), vka=vka, out=out,
                           den=dens, attend=attend, proj=proj, logit=logit, rank=rank))

        def conv_evacuation(eng, b, t_, half, mine, relu, copy):
            kind, h = CHUNKS[t_]
            for p in range(4 * half, 4 * half + 4):
                if kind != "q" and p:
                    turned(eng, b, t_, p - 1, mine, copy)
                if p % 2 != mine:
                    continue
                g = 2 * p
                n = NG * t_ + 2 * p
                i = (n // 2) % 2
                eng.wait_ge(conv_done, b * 96 + n + 2 + 16)
                if kind != "q" and p >= 2:
                    j, m = T[("ct", t_, p - 2)]
                    eng.wait_ge(t_full[j], b * T.per + m + 1)
                elif kind != "q" and t_ > 0 or t_ == 4 and p < 2:
                    j, m = T[("ct", t_ - 1, 6 + p)]
                    eng.wait_ge(t_full[j], b * T.per + m + 1)
                elif kind != "q":
                    for k in (g % 4, g % 4 + 1):
                        eng.wait_ge(qe_out[k], b * 128 + 16)
                else:
                    for k in (g % 4, g % 4 + 1):
                        eng.wait_ge(qe_out[k], (b * 8 + 4 * h + g // 4) * 16 + 16)
                (copy if kind == "v" else relu)(qe[:, g % 4:g % 4 + 2, :].rearrange("p g n -> p (g n)"), Vb[i][:, :], v_out[i])

        def turned(eng, b, t_, p, mine, copy):
            if p % 2 != mine:
                return
            o, done = tfull(eng, b, ("ct", t_, p))
            dst = kta if CHUNKS[t_][0] == "k" else vta
            for hf in range(2):
                d = dst[:, hf, :, 16 * p:16 * p + 16].rearrange("p s (g c) -> p g c s", g=2)
                copy(d, o[:, :].rearrange("p (g h c s) -> p g h c s", g=2, h=2, c=8)[:, :, hf, :, :], done if hf else None)

        @block.scalar
        def _(act):
            A = nc.scalar.activation
            act.wait_ge(setup, 8)
            act.wait_ge(bn_eps, 1)
            A(bnr[:, 3, :], bnr[:, 3, :], ACT.Sqrt, bias=eps[:, 1:2]).then_inc(bn_sd, 1)
            with act.Fori(0, B) as b:
                def relu(dst, src, done):
                    A(dst, src, ACT.Relu).then_inc(done, 1)

                def copy(dst, src, done):
                    ins = A(dst, src, ACT.Copy)
                    if done:
                        ins.then_inc(done, 1)

                def ln():
                    for i in range(4):
                        act.wait_ge(sc_out[i], b * 128 + 16)
                    for u in range(NT + 1):
                        if u < NT:
                            emptied(act, b, ("mu", u))
                            if u >= 2:
                                full(act, b, ("var", u - 2))
                            A(sq[u % 2], xt[u % 2][:, :, :], ACT.Square).then_inc(sq_done, 1)
                        if u:
                            o, done = full(act, b, ("var", u - 1))
                            if u >= 3:
                                act.wait_ge(xn_done, b * NT + u - 2)
                            A(std[(u - 1) % 2], o[:, :], ACT.Sqrt, bias=eps[:, 0:1]).then_inc(done, 1)

                def qkv(t_):
                    kind, h = CHUNKS[t_]
                    for w in range(0, NT, 2):
                        o, done = full(act, b, ("qkv", t_, w))
                        ins = A(grid_view(w), o[:, :].rearrange("p (x i j) -> p x i j", x=2, i=NB), ACT.Copy)
                        if kind == "q":
                            if t_ == 4 and w == 0:
                                act.wait_ge(zfill, 16 * (NSLOT // 512))
                            ins = A(qr[h][:, w * TILE:(w + 1) * TILE], o[:, :], ACT.Relu)
                        ins.then_inc(done, 1)

                def tr(t_):
                    for m4 in range(0, NTR, 2):
                        o, done = tfull(act, b, ("tr", t_, m4))
                        o = o[:, :].rearrange("p (j c) -> p j c", j=4)
                        n, rows = len(tiles_of(m4)), tiles_of(m4)[-1][2]
                        if CHUNKS[t_][0] == "k":
                            relu(ktn[0:rows, 4 * m4:4 * m4 + n, :], o[0:rows, 0:n, :], done)
                        else:
                            copy(vt[0:rows, m4 % 2, 0:n, 0:128], o[0:rows, 0:n, :], done)

                def dens(s):
                    o, done = full(act, b, ("den", s))
                    if s >= 2:
                        full(act, b, ("inv", s - 2, 3))
                    A(den[s % 2], o[0:64, :], ACT.Identity, bias=eps[0:64, 2:3]).then_inc(done, 1)

                def attend(s):
                    for c in range(4):
                        if c >= 2:
                            emptied(act, b, ("inv", s, c - 2))
                        elif s:
                            emptied(act, b, ("inv", s - 1, c + 2))
                        o, done = full(act, b, ("num", s, c))
                        A(num[c % 2], o[:, :], ACT.Copy).then_inc(done, 1)

                def proj(s):
                    act.wait_ge(var_done, b * NT + s + 1)
                    A(stat[:, s % 2, :, 8:9], stat[:, s % 2, :, 7:8], ACT.Sqrt, bias=eps[:, 1:2]).then_inc(sd_done, 1)

                def logit(s):
                    for k in range(KC):
                        o, done = tfull(act, b, ("tn", s, k))
                        A(tnt[:, k, :], o[:, :], ACT.Copy).then_inc(done, 1)

                image(dict(ln=ln, qkv=qkv, tr=tr, out=nothing, vka=nothing, den=dens, attend=attend, proj=proj,
                           logit=logit, rank=nothing, flush=lambda t_: turned(act, b, t_, 7, 0, copy),
                           conv=lambda t_, half: conv_evacuation(act, b, t_, half, 0, relu, copy)))

        @block.vector
        def _(dve):
            V = nc.vector
            here = [0]

            def link0(ins):
                here[0] += 1
                ins.then_inc(chain0, 1)
                dve.wait_ge(chain0, here[0])

            dve.wait_ge(w_in, 160)
            dve.wait_ge(setup, 8)
            dve.sem_inc(bn_eps, 1)
            dve.wait_ge(bn_sd, 1)
            link0(V.reciprocal(bnr[:, 3, :], bnr[:, 3, :]))
            link0(V.tensor_tensor(bnr[:, 0, :], bnr[:, 0, :], bnr[:, 3, :], ALU.mult))
            link0(V.tensor_tensor(bnr[:, 2, :], bnr[:, 2, :], bnr[:, 0, :], ALU.mult))
            V.tensor_tensor(bias[:, :], bnr[:, 1, :], bnr[:, 2, :], ALU.subtract).then_inc(setup, 1)
            V.tensor_tensor(wp[:, :, :], wp[:, :, :], bnr[:, 0:1, :].to_broadcast([128, 4, CH]), ALU.mult).then_inc(setup, 1)
            V.tensor_copy(carry[:, :], c_["carry0"]).then_inc(setup, 1)
            dve.wait_ge(setup, 11)
            with dve.Fori(0, B) as b:
                here = [0]

                def link(ins):
                    here[0] += 1
                    ins.then_inc(chain, 1)
                    dve.wait_ge(chain, b * LINKS + here[0])

                def relu(dst, src, done):
                    V.tensor_scalar_max(dst, src, 0.0).then_inc(done, 1)

                def copy(dst, src, done):
                    ins = V.tensor_copy(dst, src)
                    if done:
                        ins.then_inc(done, 1)

                def ln():
                    def centre(u):
                        s, n = XT[("ln", u)]
                        dve.wait_ge(xt_in[s], (b * XT.per + n) * 16 + 16)
                        o, done = full(dve, b, ("mu", u))
                        V.tensor_tensor(xt[s][:, :, :], xt[s][:, :, :],
                                        o[:, :].rearrange("p (o n) -> p o n", o=1).to_broadcast([128, KC, TILE]),
                                        ALU.subtract).then_inc(done, 1)

                    for u in range(NT + 1):
                        if u < NT:
                            centre(u)
                        if u:
                            v = u - 1
                            emptied(dve, b, ("var", v))
                            link(V.reciprocal(std[v % 2], std[v % 2]))
                            for k in range(KC):
                                for i in range(2):
                                    src = [a[:, 256 * i:256 * i + 256].rearrange("p (q j x) -> p q x j", q=4, x=4)
                                           for a in (xt[v % 2][:, k, :], std[v % 2])]
                                    dst = xn[:, k, :].rearrange("p (q x i j) -> p q x i j", q=4, x=4, i=NB)
                                    ins = V.tensor_tensor(dst[:, :, :, 2 * v + i, :], src[0], src[1], ALU.mult)
                            ins.then_inc(xn_done, 1)

                def qkv(t_):
                    kind, h = CHUNKS[t_]
                    for w in range(1, NT, 2):
                        o, done = full(dve, b, ("qkv", t_, w))
                        ins = V.tensor_copy(grid_view(w), o[:, :].rearrange("p (x i j) -> p x i j", x=2, i=NB))
                        if kind == "q":
                            if t_ == 4 and w == 1:
                                dve.wait_ge(zfill, 16 * (NSLOT // 512))
                            ins = V.tensor_scalar_max(qr[h][:, w * TILE:(w + 1) * TILE], o[:, :], 0.0)
                        ins.then_inc(done, 1)

                def kv(c):
                    h, conv = c % 2, c // 2
                    dve.wait_ge(k_full, b * 4 + 2 * h + conv + 1)
                    V.tensor_tensor(vk[:, c, :], Kb[:, 0:128], c_["gmask"], ALU.mult)
                    V.tensor_scalar(dn[:, c, 16 * c:16 * c + 16], c_["gm16"], Kb[:, 128:129], None, ALU.mult)\
                        .then_inc(k_out, 1)

                def tr(t_):
                    for m4 in range(1, NTR, 2):
                        o, done = tfull(dve, b, ("tr", t_, m4))
                        o = o[:, :].rearrange("p (j c) -> p j c", j=4)
                        n, rows = len(tiles_of(m4)), tiles_of(m4)[-1][2]
                        if CHUNKS[t_][0] == "k":
                            relu(ktn[0:rows, 4 * m4:4 * m4 + n, :], o[0:rows, 0:n, :], done)
                        else:
                            copy(vt[0:rows, m4 % 2, 0:n, 0:128], o[0:rows, 0:n, :], done)
                    if CHUNKS[t_][0] == "v":
                        kv(CHUNKS[t_][1])
                        V.memset(vta[:, :, :, 128:129], 1.0)

                def dens(s):
                    emptied(dve, b, ("den", s))
                    V.reciprocal(den[s % 2], den[s % 2]).then_inc(rec_done, 1)

                def attend(s):
                    for c in range(4):
                        o, done = full(dve, b, ("inv", s, c))
                        emptied(dve, b, ("num", s, c))
                        for i in range(2):
                            src = [a.rearrange("p (q x i j) -> p q x i j", q=4, x=4, i=2)[:, :, :, i, :]
                                   for a in (num[c % 2], o[:, :])]
                            dst = ao[s % 2][:, c, 256 * i:256 * i + 256].rearrange("p (q j x) -> p q x j", q=4, x=4)
                            ins = V.tensor_tensor(dst, src[0], src[1], ALU.mult)
                        ins.then_inc(done, 1)

                def proj(s):
                    dve.wait_ge(y1_out[s % 2], (b * 4 + s // 2) * 16 + 16)
                    for i in range(2):
                        o, done = full(dve, b, ("proj", s, i))
                        V.tensor_tensor(y1[s % 2][:, 2 * i:2 * i + 2, :], o[:, :].rearrange("p (j d) -> p j d", j=2),
                                        bias[:, :].rearrange("p (o d) -> p o d", o=1).to_broadcast([128, 2, CH]),
                                        ALU.add).then_inc(done, 1)
                    st = stat[:, s % 2, :, :]
                    emptied(dve, b, ("proj", s, 0))
                    emptied(dve, b, ("proj", s, 1))
                    for j in range(4):
                        ins = V.bn_stats(st[:, j, 0:6], y1[s % 2][:, j, :])
                    link(ins)
                    dve.nop(nofuse=True)
                    for j in range(4):
                        ins = V.bn_aggr(st[:, j, 6:8], st[:, j, 0:6])
                    ins.then_inc(var_done, 1)
                    dve.wait_ge(sd_done, b * NT + s + 1)
                    link(V.reciprocal(st[:, :, 14:15], st[:, :, 8:9]))
                    dve.wait_ge(sc_out[s % 4], (b * 2 + s // 4) * 64 + 16)
                    for j in range(4):
                        ins = V.tensor_scalar(tn[s % 4][:, j, :], y1[s % 2][:, j, :], st[:, j, 6:7], st[:, j, 14:15],
                                              ALU.subtract, ALU.mult)
                    ins.then_inc(tn_done, 1)

                def logit(s):
                    o, done = full(dve, b, ("logit", s))
                    st, sm = stat[:, s % 2, :, :], small[:, s % 2, :, :]
                    oh, lg, cand = sm[:, :, 0:8], sm[:, :, 8:16], sm[:, :, 16:24]
                    d = dlog[:, bass.ds(b * 32 + 4 * s, 4), :]
                    over4 = lambda a: a.rearrange("p (o e) -> p o e", o=1).to_broadcast([128, 4, NE])
                    V.tensor_tensor(lg, o[:, 0:32].rearrange("p (j e) -> p j e", j=4), over4(gate_b[:, :]),
                                    ALU.add).then_inc(done, 1)
                    emptied(dve, b, ("logit", s))
                    link(V.tensor_reduce(st[:, :, 9:10], lg, AX.X, ALU.max))
                    link(V.tensor_tensor(d, lg, st[:, :, 9:10].to_broadcast([128, 4, NE]), ALU.subtract))
                    link(V.tensor_scalar(cand, d, 0.0, None, ALU.is_ge))
                    link(V.tensor_tensor(cand, cand, over4(c_["rev"]), ALU.mult))
                    link(V.tensor_reduce(st[:, :, 10:11], cand, AX.X, ALU.max))
                    V.tensor_tensor(oh, over4(c_["rev"]), st[:, :, 10:11].to_broadcast([128, 4, NE]),
                                    ALU.is_equal).then_inc(oh_done, 1)

                def rank(s):
                    o, done = full(dve, b, ("rank", s))
                    dve.wait_ge(oh_done, b * NT + s + 1)
                    st, sm = stat[:, s % 2, :, :], small[:, s % 2, :, :]
                    oh, pos = sm[:, :, 0:8], sm[:, :, 16:24]
                    at = bass.ds(b * 32 + 4 * s, 4)
                    dve.wait_ge(carried, b * NT + s + 1)
                    link(V.tensor_tensor(pos, o[:, 0:32].rearrange("p (j e) -> p j e", j=4),
                                         carry[:, :].rearrange("p (o e) -> p o e", o=1).to_broadcast([128, 4, NE]), ALU.add))
                    V.tensor_tensor(carry[:, :], carry[:, :], o[:, 32:32 + NE], ALU.add).then_inc(carried, 1)
                    link(V.tensor_tensor(pos, pos, oh, ALU.mult))
                    link(V.tensor_reduce(st[:, :, 11:12], pos, AX.X, ALU.add))
                    link(V.tensor_scalar(st[:, :, 12:13], st[:, :, 10:11], float(-CAP), float(NE * CAP + CAP - 1),
                                         ALU.mult, ALU.add))
                    dve.wait_ge(carried, b * NT + s + 2)
                    dve.sem_inc(done, 1)
                    kp = kept[:, at].rearrange("p (j o) -> p j o", o=1)
                    link(V.tensor_tensor(kp, st[:, :, 11:12], st[:, :, 12:13], ALU.is_le))
                    V.tensor_tensor(gidx[:, at].rearrange("p (j o) -> p j o", o=1), st[:, :, 11:12], st[:, :, 12:13], ALU.min)
                    link(V.tensor_scalar(st[:, :, 13:14], kp, -float(NSLOT), float(NSLOT), ALU.mult, ALU.add))
                    V.tensor_tensor(sidx[:, s % 4, :].rearrange("p (j o) -> p j o", o=1), st[:, :, 11:12], st[:, :, 13:14],
                                    ALU.add).then_inc(sidx_done, 1)

                image(dict(ln=ln, qkv=qkv, tr=tr, out=nothing, vka=lambda h: kv(2 + h), den=dens, attend=attend,
                           proj=proj, logit=logit, rank=rank, flush=lambda t_: turned(dve, b, t_, 7, 1, copy),
                           conv=lambda t_, half: conv_evacuation(dve, b, t_, half, 1, relu, copy)))
                assert here[0] == LINKS, here[0]


def experts(nc, D):
    f32 = mybir.dt.float32
    ALU, ACT = mybir.AluOpType, mybir.ActivationFunctionType
    PER = 2 * NSB
    with ExitStack() as ctx:
        def sb(name, shape, dt=f32):
            return ctx.enter_context(nc.sbuf_tensor(name, shape, dt))

        def sem(name):
            return ctx.enter_context(nc.semaphore(name))

        w1 = [sb(f"w1_{i}", [128, KC, FF]) for i in range(2)]
        w2 = [sb(f"w2_{i}", [128, FT, CH]) for i in range(2)]
        b1 = [sb(f"b1_{i}", [128, FT]) for i in range(2)]
        b2 = [sb(f"b2_{i}", [128, CH]) for i in range(2)]
        rows = [sb(f"rows{i}", [128, 4, CH]) for i in range(2)]
        rowt = [sb(f"rowt{i}", [128, KC, TILE]) for i in range(2)]
        hid = [sb(f"hid{i}", [128, FT, TILE]) for i in range(2)]
        yr = [sb(f"yr{i}", [128, 4, CH]) for i in range(2)]
        ident = sb("ident2", [128, 128])
        prime = sb("prime2", [128, 2, NE])
        Rb = [ctx.enter_context(nc.psum_tensor(f"R{i}", [128, 512], f32)) for i in range(2)]
        Hb = [ctx.enter_context(nc.psum_tensor(f"H{i}", [128, 512], f32)) for i in range(4)]
        Yb = [ctx.enter_context(nc.psum_tensor(f"Y{i}", [128, 512], f32)) for i in range(2)]
        id_in = sem("id_in")
        w_in = [sem(f"ew_in{i}") for i in range(2)]
        rows_in = [sem(f"rows_in{i}") for i in range(2)]
        r_full = [sem(f"r_full{i}") for i in range(2)]
        r_out = [sem(f"r_out{i}") for i in range(2)]
        h_full = [sem(f"h_full{i}") for i in range(4)]
        h_out = [sem(f"h_out{i}") for i in range(4)]
        y_full = [sem(f"y_full{i}") for i in range(2)]
        y_out = [sem(f"y_out{i}") for i in range(2)]
        stored = [sem(f"stored{i}") for i in range(2)]
        block = ctx.enter_context(nc.Block())

        def slots(ap, n):
            return ap[bass.ds(n * TILE, TILE), :].rearrange("(p j) d -> p j d", j=4)

        @block.sync
        def _(sp):
            sp.dma_start(ident[:, :], D["con"][:, CON["ident"][0]:CON["ident"][1]]).then_inc(id_in, 16)
            with sp.Fori(0, NE // 2) as ep:
                for m in range(PER):
                    par, s = m // NSB, m % 2
                    if m % NSB == 0:
                        e = bass.ds(ep * 2 + par, 1)
                        hold(sp, y_full[1], ep * PER + 1 + NSB * par)
                        sp.dma_start(w1[par][:, :, :], D["w1"][e, :, :].rearrange("o (k p) f -> p (o k) f", p=128)).then_inc(w_in[par], 16)
                        sp.dma_start(w2[par][:, :, :], D["w2"][e, :, :].rearrange("o (k p) d -> p (o k) d", p=128)).then_inc(w_in[par], 16)
                        sp.dma_start(b1[par][:, :], D["b1"][e, :, :].rearrange("o p f -> p (o f)")).then_inc(w_in[par], 16)
                        sp.dma_start(b2[par][:, :], D["b2"][e, :].to_broadcast([128, CH])).then_inc(w_in[par], 16)
                    hold(sp, r_full[1], ep * PER + m + 1)
                    sp.dma_start(rows[s][:, :, :], slots(D["slots"], ep * PER + m)).then_inc(rows_in[s], 16)

        @block.gpsimd
        def _(pool):
            for first in [*r_out, *h_out, *y_out]:
                pool.sem_inc(first, 1)
            pool.sem_inc(r_full[1], 2)
            pool.sem_inc(y_full[1], NSB + 1)
            for i in range(2):
                pool.dma_start(prime[:, i, :], D["gate_b"].to_broadcast([128, NE])).then_inc(stored[i], 16)
            with pool.Fori(0, NE // 2) as ep:
                for m in range(PER):
                    for i in range(2):
                        hold(pool, y_out[i], ep * PER + m + 2)
                    pool.dma_start(slots(D["ybuf"], ep * PER + m), yr[m % 2][:, :, :]).then_inc(stored[m % 2], 16)
            for i in range(2):
                hold(pool, stored[i], 16 * NE * NSB // 2 + 16)

        @block.tensor
        def _(pe):
            mm = nc.tensor.matmul
            pe.wait_ge(id_in, 16)
            with pe.Fori(0, NE // 2) as ep:
                def second(m):
                    par, s = m // NSB, m % 2
                    for f in range(FT - 4, FT):
                        pe.wait_ge(h_out[f % 4], 2 * (ep * PER + m) + 3)
                    for i in range(2):
                        pe.wait_ge(y_out[i], ep * PER + m + 1)
                        for j in range(2 * i, 2 * i + 2):
                            for f in range(FT):
                                last = mm(Yb[i][:, 256 * (j % 2):256 * (j % 2) + 256], hid[s][:, f, 128 * j:128 * j + 128],
                                          w2[par][:, f, :], start=f == 0, stop=f == FT - 1)
                        last.then_inc(y_full[i], 1)

                for m in range(PER):
                    par, s = m // NSB, m % 2
                    if m % NSB == 0:
                        pe.wait_ge(w_in[par], ep * 64 + 64)
                    pe.wait_ge(rows_in[s], (ep * NSB + m // 2 + 1) * 16)
                    for k in range(KC):
                        pe.wait_ge(r_out[k], ep * PER + m + 1)
                        for j in range(4):
                            last = nc.tensor.transpose(Rb[k][:, 128 * j:128 * j + 128], rows[s][:, j, 128 * k:128 * k + 128],
                                                       ident[:, :])
                        last.then_inc(r_full[k], 1)
                    if m:
                        second(m - 1)
                    for k in range(KC):
                        pe.wait_ge(r_out[k], ep * PER + m + 2)
                    for f in range(FT):
                        pe.wait_ge(h_out[f % 4], 2 * (ep * PER + m) + f // 4 + 1)
                        for k in range(KC):
                            last = mm(Hb[f % 4][:, :], w1[par][:, k, 128 * f:128 * f + 128], rowt[s][:, k, :],
                                      start=k == 0, stop=k == 1)
                        last.then_inc(h_full[f % 4], 1)
                second(PER - 1)

        def hidden(eng, ep, m, mine, relu):
            par, s = m // NSB, m % 2
            for f in range(mine, FT, 2):
                eng.wait_ge(h_full[f % 4], 2 * (ep * PER + m) + f // 4 + 1)
                relu(hid[s][:, f, :], Hb[f % 4][:, :], b1[par][:, f:f + 1]).then_inc(h_out[f % 4], 1)

        @block.scalar
        def _(act):
            with act.Fori(0, NE // 2) as ep:
                for m in range(PER):
                    act.wait_ge(r_full[0], ep * PER + m + 1)
                    nc.scalar.activation(rowt[m % 2][:, 0, :], Rb[0][:, :], ACT.Copy).then_inc(r_out[0], 1)
                    hidden(act, ep, m, 0, lambda o, i, b_: nc.scalar.activation(o, i, ACT.Relu, bias=b_))

        @block.vector
        def _(dve):
            with dve.Fori(0, NE // 2) as ep:
                def biased(m):
                    par, s = m // NSB, m % 2
                    dve.wait_ge(stored[s], (ep * NSB + m // 2) * 16 + 16)
                    for i in range(2):
                        dve.wait_ge(y_full[i], ep * PER + m + 1 + (NSB + 1) * i)
                        nc.vector.tensor_tensor(yr[s][:, 2 * i:2 * i + 2, :], Yb[i][:, :].rearrange("p (j d) -> p j d", j=2),
                                                b2[par][:, :].rearrange("p (o d) -> p o d", o=1).to_broadcast([128, 2, CH]),
                                                ALU.add).then_inc(y_out[i], 1)

                for m in range(PER):
                    dve.wait_ge(r_full[1], ep * PER + m + 3)
                    nc.vector.tensor_copy(rowt[m % 2][:, 1, :], Rb[1][:, :]).then_inc(r_out[1], 1)
                    if m:
                        biased(m - 1)
                    hidden(dve, ep, m, 1, lambda o, i, b_: nc.vector.tensor_scalar(o, i, b_, 0.0, ALU.add, ALU.max))
                biased(PER - 1)


def combine(nc, keep, D, out):
    f32, u32 = mybir.dt.float32, mybir.dt.uint32
    ALU, ACT, AX = mybir.AluOpType, mybir.ActivationFunctionType, mybir.AxisListType
    dlog, kept, gidx = keep
    with ExitStack() as ctx:
        def sb(name, shape, dt=f32):
            return ctx.enter_context(nc.sbuf_tensor(name, shape, dt))

        def sem(name):
            return ctx.enter_context(nc.semaphore(name))

        NS = 4
        yg = [sb(f"yg{i}", [128, 4, CH]) for i in range(NS)]
        yl = [sb(f"yl{i}", [128, 4, CH]) for i in range(NS)]
        v = [sb(f"v{i}", [128, 4, CH]) for i in range(2)]
        mag = [sb(f"mag{i}", [128, 4, CH]) for i in range(2)]
        lim = [sb(f"lim{i}", [128, 4, CH]) for i in range(2)]
        clip = [sb(f"clip{i}", [128, 4, CH]) for i in range(2)]
        zt = [sb(f"zt{i}", [128, KC, TILE]) for i in range(2)]
        pick = sb("pick", [128, NS, 4], u32)
        wsel = sb("wsel", [128, NS, 4])
        wgt = sb("wgt", [128, TOKENS // 128])
        ident = sb("ident3", [128, 128])
        prime = sb("prime3", [128, 2, NE])
        Pb = [ctx.enter_context(nc.psum_tensor(f"P{i}", [128, 512], f32)) for i in range(4)]
        id_in = sem("id_in3")
        exp_done, chain3, w_done = sem("exp_done"), sem("chain3"), sem("w_done")
        yl_in = [sem(f"yl_in{i}") for i in range(NS)]
        yg_in = [sem(f"yg_in{i}") for i in range(NS)]
        picked = sem("picked")
        v_done, mag_done, z_done = sem("v_done"), sem("mag_done"), sem("z_done")
        p_full = [sem(f"p_full{i}") for i in range(4)]
        p_out = [sem(f"p_out{i}") for i in range(4)]
        o_out = [sem(f"o_out{i}") for i in range(2)]
        block = ctx.enter_context(nc.Block())

        @block.sync
        def _(sp):
            sp.dma_start(ident[:, :], D["con"][:, CON["ident"][0]:CON["ident"][1]]).then_inc(id_in, 16)
            for i in range(2):
                sp.dma_start(prime[:, i, :], D["gate_b"].to_broadcast([128, NE])).then_inc(o_out[i], 16)
            with sp.Fori(0, B) as b:
                def load(u):
                    hold(sp, z_done, b * NT + u + 1)
                    sp.dma_start(yl[u % NS][:, :, :], D["y1"][bass.ds(b * NTOK + u * TILE, TILE), :]
                                 .rearrange("(j p) d -> p j d", p=128)).then_inc(yl_in[u % NS], 16)

                for u in range(NS - 1):
                    load(u)
                for u in range(NT):
                    if u + NS - 1 < NT:
                        load(u + NS - 1)
                    for k in range(KC):
                        hold(sp, p_out[2 * (u % 2) + k], b * 4 + u // 2 + 2)
                    sp.dma_start(out[bass.ds(b, 1), :, u * TILE:(u + 1) * TILE].rearrange("o (k p) n -> p (o k) n", p=128),
                                 zt[u % 2][:, :, :]).then_inc(o_out[u % 2], 16)
            for i in range(2):
                hold(sp, o_out[i], 16 * QUADS // 2 + 16)

        @block.gpsimd
        def _(pool):
            for first in [*p_out, *p_full]:
                pool.sem_inc(first, 1)
            for first in (z_done, v_done):
                pool.sem_inc(first, NS)
            with pool.Fori(0, B) as b:
                for u in range(NT):
                    s = u % NS
                    hold(pool, v_done, b * NT + u + 1)
                    nc.gpsimd.tensor_copy(pick[:, s, :], gidx[:, bass.ds(b * 32 + 4 * u, 4)]).then_inc(picked, 1)
                    hold(pool, picked, b * NT + u + 1)
                    for j in range(4):
                        nc.gpsimd.indirect_dma_start(
                            out=yg[s][:, j, :], out_offset=None, in_=D["ybuf"],
                            in_offset=bass.IndirectOffsetOnAxis(ap=pick[:, s, j:j + 1], axis=0),
                            bounds_check=NSLOT - 1, oob_is_err=False).then_inc(yg_in[s], 16)

        @block.tensor
        def _(pe):
            pe.wait_ge(id_in, 16)
            with pe.Fori(0, B) as b:
                for u in range(NT):
                    pe.wait_ge(z_done, b * NT + u + 1 + NS)
                    for k in range(KC):
                        i = 2 * (u % 2) + k
                        pe.wait_ge(p_out[i], b * 4 + u // 2 + 1)
                        for j in range(4):
                            last = nc.tensor.transpose(Pb[i][:, 128 * j:128 * j + 128], v[u % 2][:, j, 128 * k:128 * k + 128],
                                                       ident[:, :])
                        last.then_inc(p_full[i], 1)

        @block.scalar
        def _(act):
            A = nc.scalar.activation
            A(dlog[:, :, :], dlog[:, :, :], ACT.Exp).then_inc(exp_done, 1)
            act.wait_ge(w_done, 1)
            with act.Fori(0, B) as b:
                for u in range(NT + 1):
                    if u < NT:
                        s = u % NS
                        act.wait_ge(yg_in[s], (b * 2 + u // NS + 1) * 64)
                        act.wait_ge(p_full[2 * (u % 2) + 1], b * 4 + u // 2 + 1)
                        for j in range(4):
                            ins = A(v[u % 2][:, j, :], yg[s][:, j, :], ACT.Copy, scale=wgt[:, bass.ds(b * 32 + 4 * u + j, 1)])
                        ins.then_inc(v_done, 1)
                        act.wait_ge(v_done, b * NT + u + 1 + NS)
                        A(mag[u % 2][:, :, :], v[u % 2][:, :, :], ACT.Abs).then_inc(mag_done, 1)
                    if u:
                        w = u - 1
                        i = 2 * (w % 2)
                        act.wait_ge(p_full[i], b * 4 + w // 2 + 2)
                        act.wait_ge(o_out[w % 2], (b * 4 + w // 2) * 16 + 16)
                        A(zt[w % 2][:, 0, :], Pb[i][:, :], ACT.Copy).then_inc(p_out[i], 1)

        @block.vector
        def _(dve):
            V = nc.vector
            dve.wait_ge(exp_done, 1)
            V.tensor_reduce(wgt[:, :].rearrange("p (n o) -> p n o", o=1), dlog[:, :, :], AX.X, ALU.add).then_inc(chain3, 1)
            dve.wait_ge(chain3, 1)
            V.reciprocal(wgt[:, :], wgt[:, :]).then_inc(chain3, 1)
            dve.wait_ge(chain3, 2)
            V.tensor_tensor(wgt[:, :], wgt[:, :], kept[:, :], ALU.mult).then_inc(w_done, 1)
            with dve.Fori(0, B) as b:
                here = [2]

                def link(ins):
                    here[0] += 1
                    ins.then_inc(chain3, 1)
                    dve.wait_ge(chain3, b * LINKS3 + here[0])

                for u in range(NT + 1):
                    if u < NT:
                        s = u % 2
                        flat = lambda a: a[:, :, :].rearrange("p j d -> p (j d)")
                        vv, mm_, ll, cc, yy = flat(v[s]), flat(mag[s]), flat(lim[s]), flat(clip[s]), flat(yl[u % NS])
                        dve.wait_ge(mag_done, b * NT + u + 1)
                        V.tensor_scalar(ll, vv, FMAX, -FMAX, ALU.min, ALU.max)
                        link(V.tensor_scalar(cc, vv, 1e4, -1e4, ALU.min, ALU.max))
                        V.scalar_tensor_tensor(ll, mm_, FMAX, ll, ALU.is_le, ALU.mult)
                        link(V.scalar_tensor_tensor(cc, mm_, FMAX, cc, ALU.is_gt, ALU.mult))
                        dve.wait_ge(yl_in[u % NS], (b * 2 + u // NS + 1) * 16)
                        link(V.tensor_tensor(ll, ll, cc, ALU.add))
                        V.tensor_tensor(vv, ll, yy, ALU.add).then_inc(z_done, 1)
                    if u:
                        w = u - 1
                        i = 2 * (w % 2) + 1
                        dve.wait_ge(p_full[i], b * 4 + w // 2 + 2)
                        dve.wait_ge(o_out[w % 2], (b * 4 + w // 2) * 16 + 16)
                        V.tensor_copy(zt[w % 2][:, 1, :], Pb[i][:, :]).then_inc(p_out[i], 1)
                assert here[0] == 2 + LINKS3, here[0]


LINKS = NT * 14
LINKS3 = NT * 3


def metaformer(nc, D, out):
    f32, u32 = mybir.dt.float32, mybir.dt.uint32
    D["slots"] = nc.dram_tensor("slots", (NSLOT, CH), f32, kind="Internal").ap()
    D["ybuf"] = nc.dram_tensor("ybuf", (NSLOT, CH), f32, kind="Internal").ap()
    D["y1"] = nc.dram_tensor("y1", (TOKENS, CH), f32, kind="Internal").ap()
    with ExitStack() as ctx:
        keep = (ctx.enter_context(nc.sbuf_tensor("dlog", [128, TOKENS // 128, NE], f32)),
                ctx.enter_context(nc.sbuf_tensor("kept", [128, TOKENS // 128], f32)),
                ctx.enter_context(nc.sbuf_tensor("gidx", [128, TOKENS // 128], u32)))
        mixer_and_dispatch(nc, keep, D)
        experts(nc, D)
        combine(nc, keep, D, out)


def constants():
    import numpy as np
    con = np.zeros((128, NCON), np.float32)
    p = np.arange(128)
    con[:, slice(*CON["ident"])] = np.eye(128)
    con[:, slice(*CON["gmask"])] = p[:, None] // 8 == p[None, :] // 8
    con[:, slice(*CON["tri"])] = p[:, None] <= p[None, :]
    con[:, slice(*CON["gm16"])] = p[:, None] // 8 == np.arange(16)[None, :]
    a = CON["spread"][0]
    for c in range(4):
        con[16 * c + p // 8, a + 128 * c + p] = 1.0
    con[:, slice(*CON["carry0"])] = np.arange(NE)[None, :] * CAP - 1
    con[:, slice(*CON["rev"])] = NE - np.arange(NE)[None, :]
    return con


def lay_out(x, w_qkv, w_dw, w_pw, w_proj, gate_w, b1):
    import numpy as np
    ch = np.array([[24 * (16 * h + g) + 8 * "qkv".index(kind) + c for g in range(NG) for c in range(8)] for kind, h in CHUNKS])
    wq = np.asarray(w_qkv).reshape(768, CH)[ch]
    wq = wq.transpose(2, 0, 1).reshape(KC, 128, NCHUNK, 128).transpose(1, 0, 2, 3)
    wp = np.asarray(w_proj).reshape(CH, 512).T.reshape(4, 128, CH).transpose(1, 0, 2)
    pad = np.zeros((768, 11, 11), np.float32)
    pad[:, 3:8, 3:8] = np.asarray(w_dw).reshape(768, 5, 5)
    py, qa, qq = np.arange(4), np.arange(2), np.arange(4)
    idx = 4 * qa[None, :, None] + py[:, None, None] - qq[None, None, :] + 3
    dw = pad[ch][:, :, idx][:, :, :, :, :, idx]
    dw = dw.reshape(NCHUNK, NG, 8, 4, 2, 4, 4, 2, 4).transpose(0, 2, 3, 6, 1, 4, 7, 5, 8)
    dw = dw.reshape(NCHUNK, 128, NG, 64)
    pw = np.asarray(w_pw).reshape(768, 8)[ch].reshape(NCHUNK, NG, 8, 8)
    pw = np.broadcast_to(pw.transpose(3, 0, 1, 2)[:, None], (8, POS, NCHUNK, NG, 8)).reshape(128, NCHUNK, NG, 8)
    gw = np.asarray(gate_w).reshape(KC, 128, NE).transpose(1, 0, 2)
    return dict(x=np.asarray(x).reshape(B, CH, NTOK), wq=wq, wp=wp, dw=dw, pw=pw, gate_w=gw,
                b1=np.asarray(b1).reshape(NE, FT, 128).transpose(0, 2, 1))


def kernel(**inputs):
    import numpy as np
    import concourse.bacc as bacc
    from concourse.bass_utils import run_bass_kernel_spmd

    i = inputs
    arrays = lay_out(i["x"], i["L0_conv_w_qkv"], i["L0_conv_w_dw"], i["L0_conv_w_pw"], i["L0_conv_w_proj"],
                     i["L0_ffn_gate_w"], i["L0_ffn_b1"])
    for name in ("bn_gamma", "bn_beta", "bn_mean", "bn_var"):
        arrays[name] = np.asarray(i["L0_conv_" + name]).reshape(1, CH)
    arrays["gate_b"] = np.asarray(i["L0_ffn_gate_b"]).reshape(1, NE)
    arrays["w1"], arrays["w2"], arrays["b2"] = (np.asarray(i["L0_ffn_" + n]) for n in ("w1", "w2", "b2"))
    arrays["con"] = constants()
    arrays = {"in_" + k: np.ascontiguousarray(v) for k, v in arrays.items()}

    nc = bacc.Bacc("TRN2", target_bir_lowering=False, num_devices=1)
    D = {k[3:]: nc.dram_tensor(k, v.shape, mybir.dt.from_np(v.dtype), kind="ExternalInput").ap() for k, v in arrays.items()}
    out = nc.dram_tensor("out", (B, CH, NTOK), mybir.dt.float32, kind="ExternalOutput").ap()
    metaformer(nc, D, out)
    r = run_bass_kernel_spmd(nc, [arrays], core_ids=[0])
    return np.asarray(r.results[0]["out"]).reshape(B, CH, HW, HW)
```

```python
import concourse.bass as bass
from concourse import mybir
from contextlib import ExitStack

B, CH, HW = 8, 256, 64
NTOK = HW * HW
KC = CH // 128
TILE = 512
NT = NTOK // TILE
BLK = 4
POS = BLK * BLK
NB = HW // BLK
GRID = NB + 1
GG = GRID * GRID
NGRID = POS * GG
NTRT = -(-NGRID // 128)
NTR = -(-NTRT // 4)
NCHUNK = 6
NG = 16
CHUNKS = [("k", 0), ("v", 0), ("k", 1), ("v", 1), ("q", 0), ("q", 1)]
NE, CAP, FF = 8, 5120, 1024
FT = FF // 128
NSLOT = NE * CAP
TOKENS = B * NTOK
QUADS = TOKENS // TILE
NSB = CAP // TILE
FMAX = 3.4028234663852886e38

CON = {}
_at = 0
for _name, _n in (("ident", 128), ("gmask", 128), ("tri", 128), ("gm16", 16), ("spread", 4 * 128),
                  ("carry0", NE), ("rev", NE), ("row7", 15)):
    CON[_name] = (_at, _at + _n)
    _at += _n
NCON = _at


class Ring:

    def __init__(self, size, keys):
        self.size, self.at = size, {k: (n % size, n // size) for n, k in enumerate(keys)}
        assert len(keys) % size == 0
        self.per = len(keys) // size

    def __getitem__(self, key):
        return self.at[key]


def nothing(*_):
    pass


def hold(eng, sem, value):
    eng.wait_ge(sem, value)
    eng.nop(nofuse=True)


def layer_norm(ph):
    for u in range(NT + 1):
        if u < NT:
            ph["mu"](u)
        if u == 5:
            ph["recip"](0)
        if u:
            ph["var"](u - 1)
        if u == 4:
            ph["root"](0)
        if u in (6, 7):
            for v in range(2):
                ph["norm"](2 * (u - 6) + v)
    ph["root"](1)
    ph["recip"](1)
    for u in range(4, NT):
        ph["norm"](u)


def image(ph):
    ph["ln"]()
    ph["qkv"](0)
    ph["tr"](0)
    for t in range(NCHUNK):
        ph["conv"](t, 0)
        if t + 1 < NCHUNK:
            ph["qkv"](t + 1)
        ph["conv"](t, 1)
        if CHUNKS[t][0] == "k":
            ph["tr"](t + 1)
            ph["flush"](t)
        if CHUNKS[t][0] == "v":
            ph["flush"](t)
            ph["vka"](CHUNKS[t][1])
            if CHUNKS[t + 1][0] == "k":
                ph["tr"](t + 1)
    ph["out"]()
    ph["den"](0)
    ph["recip"](0)
    for s in range(NT + 3):
        if s + 1 < NT:
            ph["den"](s + 1)
        if s >= 3:
            ph["rank"](s - 3)
        if 2 <= s <= NT + 1:
            ph["turn"](s - 2)
        if s < NT:
            ph["attend"](s)
        if 2 <= s <= NT + 1:
            ph["logit"](s - 2)
        if s + 1 < NT:
            ph["recip"](s + 1)
        if 1 <= s <= NT:
            ph["proj"](s - 1)


def psum_rings():
    main, turn = [], []
    layer_norm(dict(mu=lambda u: main.append(("mu", u)), norm=lambda u: main.append(("norm", u)),
                    var=nothing, root=nothing, recip=nothing))
    image(dict(ln=nothing, recip=nothing, out=nothing, vka=nothing,
               qkv=lambda t: main.extend(("qkv", t, w) for w in range(NT)),
               tr=lambda t: turn.extend(("tr", t, m) for m in range(NTR)),
               conv=lambda t, half: turn.extend(("ct", t, p - 1) for p in range(4 * half, 4 * half + 4)
                                                if p and CHUNKS[t][0] != "q"),
               flush=lambda t: turn.append(("ct", t, 7)),
               den=lambda s: main.append(("den", s)),
               attend=lambda s: main.extend((k, s, c) for c in range(4) for k in ("num", "inv")),
               proj=lambda s: main.extend(("proj", s, i) for i in range(2)),
               turn=lambda s: turn.extend(("tn", s, k) for k in range(2)),
               logit=lambda s: main.append(("logit", s)),
               rank=lambda s: main.append(("rank", s))))
    return Ring(3, main), Ring(2, turn)


def mixer_and_dispatch(nc, keep, D):
    f32, u32 = mybir.dt.float32, mybir.dt.uint32
    ALU, ACT, AX = mybir.AluOpType, mybir.ActivationFunctionType, mybir.AxisListType
    G, T = psum_rings()
    with ExitStack() as ctx:
        def sb(name, shape, dt=f32):
            return ctx.enter_context(nc.sbuf_tensor(name, shape, dt))

        def sem(name):
            return ctx.enter_context(nc.semaphore(name))

        xt = [sb(f"xt{i}", [128, KC, TILE]) for i in range(2)]
        xn = sb("xn", [128, KC, NTOK])
        grid = sb("grid", [128, BLK, BLK, GRID, GRID])
        conv_in = sb("conv_in", [128, NG, GRID, GRID])
        toep = sb("toep", [128, 4, 4, 128])
        dwt = sb("dwt", [128, 2, NG, 64])
        pwt = sb("pwt", [128, NCHUNK, NG, 8])
        kt = sb("kt", [128, NTRT * 128])
        kta = sb("kta", [128, 2, POS, 128])
        vt = sb("vt", [128, 2, 4, 129])
        qe = sb("qe", [128, 4, 256])
        q0 = sb("q0", [128, 2, NTOK])
        wq = sb("wq", [128, KC, NCHUNK, 128])
        wp = sb("wp", [128, 4, CH])
        vk = sb("vk", [128, 4, 128])
        dn = sb("dn", [128, 4, 64])
        ones = sb("ones", [128, 128])
        mean_w = sb("mean_w", [128, 128])
        eps = sb("eps", [128, 3])
        bias = sb("bias", [128, CH])
        bnr = sb("bnr", [128, 4, CH])
        gate = sb("gate", [128, KC, NE])
        gate_b = sb("gate_b", [128, NE])
        carry = sb("carry", [128, NE])
        small = sb("small", [128, 2, 4, 24])
        stat = sb("stat", [128, 2, 4, 16])
        sidx = sb("sidx", [128, 4, 4], u32)
        con = sb("con", [128, NCON])
        dlog, kept, gidx = keep
        c_ = {k: con[:, a:b] for k, (a, b) in CON.items()}
        ident = c_["ident"]
        ktn = kt[:, :].rearrange("p (m c) -> p m c", m=NTRT)
        vta = kt[:, 0:32 * 129].rearrange("p (h s c) -> p h s c", h=2, s=POS)
        ktf = kta[:, :, :, :].rearrange("p h s c -> p (h s c)")
        std = [kt[0:8, i * 256:(i + 1) * 256] for i in range(2)]
        den = [kt[0:64, i * 512:(i + 1) * 512] for i in range(2)]
        tnt = kt[:, 1024:2048].rearrange("p (k n) -> p k n", k=KC)
        cif = conv_in[:, :, :, :].rearrange("p g i j -> p (g i j)")
        y1 = [cif[:, i * 1024:(i + 1) * 1024].rearrange("p (j d) -> p j d", j=4) for i in range(2)]
        ao = [a.rearrange("p (c n) -> p c n", c=4) for a in (cif[:, 2048:4096], kt[:, 2048:4096])]
        sq = [cif[:, 2048 + i * 1024:3072 + i * 1024].rearrange("p (k n) -> p k n", k=KC) for i in range(2)]
        num = [cif[:, 4096:4608], kt[:, 4096:4608]]
        tn = [ktf[:, i * 1024:(i + 1) * 1024].rearrange("p (j d) -> p j d", j=4) for i in range(4)]
        qr = [q0[:, 0, :], xn[:, 0, :], q0[:, 1, :], xn[:, 1, :]]
        zero = q0[:, 0, 0:1024]

        Gb = [ctx.enter_context(nc.psum_tensor(f"G{i}", [128, 512], f32)) for i in range(3)]
        Vb = [ctx.enter_context(nc.psum_tensor(f"V{i}", [128, 512], f32)) for i in range(2)]
        Tb = [ctx.enter_context(nc.psum_tensor(f"T{i}", [128, 512], f32)) for i in range(2)]
        Kb = ctx.enter_context(nc.psum_tensor("K0", [128, 512], f32))
        Sb = [Kb, Vb[0]]

        g_full = [sem(f"g_full{i}") for i in range(3)]
        g_out = [sem(f"g_out{i}") for i in range(3)]
        t_full = [sem(f"t_full{i}") for i in range(2)]
        t_out = [sem(f"t_out{i}") for i in range(2)]
        v_out = [sem(f"v_out{i}") for i in range(2)]
        conv_done = sem("conv_done")
        k_full, k_out = sem("k_full"), sem("k_out")
        w_in = sem("w_in")
        setup = sem("setup")
        zset, zfill = sem("zset"), sem("zfill")
        begin_at_1 = [*g_out, *t_out, *v_out]
        prime = sb("prime", [128, 10, NE])
        xt_in = [sem(f"xt_in{i}") for i in range(2)]
        sq_done = sem("sq_done")
        ss_done, root_done, inv_done = sem("ss_done"), sem("root_done"), sem("inv_done")
        ci_in = [sem(f"ci_in{g}") for g in range(NG)]
        dwt_in = [sem(f"dwt_in{i}") for i in range(2)]
        toep_done = sem("toep_done")
        qe_out = [sem(f"qe_out{i}") for i in range(4)]
        rec_done = sem("rec_done")
        y1_out = [sem(f"y1_out{i}") for i in range(2)]
        var_done, sd_done, tn_done = sem("var_done"), sem("sd_done"), sem("tn_done")
        oh_done, sidx_done = sem("oh_done"), sem("sidx_done")
        sc_out = [sem(f"sc_out{i}") for i in range(4)]
        carried = sem("carried")
        bn_eps, bn_sd = sem("bn_eps"), sem("bn_sd")
        chain0 = sem("chain0")
        chain = sem("chain")

        XT = Ring(2, [("ln", u) for u in range(NT)] + [("proj", u) for u in range(NT)])

        def full(eng, b, key):
            bank, n = G[key]
            eng.wait_ge(g_full[bank], b * G.per + n + 1)
            return Gb[bank], g_out[bank]

        def tfull(eng, b, key):
            bank, n = T[key]
            eng.wait_ge(t_full[bank], b * T.per + n + 1)
            return Tb[bank], t_out[bank]

        def emptied(eng, b, key):
            bank, n = G[key]
            hold(eng, g_out[bank], b * G.per + n + 2)

        def grid_ready(eng, b, t_):
            for w in (NT - 3, NT - 2, NT - 1):
                emptied(eng, b, ("qkv", t_, w))

        def tiles_of(m4):
            return [(j, 4 * m4 + j, min(128, NGRID - 128 * (4 * m4 + j))) for j in range(4) if 4 * m4 + j < NTRT]

        def block_rows(u):
            return xn[:, :, :].rearrange("p k (s n) -> p k s n", s=POS)[:, :, :, 32 * u:32 * u + 32]

        def grid_view(w):
            qy, pair = w // 2, w % 2
            py, i0 = (qy + 2) % BLK, (qy + 2) // BLK
            px, j0 = (2, 0) if pair == 0 else (0, 1)
            return grid[:, py, px:px + 2, i0:i0 + NB, j0:j0 + NB]

        block = ctx.enter_context(nc.Block())

        @block.sync
        def _(sp):
            loads = [(con[:, :], D["con"]), (wq[:, :, :, :], D["wq"]), (wp[:, :, :], D["wp"]), (pwt[:, :, :, :], D["pw"]),
                     (gate[:, :, :], D["gate_w"]), (gate_b[:, :], D["gate_b"].to_broadcast([128, NE]))]
            loads += [(bnr[:, i, :], D[k].to_broadcast([128, CH])) for i, k in
                      enumerate(("bn_gamma", "bn_beta", "bn_mean", "bn_var"))]
            for dst, src in loads:
                sp.dma_start(dst, src).then_inc(w_in, 16)
            assert len(loads) == 10
            for i, first in enumerate([*qe_out, *y1_out]):
                sp.dma_start(prime[:, i, :], D["gate_b"].to_broadcast([128, NE])).then_inc(first, 16)
            with sp.Fori(0, B) as b:
                def load_x(key):
                    s, n = XT[key]
                    if key[0] == "ln" and key[1] >= 2:
                        emptied(sp, b, ("mu", key[1] - 2))
                    if key[0] == "proj" and key[1] < 2:
                        emptied(sp, b, ("mu", NT - 2 + key[1]))
                    sp.dma_start(xt[s][:, :, :], D["x"][bass.ds(b, 1), :, key[1] * TILE:(key[1] + 1) * TILE]
                                 .rearrange("o (k p) n -> p (o k) n", p=128)).then_inc(xt_in[s], 16)

                def load_dwt(t_):
                    if t_ < 2:
                        hold(sp, toep_done, b * 96 + 1)
                    else:
                        hold(sp, toep_done, b * 96 + 16 * (t_ - 1) + 1)
                    sp.dma_start(dwt[:, t_ % 2, :, :], D["dw"][t_, :, :, :]).then_inc(dwt_in[t_ % 2], 16)

                def regroup(t_, half):
                    if half == 0:
                        grid_ready(sp, b, t_)
                        if t_ == 0:
                            for i in range(2):
                                hold(sp, y1_out[i], b * 64 + 16)
                    for g in range(8 * half, 8 * half + 8):
                        hold(sp, conv_done, b * 96 + 16 * t_ + g + 1)
                        sp.dma_start(conv_in[:, g, :, :].rearrange("p i j -> p (i j)"),
                                     grid[8 * g:8 * g + 8, :, :, :, :].rearrange("p y x i j -> p (y x) (i j)"))\
                            .then_inc(ci_in[g], 16)

                def q_back(t_, half):
                    h = CHUNKS[t_][1]
                    for g in range(8 * half, 8 * half + 8):
                        n = NG * t_ + g
                        hold(sp, v_out[(n // 2) % 2], b * 24 + n // 4 + 2)
                        sp.dma_start(qr[2 + h][8 * g:8 * g + 8, :].rearrange("p (s n) -> p s n", s=POS),
                                     qe[:, g % 4, :]).then_inc(qe_out[g % 4], 16)

                load_x(("ln", 0))
                load_x(("ln", 1))
                load_dwt(0)
                load_dwt(1)
                for u in range(2, NT):
                    load_x(("ln", u))
                regroup(0, 0)
                regroup(0, 1)
                for t_ in range(1, NCHUNK):
                    if CHUNKS[t_ - 1][0] == "q":
                        q_back(t_ - 1, 0)
                    regroup(t_, 0)
                    if CHUNKS[t_ - 1][0] == "q":
                        q_back(t_ - 1, 1)
                    regroup(t_, 1)
                    if t_ + 1 < NCHUNK:
                        load_dwt(t_ + 1)
                q_back(5, 0)
                q_back(5, 1)
                load_x(("proj", 0))
                load_x(("proj", 1))
                for u in range(NT):
                    emptied(sp, b, ("proj", u, 0))
                    emptied(sp, b, ("proj", u, 1))
                    sp.dma_start(D["y1"][bass.ds(b * NTOK + u * TILE, TILE), :].rearrange("(j p) d -> p j d", p=128),
                                 y1[u % 2]).then_inc(y1_out[u % 2], 16)
                    if u + 2 < NT:
                        load_x(("proj", u + 2))
            for i in range(2):
                hold(sp, y1_out[i], B * 64 + 16)

        @block.gpsimd
        def _(pool):
            for first in [*begin_at_1, k_out, toep_done, carried]:
                pool.sem_inc(first, 1)
            for i, first in enumerate(sc_out):
                pool.dma_start(prime[:, 6 + i, :], D["gate_b"].to_broadcast([128, NE])).then_inc(first, 16)
            nc.gpsimd.memset(zero, 0.0).then_inc(zset, 1)
            nc.gpsimd.memset(grid[:, :, :, :, :], 0.0).then_inc(setup, 1)
            nc.gpsimd.memset(ones[:, :], 1.0).then_inc(setup, 1)
            nc.gpsimd.memset(mean_w[:, :], 1.0 / CH).then_inc(setup, 1)
            nc.gpsimd.memset(dn[:, :, :], 0.0).then_inc(setup, 1)
            nc.gpsimd.memset(vt[:, :, :, 128:129], 1.0).then_inc(setup, 1)
            nc.gpsimd.memset(eps[:, 0:1], 1e-6).then_inc(setup, 1)
            nc.gpsimd.memset(eps[:, 1:2], 1e-5).then_inc(setup, 1)
            nc.gpsimd.memset(eps[:, 2:3], 1e-15).then_inc(setup, 1)
            hold(pool, w_in, 160)
            hold(pool, zfill, 16 * (NSLOT // 512))
            with pool.Fori(0, B) as b:
                for t_ in range(NCHUNK):
                    hold(pool, dwt_in[t_ % 2], b * 48 + 16 * (t_ // 2) + 16)
                    for g in range(NG):
                        n = NG * t_ + g
                        hold(pool, conv_done, b * 96 + n + 13)
                        nc.gpsimd.tensor_tensor(
                            toep[:, n % 4, :, :].rearrange("p q (c s) -> p q c s", c=8),
                            dwt[:, t_ % 2, g, :].rearrange("p (q o s) -> p q o s", q=4, o=1).to_broadcast([128, 4, 8, POS]),
                            pwt[:, t_, g, :].rearrange("p (o c s) -> p o c s", o=1, s=1).to_broadcast([128, 4, 8, POS]),
                            ALU.mult).then_inc(toep_done, 1)
                for u in range(NT):
                    hold(pool, sidx_done, b * 8 + u + 1)
                    for j in range(4):
                        nc.gpsimd.indirect_dma_start(
                            out=D["slots"], out_offset=bass.IndirectOffsetOnAxis(ap=sidx[:, u % 4, j:j + 1], axis=0),
                            in_=tn[u % 4][:, j, :], in_offset=None,
                            bounds_check=NSLOT - 1, oob_is_err=False).then_inc(sc_out[u % 4], 16)
            for i in range(4):
                hold(pool, sc_out[i], B * 128 + 16)

        @block.tensor
        def _(pe):
            def bank(b, key):
                i, n = G[key]
                pe.wait_ge(g_out[i], b * G.per + n + 1)
                return Gb[i], g_full[i]

            def tbank(b, key):
                i, n = T[key]
                pe.wait_ge(t_out[i], b * T.per + n + 1)
                return Tb[i], t_full[i]

            mm = nc.tensor.matmul
            pe.sem_inc(conv_done, 16)
            pe.wait_ge(w_in, 160)
            pe.wait_ge(setup, 8 + 3)
            with pe.Fori(0, B) as b:
                def mu(u):
                    s, n = XT[("ln", u)]
                    pe.wait_ge(xt_in[s], (b * XT.per + n) * 16 + 16)
                    o, done = bank(b, ("mu", u))
                    for k in range(KC):
                        last = mm(o[:, :], mean_w[:, :], xt[s][:, k, :], start=k == 0, stop=k == 1)
                    last.then_inc(done, 1)

                def var(u):
                    pe.wait_ge(sq_done, b * NT + u + 1)
                    if u == 4:
                        pe.wait_ge(v_out[0], b * 24 + 1)
                    for h in range(2):
                        at = 7 - (2 * (u % 4) + h)
                        for k in range(KC):
                            last = mm(Sb[u // 4][0:8, 0:256], c_["row7"][:, at:at + 8], sq[u % 2][:, k, 256 * h:256 * h + 256],
                                      start=u % 4 + h + k == 0, stop=u % 4 + h + k == 5)
                    last.then_inc(ss_done, 1)

                def norm(u):
                    if u % 4 == 0:
                        pe.wait_ge(inv_done, b * 2 + u // 4 + 1)
                    o, done = bank(b, ("norm", u))
                    for h in range(2):
                        r = 2 * (u % 4) + h
                        last = mm(o[:, 256 * h:256 * h + 256], ident[0:8, r:r + 1].to_broadcast([8, 128]), std[u // 4],
                                  start=True, stop=True)
                    last.then_inc(done, 1)

                def ln():
                    layer_norm(dict(mu=mu, var=var, root=nothing, recip=nothing, norm=norm))
                    for u in range(NT - 3, NT):
                        emptied(pe, b, ("norm", u))

                def qkv(t_):
                    if t_:
                        for g in range(8, NG):
                            pe.wait_ge(ci_in[g], b * 96 + 16 * t_)
                    for w in range(NT):
                        o, done = bank(b, ("qkv", t_, w))
                        for k in range(KC):
                            last = mm(o[:, :], wq[:, k, t_, :], xn[:, k, w * TILE:(w + 1) * TILE],
                                      start=k == 0, stop=k == 1)
                        last.then_inc(done, 1)

                def tr(t_):
                    kind, h = CHUNKS[t_]
                    grid_ready(pe, b, t_)

                    def own_vk(m4):
                        i, n = T[("tr", t_, m4)]
                        pe.wait_ge(t_out[i], b * T.per + n + 2)
                        for j, m, n_ in tiles_of(m4):
                            last = mm(Kb[:, 0:129], ktn[0:n_, m, :], vt[0:n_, m4 % 2, j, :], start=m == 0, stop=m == NTRT - 1)
                        if m4 == NTR - 1:
                            last.then_inc(k_full, 1)

                    if kind == "v":
                        pe.wait_ge(k_out, b * 4 + 2 * h + 1)
                    flat = grid[:, :, :, :, :].rearrange("p y x i j -> p (y x i j)")
                    for m4 in range(NTR):
                        o, done = tbank(b, ("tr", t_, m4))
                        for j, m, n_ in tiles_of(m4):
                            last = nc.tensor.transpose(o[0:n_, 128 * j:128 * j + 128], flat[:, 128 * m:128 * m + n_], ident)
                        last.then_inc(done, 1)
                        if kind == "v" and m4:
                            own_vk(m4 - 1)
                    if kind == "v":
                        own_vk(NTR - 1)

                def conv(t_, half):
                    for g in range(8 * half, 8 * half + 8):
                        n = NG * t_ + g
                        pe.wait_ge(ci_in[g], b * 96 + 16 * (t_ + 1))
                        pe.wait_ge(toep_done, b * 96 + n + 2)
                        i = (n // 2) % 2
                        if g % 2 == 0:
                            pe.wait_ge(v_out[i], b * 24 + n // 4 + 1)
                        o = Vb[i]
                        at = 256 * (g % 2)
                        for q in range(4):
                            y, x = q // 2, q % 2
                            last = mm(o[:, at:at + 256], toep[:, n % 4, q, :], conv_in[:, g, y:y + NB, x:x + NB],
                                      start=q == 0, stop=q == 3)
                        last.then_inc(conv_done, 1)
                        if g % 2 and g > 1 and CHUNKS[t_][0] != "q":
                            turn_conv(t_, g // 2 - 1)

                def turn_conv(t_, p):
                    n = NG * t_ + 2 * p
                    pe.wait_ge(v_out[(n // 2) % 2], b * 24 + n // 4 + 2)
                    o, done = tbank(b, ("ct", t_, p))
                    for i in range(4):
                        last = nc.tensor.transpose(o[:, 128 * i:128 * i + 128],
                                                   qe[:, (2 * p + i // 2) % 4, 128 * (i % 2):128 * (i % 2) + 128], ident)
                    last.then_inc(done, 1)

                def vka(h):
                    pe.wait_ge(k_out, b * 4 + 2 * h + 2)
                    for p in (6, 7):
                        i, n = T[("ct", 2 * h + 1, p)]
                        pe.wait_ge(t_out[i], b * T.per + n + 2)
                    for m in range(32):
                        hf, s = m // POS, m % POS
                        last = mm(Kb[:, 0:129], kta[:, hf, s, :], vta[:, hf, s, :], start=m == 0, stop=m == 31)
                    last.then_inc(k_full, 1)

                def out():
                    for i in range(4):
                        pe.wait_ge(qe_out[i], b * 128 + 128 + 16)
                    pe.wait_ge(k_out, b * 4 + 5)


                def tile_of(c, s):
                    return qr[c].rearrange("p (s n) -> p s n", s=POS)[:, :, 32 * s:32 * s + 32]

                def dens(s):
                    o, done = bank(b, ("den", s))
                    for c in range(4):
                        last = mm(o[0:64, :], dn[:, c, :], tile_of(c, s), start=c == 0, stop=c == 3)
                    last.then_inc(done, 1)

                def attend(s):
                    spread = c_["spread"].rearrange("p (c m) -> p c m", c=4)
                    for c in range(4):
                        o, done = bank(b, ("num", s, c))
                        mm(o[:, :], vk[:, c, :], tile_of(c, s), start=True, stop=True).then_inc(done, 1)
                        if c == 0:
                            pe.wait_ge(rec_done, b * NT + s + 1)
                        o, done = bank(b, ("inv", s, c))
                        mm(o[:, :], spread[0:64, c, :], den[s % 2], start=True, stop=True).then_inc(done, 1)

                def proj(s):
                    emptied(pe, b, ("inv", s, 3))
                    sl, n = XT[("proj", s)]
                    pe.wait_ge(xt_in[sl], (b * XT.per + n) * 16 + 16)
                    for i in range(2):
                        o, done = bank(b, ("proj", s, i))
                        for j in range(2):
                            at = (2 * i + j) * 128
                            oo = o[:, 256 * j:256 * j + 256]
                            for c in range(4):
                                mm(oo, ao[s % 2][:, c, at:at + 128], wp[:, c, :], start=c == 0, stop=False)
                            for k in range(KC):
                                last = mm(oo[:, 128 * k:128 * k + 128], xt[sl][:, k, at:at + 128], ident,
                                          start=False, stop=k == 1)
                        last.then_inc(done, 1)

                def turn(s):
                    pe.wait_ge(tn_done, b * NT + s + 1)
                    for k in range(KC):
                        o, done = tbank(b, ("tn", s, k))
                        for j in range(4):
                            last = nc.tensor.transpose(o[:, 128 * j:128 * j + 128], tn[s % 4][:, j, 128 * k:128 * k + 128], ident)
                        last.then_inc(done, 1)

                def logit(s):
                    o, done = bank(b, ("logit", s))
                    for k in range(KC):
                        i, n = T[("tn", s, k)]
                        pe.wait_ge(t_out[i], b * T.per + n + 2)
                    for j in range(4):
                        for k in range(KC):
                            last = mm(o[:, NE * j:NE * j + NE], tnt[:, k, 128 * j:128 * j + 128], gate[:, k, :],
                                      start=k == 0, stop=k == 1)
                    last.then_inc(done, 1)

                def rank(s):
                    pe.wait_ge(oh_done, b * NT + s + 1)
                    oh = small[:, s % 2, :, 0:NE]
                    o, done = bank(b, ("rank", s))
                    mm(o[:, 0:32], c_["tri"], oh, start=True, stop=False)
                    for j in range(3):
                        for jj in range(j + 1, 4):
                            mm(o[:, NE * jj:NE * jj + NE], ones[:, :], oh[:, j, :], start=False, stop=(j == 2))
                    for j in range(4):
                        last = mm(o[:, 32:32 + NE], ones[:, :], oh[:, j, :], start=j == 0, stop=j == 3)
                    last.then_inc(done, 1)

                image(dict(ln=ln, qkv=qkv, tr=tr, conv=conv, flush=lambda t_: turn_conv(t_, 7), vka=vka, out=out,
                           den=dens, recip=nothing, attend=attend, proj=proj, turn=turn, logit=logit, rank=rank))

        def conv_evacuation(eng, b, t_, half, mine, relu, copy):
            kind, h = CHUNKS[t_]
            for p in range(4 * half, 4 * half + 4):
                if kind != "q" and p:
                    turned(eng, b, t_, p - 1, mine, copy)
                if p % 2 != mine:
                    continue
                g = 2 * p
                n = NG * t_ + 2 * p
                i = (n // 2) % 2
                eng.wait_ge(conv_done, b * 96 + n + 2 + 16)
                if kind != "q" and p >= 2:
                    j, m = T[("ct", t_, p - 2)]
                    eng.wait_ge(t_full[j], b * T.per + m + 1)
                elif kind != "q" and t_ > 0 or t_ == 4 and p < 2:
                    j, m = T[("ct", t_ - 1, 6 + p)]
                    eng.wait_ge(t_full[j], b * T.per + m + 1)
                elif kind != "q":
                    for k in (g % 4, g % 4 + 1):
                        eng.wait_ge(qe_out[k], b * 128 + 16)
                else:
                    for k in (g % 4, g % 4 + 1):
                        eng.wait_ge(qe_out[k], (b * 8 + 4 * h + g // 4) * 16 + 16)
                (copy if kind == "v" else relu)(qe[:, g % 4:g % 4 + 2, :].rearrange("p g n -> p (g n)"), Vb[i][:, :], v_out[i])

        def turned(eng, b, t_, p, mine, copy):
            if p % 2 != mine:
                return
            if t_ == 0 and p < 2:
                for i in range(4):
                    eng.wait_ge(sc_out[i], b * 128 + 16)
            o, done = tfull(eng, b, ("ct", t_, p))
            dst = kta if CHUNKS[t_][0] == "k" else vta
            for hf in range(2):
                d = dst[:, hf, :, 16 * p:16 * p + 16].rearrange("p s (g c) -> p g c s", g=2)
                copy(d, o[:, :].rearrange("p (g h c s) -> p g h c s", g=2, h=2, c=8)[:, :, hf, :, :], done if hf else None)

        @block.scalar
        def _(act):
            A = nc.scalar.activation
            act.wait_ge(zset, 1)
            for i in range(NSLOT * CH // (128 * 1024)):
                act.dma_start(D["slots"][i * 512:(i + 1) * 512, :].rearrange("(p r) d -> p (r d)", p=128),
                              zero).then_inc(zfill, 16)
            act.wait_ge(setup, 8)
            act.wait_ge(bn_eps, 1)
            A(bnr[:, 3, :], bnr[:, 3, :], ACT.Sqrt, bias=eps[:, 1:2]).then_inc(bn_sd, 1)
            with act.Fori(0, B) as b:
                def relu(dst, src, done):
                    A(dst, src, ACT.Relu).then_inc(done, 1)

                def copy(dst, src, done):
                    ins = A(dst, src, ACT.Copy)
                    if done:
                        ins.then_inc(done, 1)

                def mu(u):
                    emptied(act, b, ("mu", u))
                    if u >= 2:
                        act.wait_ge(ss_done, b * NT + u - 1)
                    A(sq[u % 2].rearrange("p k (s n) -> p k s n", s=POS), block_rows(u), ACT.Square).then_inc(sq_done, 1)

                def root(half):
                    act.wait_ge(ss_done, b * NT + 4 * half + 4)
                    A(std[half], Sb[half][0:8, 0:256], ACT.Sqrt, bias=eps[0:8, 0:1]).then_inc(root_done, 1)

                def ln():
                    layer_norm(dict(mu=mu, var=nothing, root=root, recip=nothing, norm=nothing))

                def qkv(t_):
                    kind, h = CHUNKS[t_]
                    for w in range(0, NT, 2):
                        o, done = full(act, b, ("qkv", t_, w))
                        ins = A(grid_view(w), o[:, :].rearrange("p (x i j) -> p x i j", x=2, i=NB), ACT.Copy)
                        if kind == "q":
                            if t_ == 4 and w == 0:
                                act.wait_ge(zfill, 16 * (NSLOT // 512))
                            ins = A(qr[h][:, w * TILE:(w + 1) * TILE], o[:, :], ACT.Relu)
                        ins.then_inc(done, 1)

                def tr(t_):
                    for m4 in range(0, NTR, 2):
                        o, done = tfull(act, b, ("tr", t_, m4))
                        o = o[:, :].rearrange("p (j c) -> p j c", j=4)
                        n, rows = len(tiles_of(m4)), tiles_of(m4)[-1][2]
                        if CHUNKS[t_][0] == "k":
                            relu(ktn[0:rows, 4 * m4:4 * m4 + n, :], o[0:rows, 0:n, :], done)
                        else:
                            copy(vt[0:rows, m4 % 2, 0:n, 0:128], o[0:rows, 0:n, :], done)

                def dens(s):
                    o, done = full(act, b, ("den", s))
                    if s >= 2:
                        full(act, b, ("inv", s - 2, 3))
                    A(den[s % 2], o[0:64, :], ACT.Identity, bias=eps[0:64, 2:3]).then_inc(done, 1)

                def attend(s):
                    for c in range(4):
                        if c >= 2:
                            emptied(act, b, ("inv", s, c - 2))
                        elif s:
                            emptied(act, b, ("inv", s - 1, c + 2))
                        o, done = full(act, b, ("num", s, c))
                        A(num[c % 2], o[:, :], ACT.Copy).then_inc(done, 1)

                def proj(s):
                    act.wait_ge(var_done, b * NT + s + 1)
                    A(stat[:, s % 2, :, 8:9], stat[:, s % 2, :, 7:8], ACT.Sqrt, bias=eps[:, 1:2]).then_inc(sd_done, 1)

                def turn(s):
                    for k in range(KC):
                        o, done = tfull(act, b, ("tn", s, k))
                        A(tnt[:, k, :], o[:, :], ACT.Copy).then_inc(done, 1)

                image(dict(ln=ln, qkv=qkv, tr=tr, out=nothing, vka=nothing, den=dens, attend=attend, proj=proj,
                           turn=turn, logit=nothing, recip=nothing, rank=nothing, flush=lambda t_: turned(act, b, t_, 7, 0, copy),
                           conv=lambda t_, half: conv_evacuation(act, b, t_, half, 0, relu, copy)))

        @block.vector
        def _(dve):
            V = nc.vector
            here = [0]

            def link0(ins):
                here[0] += 1
                ins.then_inc(chain0, 1)
                dve.wait_ge(chain0, here[0])

            dve.wait_ge(w_in, 160)
            dve.wait_ge(setup, 8)
            dve.sem_inc(bn_eps, 1)
            dve.wait_ge(bn_sd, 1)
            link0(V.reciprocal(bnr[:, 3, :], bnr[:, 3, :]))
            link0(V.tensor_tensor(bnr[:, 0, :], bnr[:, 0, :], bnr[:, 3, :], ALU.mult))
            link0(V.tensor_tensor(bnr[:, 2, :], bnr[:, 2, :], bnr[:, 0, :], ALU.mult))
            V.tensor_tensor(bias[:, :], bnr[:, 1, :], bnr[:, 2, :], ALU.subtract).then_inc(setup, 1)
            V.tensor_tensor(wp[:, :, :], wp[:, :, :], bnr[:, 0:1, :].to_broadcast([128, 4, CH]), ALU.mult).then_inc(setup, 1)
            V.tensor_copy(carry[:, :], c_["carry0"]).then_inc(setup, 1)
            dve.wait_ge(setup, 11)
            with dve.Fori(0, B) as b:
                here = [0]

                def link(ins):
                    here[0] += 1
                    ins.then_inc(chain, 1)
                    dve.wait_ge(chain, b * LINKS + here[0])

                def relu(dst, src, done):
                    V.tensor_scalar_max(dst, src, 0.0).then_inc(done, 1)

                def copy(dst, src, done):
                    ins = V.tensor_copy(dst, src)
                    if done:
                        ins.then_inc(done, 1)

                def mu(u):
                    s, n = XT[("ln", u)]
                    dve.wait_ge(xt_in[s], (b * XT.per + n) * 16 + 16)
                    o, done = full(dve, b, ("mu", u))
                    for k in range(KC):
                        for i in range(2):
                            src = [a[:, 256 * i:256 * i + 256].rearrange("p (q j x) -> p q x j", q=4, x=4)
                                   for a in (xt[s][:, k, :], o)]
                            dst = xn[:, k, :].rearrange("p (q x i j) -> p q x i j", q=4, x=4, i=NB)
                            ins = V.tensor_tensor(dst[:, :, :, 2 * u + i, :], src[0], src[1], ALU.subtract)
                    ins.then_inc(done, 1)

                def inverse(half):
                    dve.wait_ge(root_done, b * 2 + half + 1)
                    V.reciprocal(std[half], std[half]).then_inc(inv_done, 1)

                def norm(u):
                    o, done = full(dve, b, ("norm", u))
                    V.tensor_tensor(block_rows(u), block_rows(u), o[:, :].rearrange("p (o s n) -> p o s n", o=1, s=POS)
                                    .to_broadcast([128, KC, POS, 2 * NB]), ALU.mult).then_inc(done, 1)

                def ln():
                    layer_norm(dict(mu=mu, var=nothing, root=nothing, recip=inverse, norm=norm))

                def qkv(t_):
                    kind, h = CHUNKS[t_]
                    for w in range(1, NT, 2):
                        o, done = full(dve, b, ("qkv", t_, w))
                        ins = V.tensor_copy(grid_view(w), o[:, :].rearrange("p (x i j) -> p x i j", x=2, i=NB))
                        if kind == "q":
                            if t_ == 4 and w == 1:
                                dve.wait_ge(zfill, 16 * (NSLOT // 512))
                            ins = V.tensor_scalar_max(qr[h][:, w * TILE:(w + 1) * TILE], o[:, :], 0.0)
                        ins.then_inc(done, 1)

                def kv(c):
                    h, conv = c % 2, c // 2
                    dve.wait_ge(k_full, b * 4 + 2 * h + conv + 1)
                    V.tensor_tensor(vk[:, c, :], Kb[:, 0:128], c_["gmask"], ALU.mult)
                    V.tensor_scalar(dn[:, c, 16 * c:16 * c + 16], c_["gm16"], Kb[:, 128:129], None, ALU.mult)\
                        .then_inc(k_out, 1)

                def tr(t_):
                    for m4 in range(1, NTR, 2):
                        o, done = tfull(dve, b, ("tr", t_, m4))
                        o = o[:, :].rearrange("p (j c) -> p j c", j=4)
                        n, rows = len(tiles_of(m4)), tiles_of(m4)[-1][2]
                        if CHUNKS[t_][0] == "k":
                            relu(ktn[0:rows, 4 * m4:4 * m4 + n, :], o[0:rows, 0:n, :], done)
                        else:
                            copy(vt[0:rows, m4 % 2, 0:n, 0:128], o[0:rows, 0:n, :], done)
                    if CHUNKS[t_][0] == "v":
                        kv(CHUNKS[t_][1])
                        V.memset(vta[:, :, :, 128:129], 1.0)

                def recip(s):
                    emptied(dve, b, ("den", s))
                    V.reciprocal(den[s % 2], den[s % 2]).then_inc(rec_done, 1)

                def attend(s):
                    for c in range(4):
                        o, done = full(dve, b, ("inv", s, c))
                        emptied(dve, b, ("num", s, c))
                        for i in range(2):
                            src = [a.rearrange("p (q x i j) -> p q x i j", q=4, x=4, i=2)[:, :, :, i, :]
                                   for a in (num[c % 2], o[:, :])]
                            dst = ao[s % 2][:, c, 256 * i:256 * i + 256].rearrange("p (q j x) -> p q x j", q=4, x=4)
                            ins = V.tensor_tensor(dst, src[0], src[1], ALU.mult)
                        ins.then_inc(done, 1)

                def proj(s):
                    dve.wait_ge(y1_out[s % 2], (b * 4 + s // 2) * 16 + 16)
                    for i in range(2):
                        o, done = full(dve, b, ("proj", s, i))
                        V.tensor_tensor(y1[s % 2][:, 2 * i:2 * i + 2, :], o[:, :].rearrange("p (j d) -> p j d", j=2),
                                        bias[:, :].rearrange("p (o d) -> p o d", o=1).to_broadcast([128, 2, CH]),
                                        ALU.add).then_inc(done, 1)
                    st = stat[:, s % 2, :, :]
                    emptied(dve, b, ("proj", s, 0))
                    emptied(dve, b, ("proj", s, 1))
                    for j in range(4):
                        ins = V.bn_stats(st[:, j, 0:6], y1[s % 2][:, j, :])
                    link(ins)
                    dve.nop(nofuse=True)
                    for j in range(4):
                        ins = V.bn_aggr(st[:, j, 6:8], st[:, j, 0:6])
                    ins.then_inc(var_done, 1)
                    dve.wait_ge(sd_done, b * NT + s + 1)
                    link(V.reciprocal(st[:, :, 14:15], st[:, :, 8:9]))
                    dve.wait_ge(sc_out[s % 4], (b * 2 + s // 4) * 64 + 16)
                    for j in range(4):
                        ins = V.tensor_scalar(tn[s % 4][:, j, :], y1[s % 2][:, j, :], st[:, j, 6:7], st[:, j, 14:15],
                                              ALU.subtract, ALU.mult)
                    ins.then_inc(tn_done, 1)

                def logit(s):
                    o, done = full(dve, b, ("logit", s))
                    st, sm = stat[:, s % 2, :, :], small[:, s % 2, :, :]
                    oh, lg, cand = sm[:, :, 0:8], sm[:, :, 8:16], sm[:, :, 16:24]
                    d = dlog[:, bass.ds(b * 32 + 4 * s, 4), :]
                    over4 = lambda a: a.rearrange("p (o e) -> p o e", o=1).to_broadcast([128, 4, NE])
                    V.tensor_tensor(lg, o[:, 0:32].rearrange("p (j e) -> p j e", j=4), over4(gate_b[:, :]),
                                    ALU.add).then_inc(done, 1)
                    emptied(dve, b, ("logit", s))
                    link(V.tensor_reduce(st[:, :, 9:10], lg, AX.X, ALU.max))
                    link(V.tensor_tensor(d, lg, st[:, :, 9:10].to_broadcast([128, 4, NE]), ALU.subtract))
                    link(V.tensor_scalar(cand, d, 0.0, None, ALU.is_ge))
                    link(V.tensor_tensor(cand, cand, over4(c_["rev"]), ALU.mult))
                    link(V.tensor_reduce(st[:, :, 10:11], cand, AX.X, ALU.max))
                    V.tensor_tensor(oh, over4(c_["rev"]), st[:, :, 10:11].to_broadcast([128, 4, NE]),
                                    ALU.is_equal).then_inc(oh_done, 1)

                def rank(s):
                    o, done = full(dve, b, ("rank", s))
                    dve.wait_ge(oh_done, b * NT + s + 1)
                    st, sm = stat[:, s % 2, :, :], small[:, s % 2, :, :]
                    oh, pos = sm[:, :, 0:8], sm[:, :, 16:24]
                    at = bass.ds(b * 32 + 4 * s, 4)
                    dve.wait_ge(carried, b * NT + s + 1)
                    link(V.tensor_tensor(pos, o[:, 0:32].rearrange("p (j e) -> p j e", j=4),
                                         carry[:, :].rearrange("p (o e) -> p o e", o=1).to_broadcast([128, 4, NE]), ALU.add))
                    V.tensor_tensor(carry[:, :], carry[:, :], o[:, 32:32 + NE], ALU.add).then_inc(carried, 1)
                    link(V.tensor_tensor(pos, pos, oh, ALU.mult))
                    link(V.tensor_reduce(st[:, :, 11:12], pos, AX.X, ALU.add))
                    link(V.tensor_scalar(st[:, :, 12:13], st[:, :, 10:11], float(-CAP), float(NE * CAP + CAP - 1),
                                         ALU.mult, ALU.add))
                    dve.wait_ge(carried, b * NT + s + 2)
                    dve.sem_inc(done, 1)
                    kp = kept[:, at].rearrange("p (j o) -> p j o", o=1)
                    link(V.tensor_tensor(kp, st[:, :, 11:12], st[:, :, 12:13], ALU.is_le))
                    V.tensor_tensor(gidx[:, at].rearrange("p (j o) -> p j o", o=1), st[:, :, 11:12], st[:, :, 12:13], ALU.min)
                    link(V.tensor_scalar(st[:, :, 13:14], kp, -float(NSLOT), float(NSLOT), ALU.mult, ALU.add))
                    V.tensor_tensor(sidx[:, s % 4, :].rearrange("p (j o) -> p j o", o=1), st[:, :, 11:12], st[:, :, 13:14],
                                    ALU.add).then_inc(sidx_done, 1)

                image(dict(ln=ln, qkv=qkv, tr=tr, out=nothing, vka=lambda h: kv(2 + h), den=nothing, recip=recip,
                           attend=attend, proj=proj, turn=nothing, logit=logit, rank=rank, flush=lambda t_: turned(dve, b, t_, 7, 1, copy),
                           conv=lambda t_, half: conv_evacuation(dve, b, t_, half, 1, relu, copy)))
                assert here[0] == LINKS, here[0]


def experts(nc, D):
    f32, f32r = mybir.dt.float32, mybir.dt.float32r
    ALU, ACT = mybir.AluOpType, mybir.ActivationFunctionType
    PER = 2 * NSB
    HALVES = ((0, 0), (0, 1), (1, 0))
    SECOND_LOAD = 4
    with ExitStack() as ctx:
        def sb(name, shape, dt=f32):
            return ctx.enter_context(nc.sbuf_tensor(name, shape, dt))

        def sem(name):
            return ctx.enter_context(nc.semaphore(name))

        w1s = sb("w1s", [128, KC, FF])
        w2s = sb("w2s", [128, FT, CH])
        w1 = [[sb(f"w1_{i}{h}", [128, KC, FF], f32r) for h in range(2)] for i in range(2)]
        w2 = [[sb(f"w2_{i}{h}", [128, FT, CH], f32r) for h in range(2)] for i in range(2)]
        b1 = [sb(f"b1_{i}", [128, FT]) for i in range(2)]
        b2 = [sb(f"b2_{i}", [128, CH]) for i in range(2)]
        rows = [sb(f"rows{i}", [128, 4, CH]) for i in range(2)]
        rowt = [[sb(f"rowt{i}{h}", [128, KC, TILE], f32r) for h in range(2)] for i in range(2)]
        act_out = sb("act_out", [128, 4, TILE])
        hid = [[sb(f"hid{i}{h}", [128, FT, TILE], f32r) for h in range(2)] for i in range(2)]
        yr = [sb(f"yr{i}", [128, 4, CH]) for i in range(2)]
        ident = sb("ident2", [128, 128])
        prime = sb("prime2", [128, 2, NE])
        Rb = [ctx.enter_context(nc.psum_tensor(f"R{i}", [128, 512], f32)) for i in range(2)]
        Hb = [ctx.enter_context(nc.psum_tensor(f"H{i}", [128, 512], f32)) for i in range(4)]
        Yb = [ctx.enter_context(nc.psum_tensor(f"Y{i}", [128, 512], f32)) for i in range(2)]
        id_in = sem("id_in")
        w_in = [sem(f"ew_in{i}") for i in range(2)]
        w_split = sem("w_split")
        w_hi = sem("w_hi")
        rows_in = [sem(f"rows_in{i}") for i in range(2)]
        r_full = [sem(f"r_full{i}") for i in range(2)]
        r_hi = sem("r_hi")
        r_out = [sem(f"r_out{i}") for i in range(2)]
        h_full = [sem(f"h_full{i}") for i in range(4)]
        h_out = [sem(f"h_out{i}") for i in range(4)]
        h_split = sem("h_split")
        y_full = [sem(f"y_full{i}") for i in range(2)]
        y_out = [sem(f"y_out{i}") for i in range(2)]
        stored = [sem(f"stored{i}") for i in range(2)]
        block = ctx.enter_context(nc.Block())

        def slots(ap, n):
            return ap[bass.ds(n * TILE, TILE), :].rearrange("(p j) d -> p j d", j=4)

        @block.sync
        def _(sp):
            sp.dma_start(ident[:, :], D["con"][:, CON["ident"][0]:CON["ident"][1]]).then_inc(id_in, 16)
            with sp.Fori(0, NE // 2) as ep:
                def weights(par):
                    e = bass.ds(ep * 2 + par, 1)
                    hold(sp, y_full[1], ep * PER + 1 + NSB * par)
                    hold(sp, w_split, ep * 4 + 2 * par + 1)
                    sp.dma_start(w1s[:, :, :], D["w1"][e, :, :].rearrange("o (k p) f -> p (o k) f", p=128)).then_inc(w_in[0], 16)
                    sp.dma_start(b1[par][:, :], D["b1"][e, :, :].rearrange("o p f -> p (o f)")).then_inc(w_in[0], 16)
                    sp.dma_start(w2s[:, :, :], D["w2"][e, :, :].rearrange("o (k p) d -> p (o k) d", p=128)).then_inc(w_in[1], 16)
                    sp.dma_start(b2[par][:, :], D["b2"][e, :].to_broadcast([128, CH])).then_inc(w_in[1], 16)

                for m in range(PER):
                    if m == 0:
                        weights(0)
                    if m == SECOND_LOAD:
                        weights(1)
                    hold(sp, r_full[1], ep * PER + m + 1)
                    sp.dma_start(rows[m % 2][:, :, :], slots(D["slots"], ep * PER + m)).then_inc(rows_in[m % 2], 16)

        @block.gpsimd
        def _(pool):
            for first in [*r_out, *h_out, *y_out, w_split]:
                pool.sem_inc(first, 1)
            pool.sem_inc(h_split, 4)
            pool.sem_inc(r_full[1], 2)
            pool.sem_inc(y_full[1], NSB + 1)
            for i in range(2):
                pool.dma_start(prime[:, i, :], D["gate_b"].to_broadcast([128, NE])).then_inc(stored[i], 16)
            with pool.Fori(0, NE // 2) as ep:
                for m in range(PER):
                    for i in range(2):
                        hold(pool, y_out[i], ep * PER + m + 2)
                    pool.dma_start(slots(D["ybuf"], ep * PER + m), yr[m % 2][:, :, :]).then_inc(stored[m % 2], 16)
            for i in range(2):
                hold(pool, stored[i], 16 * NE * NSB // 2 + 16)

        @block.tensor
        def _(pe):
            mm = nc.tensor.matmul
            pe.wait_ge(id_in, 16)
            with pe.Fori(0, NE // 2) as ep:
                def turn(m):
                    pe.wait_ge(rows_in[m % 2], (ep * NSB + m // 2 + 1) * 16)
                    for k in range(KC):
                        pe.wait_ge(r_out[k], ep * PER + m + 1)
                        for j in range(4):
                            last = nc.tensor.transpose(Rb[k][:, 128 * j:128 * j + 128], rows[m % 2][:, j, 128 * k:128 * k + 128],
                                                       ident[:, :])
                        last.then_inc(r_full[k], 1)

                def first(m):
                    par, s = m // NSB, m % 2
                    if m % NSB == 0:
                        pe.wait_ge(w_split, ep * 4 + 2 * par + 2)
                    for k in range(KC):
                        pe.wait_ge(r_out[k], ep * PER + m + 2)
                    for f in range(FT):
                        pe.wait_ge(h_out[f % 4], 2 * (ep * PER + m) + f // 4 + 1)
                        for k in range(KC):
                            for hw, hx in HALVES:
                                last = mm(Hb[f % 4][:, :], w1[par][hw][:, k, 128 * f:128 * f + 128], rowt[s][hx][:, k, :],
                                          start=k + hw + hx == 0, stop=k + hw == 2)
                        last.then_inc(h_full[f % 4], 1)

                def second(m):
                    par, s = m // NSB, m % 2
                    if m % NSB == 0:
                        pe.wait_ge(w_split, ep * 4 + 2 * par + 3)
                    pe.wait_ge(h_split, (ep * PER + m) * FT + FT + 4)
                    for i in range(2):
                        pe.wait_ge(y_out[i], ep * PER + m + 1)
                        for j in range(2 * i, 2 * i + 2):
                            for f in range(FT):
                                for hh, hw in HALVES:
                                    last = mm(Yb[i][:, 256 * (j % 2):256 * (j % 2) + 256],
                                              hid[s][hh][:, f, 128 * j:128 * j + 128], w2[par][hw][:, f, :],
                                              start=f + hh + hw == 0, stop=f + hh == FT)
                        last.then_inc(y_full[i], 1)

                turn(0)
                for m in range(PER):
                    first(m)
                    if m + 1 < PER:
                        turn(m + 1)
                    if m:
                        second(m - 1)
                second(PER - 1)

        @block.scalar
        def _(act):
            A = nc.scalar.activation
            with act.Fori(0, NE // 2) as ep:
                def turn(m):
                    for k in range(KC):
                        act.wait_ge(r_full[k], ep * PER + m + 1 + 2 * k)
                        A(rowt[m % 2][0][:, k, :], Rb[k][:, :], ACT.Copy).then_inc(r_hi, 1)

                turn(0)
                for m in range(PER):
                    par = m // NSB
                    for f in range(FT):
                        act.wait_ge(h_full[f % 4], 2 * (ep * PER + m) + f // 4 + 1)
                        act.wait_ge(h_split, (ep * PER + m) * FT + f + 1)
                        A(act_out[:, f % 4, :], Hb[f % 4][:, :], ACT.Relu, bias=b1[par][:, f:f + 1])
                        A(hid[m % 2][0][:, f, :], Hb[f % 4][:, :], ACT.Relu, bias=b1[par][:, f:f + 1]).then_inc(h_out[f % 4], 1)
                    if m + 1 < PER:
                        turn(m + 1)

        @block.vector
        def _(dve):
            V = nc.vector
            with dve.Fori(0, NE // 2) as ep:
                def split(par, layer):
                    src, dst = ((w1s, w1[par]), (w2s, w2[par]))[layer]
                    dve.wait_ge(w_in[layer], (ep * 4 + 2 * par + 2) * 16)
                    V.tensor_copy(dst[0][:, :, :], src[:, :, :]).then_inc(w_hi, 1)
                    dve.wait_ge(w_hi, ep * 4 + 2 * par + layer + 1)
                    V.tensor_tensor(dst[1][:, :, :], src[:, :, :], dst[0][:, :, :], ALU.subtract).then_inc(w_split, 1)

                def turn(m):
                    for k in range(KC):
                        dve.wait_ge(r_hi, (ep * PER + m) * KC + k + 1)
                        V.tensor_tensor(rowt[m % 2][1][:, k, :], Rb[k][:, :], rowt[m % 2][0][:, k, :], ALU.subtract)\
                            .then_inc(r_out[k], 1)

                def biased(m):
                    par, s = m // NSB, m % 2
                    dve.wait_ge(stored[s], (ep * NSB + m // 2) * 16 + 16)
                    for i in range(2):
                        dve.wait_ge(y_full[i], ep * PER + m + 1 + (NSB + 1) * i)
                        V.tensor_tensor(yr[s][:, 2 * i:2 * i + 2, :], Yb[i][:, :].rearrange("p (j d) -> p j d", j=2),
                                        b2[par][:, :].rearrange("p (o d) -> p o d", o=1).to_broadcast([128, 2, CH]),
                                        ALU.add).then_inc(y_out[i], 1)

                split(0, 0)
                turn(0)
                split(0, 1)
                for m in range(PER):
                    for f in range(FT):
                        dve.wait_ge(h_out[f % 4], 2 * (ep * PER + m) + f // 4 + 2)
                        V.tensor_tensor(hid[m % 2][1][:, f, :], act_out[:, f % 4, :], hid[m % 2][0][:, f, :], ALU.subtract)\
                            .then_inc(h_split, 1)
                    if m + 1 < PER:
                        turn(m + 1)
                    if m == SECOND_LOAD + 1:
                        split(1, 0)
                        split(1, 1)
                    if m:
                        biased(m - 1)
                biased(PER - 1)


def combine(nc, keep, D, out):
    f32, u32 = mybir.dt.float32, mybir.dt.uint32
    ALU, ACT, AX = mybir.AluOpType, mybir.ActivationFunctionType, mybir.AxisListType
    dlog, kept, gidx = keep
    with ExitStack() as ctx:
        def sb(name, shape, dt=f32):
            return ctx.enter_context(nc.sbuf_tensor(name, shape, dt))

        def sem(name):
            return ctx.enter_context(nc.semaphore(name))

        NS = 4
        yg = [sb(f"yg{i}", [128, 4, CH]) for i in range(NS)]
        yl = [sb(f"yl{i}", [128, 4, CH]) for i in range(NS)]
        v = [sb(f"v{i}", [128, 4, CH]) for i in range(2)]
        mag = [sb(f"mag{i}", [128, 4, CH]) for i in range(2)]
        lim = [sb(f"lim{i}", [128, 4, CH]) for i in range(2)]
        clip = [sb(f"clip{i}", [128, 4, CH]) for i in range(2)]
        zt = [sb(f"zt{i}", [128, KC, TILE]) for i in range(2)]
        pick = sb("pick", [128, NS, 4], u32)
        wsel = sb("wsel", [128, NS, 4])
        wgt = sb("wgt", [128, TOKENS // 128])
        ident = sb("ident3", [128, 128])
        prime = sb("prime3", [128, 2, NE])
        Pb = [ctx.enter_context(nc.psum_tensor(f"P{i}", [128, 512], f32)) for i in range(4)]
        id_in = sem("id_in3")
        exp_done, chain3, w_done = sem("exp_done"), sem("chain3"), sem("w_done")
        yl_in = [sem(f"yl_in{i}") for i in range(NS)]
        yg_in = [sem(f"yg_in{i}") for i in range(NS)]
        picked = sem("picked")
        v_done, mag_done, z_done = sem("v_done"), sem("mag_done"), sem("z_done")
        p_full = [sem(f"p_full{i}") for i in range(4)]
        p_out = [sem(f"p_out{i}") for i in range(4)]
        o_out = [sem(f"o_out{i}") for i in range(2)]
        block = ctx.enter_context(nc.Block())

        @block.sync
        def _(sp):
            sp.dma_start(ident[:, :], D["con"][:, CON["ident"][0]:CON["ident"][1]]).then_inc(id_in, 16)
            for i in range(2):
                sp.dma_start(prime[:, i, :], D["gate_b"].to_broadcast([128, NE])).then_inc(o_out[i], 16)
            with sp.Fori(0, B) as b:
                def load(u):
                    hold(sp, z_done, b * NT + u + 1)
                    sp.dma_start(yl[u % NS][:, :, :], D["y1"][bass.ds(b * NTOK + u * TILE, TILE), :]
                                 .rearrange("(j p) d -> p j d", p=128)).then_inc(yl_in[u % NS], 16)

                for u in range(NS - 1):
                    load(u)
                for u in range(NT):
                    if u + NS - 1 < NT:
                        load(u + NS - 1)
                    for k in range(KC):
                        hold(sp, p_out[2 * (u % 2) + k], b * 4 + u // 2 + 2)
                    sp.dma_start(out[bass.ds(b, 1), :, u * TILE:(u + 1) * TILE].rearrange("o (k p) n -> p (o k) n", p=128),
                                 zt[u % 2][:, :, :]).then_inc(o_out[u % 2], 16)
            for i in range(2):
                hold(sp, o_out[i], 16 * QUADS // 2 + 16)

        @block.gpsimd
        def _(pool):
            for first in [*p_out, *p_full]:
                pool.sem_inc(first, 1)
            for first in (z_done, v_done):
                pool.sem_inc(first, NS)
            with pool.Fori(0, B) as b:
                for u in range(NT):
                    s = u % NS
                    hold(pool, v_done, b * NT + u + 1)
                    nc.gpsimd.tensor_copy(pick[:, s, :], gidx[:, bass.ds(b * 32 + 4 * u, 4)]).then_inc(picked, 1)
                    hold(pool, picked, b * NT + u + 1)
                    for j in range(4):
                        nc.gpsimd.indirect_dma_start(
                            out=yg[s][:, j, :], out_offset=None, in_=D["ybuf"],
                            in_offset=bass.IndirectOffsetOnAxis(ap=pick[:, s, j:j + 1], axis=0),
                            bounds_check=NSLOT - 1, oob_is_err=False).then_inc(yg_in[s], 16)

        @block.tensor
        def _(pe):
            pe.wait_ge(id_in, 16)
            with pe.Fori(0, B) as b:
                for u in range(NT):
                    pe.wait_ge(z_done, b * NT + u + 1 + NS)
                    for k in range(KC):
                        i = 2 * (u % 2) + k
                        pe.wait_ge(p_out[i], b * 4 + u // 2 + 1)
                        for j in range(4):
                            last = nc.tensor.transpose(Pb[i][:, 128 * j:128 * j + 128], v[u % 2][:, j, 128 * k:128 * k + 128],
                                                       ident[:, :])
                        last.then_inc(p_full[i], 1)

        @block.scalar
        def _(act):
            A = nc.scalar.activation
            A(dlog[:, :, :], dlog[:, :, :], ACT.Exp).then_inc(exp_done, 1)
            act.wait_ge(w_done, 1)
            with act.Fori(0, B) as b:
                for u in range(NT + 1):
                    if u < NT:
                        s = u % NS
                        act.wait_ge(yg_in[s], (b * 2 + u // NS + 1) * 64)
                        act.wait_ge(p_full[2 * (u % 2) + 1], b * 4 + u // 2 + 1)
                        for j in range(4):
                            ins = A(v[u % 2][:, j, :], yg[s][:, j, :], ACT.Copy, scale=wgt[:, bass.ds(b * 32 + 4 * u + j, 1)])
                        ins.then_inc(v_done, 1)
                        act.wait_ge(v_done, b * NT + u + 1 + NS)
                        A(mag[u % 2][:, :, :], v[u % 2][:, :, :], ACT.Abs).then_inc(mag_done, 1)
                    if u:
                        w = u - 1
                        i = 2 * (w % 2)
                        act.wait_ge(p_full[i], b * 4 + w // 2 + 2)
                        act.wait_ge(o_out[w % 2], (b * 4 + w // 2) * 16 + 16)
                        A(zt[w % 2][:, 0, :], Pb[i][:, :], ACT.Copy).then_inc(p_out[i], 1)

        @block.vector
        def _(dve):
            V = nc.vector
            dve.wait_ge(exp_done, 1)
            V.tensor_reduce(wgt[:, :].rearrange("p (n o) -> p n o", o=1), dlog[:, :, :], AX.X, ALU.add).then_inc(chain3, 1)
            dve.wait_ge(chain3, 1)
            V.reciprocal(wgt[:, :], wgt[:, :]).then_inc(chain3, 1)
            dve.wait_ge(chain3, 2)
            V.tensor_tensor(wgt[:, :], wgt[:, :], kept[:, :], ALU.mult).then_inc(w_done, 1)
            with dve.Fori(0, B) as b:
                here = [2]

                def link(ins):
                    here[0] += 1
                    ins.then_inc(chain3, 1)
                    dve.wait_ge(chain3, b * LINKS3 + here[0])

                for u in range(NT + 1):
                    if u < NT:
                        s = u % 2
                        flat = lambda a: a[:, :, :].rearrange("p j d -> p (j d)")
                        vv, mm_, ll, cc, yy = flat(v[s]), flat(mag[s]), flat(lim[s]), flat(clip[s]), flat(yl[u % NS])
                        dve.wait_ge(mag_done, b * NT + u + 1)
                        V.tensor_scalar(ll, vv, FMAX, -FMAX, ALU.min, ALU.max)
                        link(V.tensor_scalar(cc, vv, 1e4, -1e4, ALU.min, ALU.max))
                        V.scalar_tensor_tensor(ll, mm_, FMAX, ll, ALU.is_le, ALU.mult)
                        link(V.scalar_tensor_tensor(cc, mm_, FMAX, cc, ALU.is_gt, ALU.mult))
                        dve.wait_ge(yl_in[u % NS], (b * 2 + u // NS + 1) * 16)
                        link(V.tensor_tensor(ll, ll, cc, ALU.add))
                        V.tensor_tensor(vv, ll, yy, ALU.add).then_inc(z_done, 1)
                    if u:
                        w = u - 1
                        i = 2 * (w % 2) + 1
                        dve.wait_ge(p_full[i], b * 4 + w // 2 + 2)
                        dve.wait_ge(o_out[w % 2], (b * 4 + w // 2) * 16 + 16)
                        V.tensor_copy(zt[w % 2][:, 1, :], Pb[i][:, :]).then_inc(p_out[i], 1)
                assert here[0] == 2 + LINKS3, here[0]


LINKS = NT * 13
LINKS3 = NT * 3


def metaformer(nc, D, out):
    f32, u32 = mybir.dt.float32, mybir.dt.uint32
    D["slots"] = nc.dram_tensor("slots", (NSLOT, CH), f32, kind="Internal").ap()
    D["ybuf"] = nc.dram_tensor("ybuf", (NSLOT, CH), f32, kind="Internal").ap()
    D["y1"] = nc.dram_tensor("y1", (TOKENS, CH), f32, kind="Internal").ap()
    with ExitStack() as ctx:
        keep = (ctx.enter_context(nc.sbuf_tensor("dlog", [128, TOKENS // 128, NE], f32)),
                ctx.enter_context(nc.sbuf_tensor("kept", [128, TOKENS // 128], f32)),
                ctx.enter_context(nc.sbuf_tensor("gidx", [128, TOKENS // 128], u32)))
        mixer_and_dispatch(nc, keep, D)
        experts(nc, D)
        combine(nc, keep, D, out)


def constants():
    import numpy as np
    con = np.zeros((128, NCON), np.float32)
    p = np.arange(128)
    con[:, slice(*CON["ident"])] = np.eye(128)
    con[:, slice(*CON["gmask"])] = p[:, None] // 8 == p[None, :] // 8
    con[:, slice(*CON["tri"])] = p[:, None] <= p[None, :]
    con[:, slice(*CON["gm16"])] = p[:, None] // 8 == np.arange(16)[None, :]
    a = CON["spread"][0]
    for c in range(4):
        con[16 * c + p // 8, a + 128 * c + p] = 1.0
    con[:, slice(*CON["carry0"])] = np.arange(NE)[None, :] * CAP - 1
    con[:, CON["row7"][0] + 7] = 1.0 / CH
    con[:, slice(*CON["rev"])] = NE - np.arange(NE)[None, :]
    return con


def lay_out(x, w_qkv, w_dw, w_pw, w_proj, gate_w, b1):
    import numpy as np
    ch = np.array([[24 * (16 * h + g) + 8 * "qkv".index(kind) + c for g in range(NG) for c in range(8)] for kind, h in CHUNKS])
    wq = np.asarray(w_qkv).reshape(768, CH)[ch]
    wq = wq.transpose(2, 0, 1).reshape(KC, 128, NCHUNK, 128).transpose(1, 0, 2, 3)
    wp = np.asarray(w_proj).reshape(CH, 512).T.reshape(4, 128, CH).transpose(1, 0, 2)
    pad = np.zeros((768, 11, 11), np.float32)
    pad[:, 3:8, 3:8] = np.asarray(w_dw).reshape(768, 5, 5)
    py, qa, qq = np.arange(4), np.arange(2), np.arange(4)
    idx = 4 * qa[None, :, None] + py[:, None, None] - qq[None, None, :] + 3
    dw = pad[ch][:, :, idx][:, :, :, :, :, idx]
    dw = dw.reshape(NCHUNK, NG, 8, 4, 2, 4, 4, 2, 4).transpose(0, 2, 3, 6, 1, 4, 7, 5, 8)
    dw = dw.reshape(NCHUNK, 128, NG, 64)
    pw = np.asarray(w_pw).reshape(768, 8)[ch].reshape(NCHUNK, NG, 8, 8)
    pw = np.broadcast_to(pw.transpose(3, 0, 1, 2)[:, None], (8, POS, NCHUNK, NG, 8)).reshape(128, NCHUNK, NG, 8)
    gw = np.asarray(gate_w).reshape(KC, 128, NE).transpose(1, 0, 2)
    return dict(x=np.asarray(x).reshape(B, CH, NTOK), wq=wq, wp=wp, dw=dw, pw=pw, gate_w=gw,
                b1=np.asarray(b1).reshape(NE, FT, 128).transpose(0, 2, 1))


def kernel(**inputs):
    import numpy as np
    import concourse.bacc as bacc
    from concourse.bass_utils import run_bass_kernel_spmd

    i = inputs
    arrays = lay_out(i["x"], i["L0_conv_w_qkv"], i["L0_conv_w_dw"], i["L0_conv_w_pw"], i["L0_conv_w_proj"],
                     i["L0_ffn_gate_w"], i["L0_ffn_b1"])
    for name in ("bn_gamma", "bn_beta", "bn_mean", "bn_var"):
        arrays[name] = np.asarray(i["L0_conv_" + name]).reshape(1, CH)
    arrays["gate_b"] = np.asarray(i["L0_ffn_gate_b"]).reshape(1, NE)
    arrays["w1"], arrays["w2"], arrays["b2"] = (np.asarray(i["L0_ffn_" + n]) for n in ("w1", "w2", "b2"))
    arrays["con"] = constants()
    arrays = {"in_" + k: np.ascontiguousarray(v) for k, v in arrays.items()}

    nc = bacc.Bacc("TRN2", target_bir_lowering=False, num_devices=1)
    D = {k[3:]: nc.dram_tensor(k, v.shape, mybir.dt.from_np(v.dtype), kind="ExternalInput").ap() for k, v in arrays.items()}
    out = nc.dram_tensor("out", (B, CH, NTOK), mybir.dt.float32, kind="ExternalOutput").ap()
    metaformer(nc, D, out)
    r = run_bass_kernel_spmd(nc, [arrays], core_ids=[0])
    return np.asarray(r.results[0]["out"]).reshape(B, CH, HW, HW)
```

```python
import concourse.bass as bass
from concourse import mybir
from contextlib import ExitStack

B, CH, HW = 8, 256, 64
NTOK = HW * HW
KC = CH // 128
TILE = 512
NT = NTOK // TILE
BLK = 4
POS = BLK * BLK
NB = HW // BLK
GRID = NB + 1
GG = GRID * GRID
NGRID = POS * GG
NTRT = -(-NGRID // 128)
NTR = -(-NTRT // 4)
NCHUNK = 6
NG = 16
CHUNKS = [("k", 0), ("v", 0), ("k", 1), ("v", 1), ("q", 0), ("q", 1)]
FIRST_Q = 4
NPAIR = NG // 2
AHEAD = 3
HALVES = ((0, 0), (0, 1), (1, 0))
NE, CAP, FF = 8, 5120, 1024
FT = FF // 128
NSLOT = NE * CAP
TOKENS = B * NTOK
QUADS = TOKENS // TILE
NFILL = NSLOT // 512
NSB = CAP // TILE
FMAX = 3.4028234663852886e38

CON = {}
_at = 0
for _name, _n in (("ident", 128), ("gmask", 128), ("gm16", 16), ("carry0", NE), ("rev", NE), ("row7", 15)):
    CON[_name] = (_at, _at + _n)
    _at += _n
NCON = _at


class Ring:

    def __init__(self, size, keys):
        self.size, self.at = size, {k: (n % size, n // size) for n, k in enumerate(keys)}
        assert len(keys) % size == 0
        self.per = len(keys) // size

    def __getitem__(self, key):
        return self.at[key]


def nothing(*_):
    pass


def hold(eng, sem, value):
    eng.wait_ge(sem, value)
    eng.nop(nofuse=True)


def layer_norm(ph):
    for u in range(NT + 1):
        if u < NT:
            ph["mu"](u)
        if u == 5:
            ph["recip"](0)
        if u:
            ph["var"](u - 1)
        if u == 4:
            ph["root"](0)
        if u in (6, 7):
            for v in range(2):
                ph["norm"](2 * (u - 6) + v)
    ph["root"](1)
    ph["recip"](1)
    for u in range(4, NT):
        ph["norm"](u)


def image(ph):
    ph["ln"]()
    ph["qkv"](0)
    ph["tr"](0)
    ph["prep"](0)
    for t in range(NCHUNK):
        ph["conv"](t, 0)
        if t + 1 < NCHUNK and t + 1 != FIRST_Q:
            ph["qkv"](t + 1)
        ph["conv"](t, 1)
        if CHUNKS[t][0] == "k":
            ph["tr"](t + 1)
            ph["flush"](t)
        if CHUNKS[t][0] == "v":
            ph["flush"](t)
            if t + 1 == FIRST_Q:
                ph["qkv"](t + 1)
            ph["vka"](CHUNKS[t][1])
            if t + 1 == FIRST_Q:
                ph["prep"](t + 1)
            else:
                ph["tr"](t + 1)
    ph["out"]()
    ph["den"](0)
    ph["recip"](0)
    for s in range(NT - 1):
        ph["den"](s + 1)
        if s >= 3:
            ph["rank"](s - 3)
        if s >= 2:
            ph["turn"](s - 2)
        ph["attend"](s)
        if s >= 2:
            ph["logit"](s - 2)
        ph["recip"](s + 1)
        if s >= 1:
            ph["proj"](s - 1)
    for step, s in (("rank", NT - 4), ("attend", NT - 1), ("turn", NT - 3), ("proj", NT - 2), ("logit", NT - 3),
                    ("proj", NT - 1), ("rank", NT - 3), ("turn", NT - 2), ("logit", NT - 2), ("turn", NT - 1),
                    ("logit", NT - 1), ("rank", NT - 2), ("rank", NT - 1)):
        ph[step](s)


def psum_rings():
    main, turn = [], []
    layer_norm(dict(mu=lambda u: main.append(("mu", u)), norm=lambda u: main.append(("norm", u)),
                    var=nothing, root=nothing, recip=nothing))
    image(dict(ln=nothing, recip=nothing, prep=nothing, out=nothing, vka=nothing,
               qkv=lambda t: main.extend(("qkv", t, w) for w in range(NT)),
               tr=lambda t: turn.extend(("tr", t, m) for m in range(NTR)),
               conv=lambda t, half: turn.extend(("ct", t, p - 1) for p in range(4 * half, 4 * half + 4)
                                                if p and CHUNKS[t][0] != "q"),
               flush=lambda t: turn.append(("ct", t, 7)),
               den=nothing,
               attend=lambda s: main.extend((k, s, c) for c in range(4) for k in ("num", "inv")),
               proj=lambda s: main.extend(("proj", s, i) for i in range(2)),
               turn=lambda s: turn.extend(("tn", s, k) for k in range(2)),
               logit=nothing, rank=lambda s: turn.append(("rank", s))))
    return Ring(3, main), Ring(2, turn)


def mixer_and_dispatch(nc, keep, D):
    f32, f32r, u32 = mybir.dt.float32, mybir.dt.float32r, mybir.dt.uint32
    ALU, ACT, AX = mybir.AluOpType, mybir.ActivationFunctionType, mybir.AxisListType
    G, T = psum_rings()
    with ExitStack() as ctx:
        def sb(name, shape, dt=f32):
            return ctx.enter_context(nc.sbuf_tensor(name, shape, dt))

        def under(*specs):
            with ExitStack() as shared:
                return [shared.enter_context(nc.sbuf_tensor(*spec)) for spec in specs]

        def sem(name):
            return ctx.enter_context(nc.semaphore(name))

        xt = [sb(f"xt{i}", [128, KC, TILE]) for i in range(2)]
        xn = sb("xn", [128, KC, NTOK])
        grid = sb("grid", [128, BLK, BLK, GRID, GRID])
        [conv_in] = under(("conv_in", [128, NG, GRID, GRID], f32r))
        late = sb("late", [128, NG * GG])
        [toep_lo] = under(("toep_lo", [128, 2, 2, 4, 128], f32r))
        toep = sb("toep", [128, 2, 2, 4, 128])
        dwt = sb("dwt", [128, 2, NG, 64])
        pwt = sb("pwt", [128, NCHUNK, NG, 8])
        [conv_hi_b] = under(("conv_hi_b", [128, NG, GRID, GRID], f32r))
        kt = sb("kt", [128, NTRT * 128])
        toep_hi_b, toep_lo_b = under(("toep_hi_b", [128, 2, 2, 4, 128], f32r), ("toep_lo_b", [128, 2, 4, 128], f32r))
        kta = sb("kta", [128, 2, POS, 128])
        vt = sb("vt", [128, 2, 4, 129])
        [rec] = under(("rec", [128, 2, TILE], f32r))
        qe = sb("qe", [128, 4, 256])
        conv_hi_a, toep_hi_a, toep_lo_a = under(("conv_hi_a", [128, NG, GRID, GRID], f32r),
                                                ("toep_hi_a", [128, 2, 2, 4, 128], f32r), ("toep_lo_a", [128, 2, 4, 128], f32r))
        q0 = sb("q0", [128, 2, NTOK])
        wq = sb("wq", [128, KC, NCHUNK, 128])
        wp = sb("wp", [128, 4, CH])
        vk = sb("vk", [128, 4, 128])
        dn = sb("dn", [128, 4, 64])
        zeros_and_ones = sb("zeros_and_ones", [128, 6, 128], f32r)
        chosen = sb("chosen", [128, 2, 5, NE], f32r)
        mean_w = sb("mean_w", [128, 128])
        eps = sb("eps", [128, 3])
        bias = sb("bias", [128, CH])
        bnr = sb("bnr", [128, 4, CH])
        gate = sb("gate", [128, KC, NE])
        gate_b = sb("gate_b", [128, NE])
        carry = sb("carry", [128, NE])
        small = sb("small", [128, 2, 4, 24])
        stat = sb("stat", [128, 2, 4, 16])
        sidx = sb("sidx", [128, 4, 4], u32)
        con = sb("con", [128, NCON])
        dlog, kept, gidx = keep
        c_ = {k: con[:, a:b] for k, (a, b) in CON.items()}
        ident = c_["ident"]
        spread = zeros_and_ones[:, 0:4, :]
        tri, ones = zeros_and_ones[:, 4, :], zeros_and_ones[:, 5, :]
        ktn = kt[:, :].rearrange("p (m c) -> p m c", m=NTRT)
        vta = kt[:, 0:32 * 129].rearrange("p (h s c) -> p h s c", h=2, s=POS)
        ktf = kta[:, :, :, :].rearrange("p h s c -> p (h s c)")
        std = [kt[0:8, i * 256:(i + 1) * 256] for i in range(2)]
        den = [kt[0:64, i * 512:(i + 1) * 512] for i in range(2)]
        tnt = kt[:, 1024:2048].rearrange("p (k n) -> p k n", k=KC)
        conv_hi, toep_hi = [conv_hi_a, conv_hi_b], [toep_hi_a, toep_hi_b]
        toep_third = [a[:, at:at + 1024].rearrange("p (g q m) -> p g q m", g=2, q=4)
                      for a, at in ((q0[:, :, :].rearrange("p h n -> p (h n)"), NG * GG + 2048), (ktf, 2048))]
        cif = late[:, :]
        y1 = [cif[:, i * 1024:(i + 1) * 1024].rearrange("p (j d) -> p j d", j=4) for i in range(2)]
        ao = [a.rearrange("p (c n) -> p c n", c=4) for a in (cif[:, 2048:4096], kt[:, 2048:4096])]
        sq = [cif[:, 2048 + i * 1024:3072 + i * 1024].rearrange("p (k n) -> p k n", k=KC) for i in range(2)]
        num = [cif[:, 4096:4608], kt[:, 4096:4608]]
        tn = [ktf[:, i * 1024:(i + 1) * 1024].rearrange("p (j d) -> p j d", j=4) for i in range(4)]
        qr = [q0[:, 0, :], xn[:, 0, :], q0[:, 1, :], xn[:, 1, :]]
        zero = q0[:, 1, NTOK - CH:NTOK]

        Gb = [ctx.enter_context(nc.psum_tensor(f"G{i}", [128, 512], f32)) for i in range(3)]
        Vb = [ctx.enter_context(nc.psum_tensor(f"V{i}", [128, 512], f32)) for i in range(2)]
        Tb = [ctx.enter_context(nc.psum_tensor(f"T{i}", [128, 512], f32)) for i in range(2)]
        Kb = ctx.enter_context(nc.psum_tensor("K0", [128, 512], f32))
        Sb = [Kb, Vb[0]]

        g_full = [sem(f"g_full{i}") for i in range(3)]
        g_out = [sem(f"g_out{i}") for i in range(3)]
        t_full = [sem(f"t_full{i}") for i in range(2)]
        t_out = [sem(f"t_out{i}") for i in range(2)]
        v_out = [sem(f"v_out{i}") for i in range(2)]
        conv_done = sem("conv_done")
        k_full, k_out = sem("k_full"), sem("k_out")
        den_full, den_out = sem("den_full"), sem("den_out")
        logit_full, logit_out = sem("logit_full"), sem("logit_out")
        w_in = sem("w_in")
        setup = sem("setup")
        zset, zfill = sem("zset"), sem("zfill")
        begin_at_1 = [*g_out, *t_out, *v_out]
        prime = sb("prime", [128, 10, NE])
        xt_in = [sem(f"xt_in{i}") for i in range(2)]
        sq_done = sem("sq_done")
        ss_done, root_done, inv_done = sem("ss_done"), sem("root_done"), sem("inv_done")
        ci_in = [sem(f"ci_in{g}") for g in range(NG)]
        dwt_in = [sem(f"dwt_in{i}") for i in range(2)]
        toep_done = sem("toep_done")
        toep_high, toep_split = sem("toep_high"), sem("toep_split")
        in_high, in_split = sem("in_high"), sem("in_split")
        qe_out = [sem(f"qe_out{i}") for i in range(4)]
        rec_done = sem("rec_done")
        y1_out = [sem(f"y1_out{i}") for i in range(2)]
        var_done, sd_done, tn_done = sem("var_done"), sem("sd_done"), sem("tn_done")
        oh_done, sidx_done = sem("oh_done"), sem("sidx_done")
        sc_out = [sem(f"sc_out{i}") for i in range(4)]
        carried = sem("carried")
        bn_eps, bn_sd = sem("bn_eps"), sem("bn_sd")
        chain0 = sem("chain0")
        chain = sem("chain")

        XT = Ring(2, [("ln", u) for u in range(NT)] + [("proj", u) for u in range(NT)])

        def full(eng, b, key):
            bank, n = G[key]
            eng.wait_ge(g_full[bank], b * G.per + n + 1)
            return Gb[bank], g_out[bank]

        def tfull(eng, b, key):
            bank, n = T[key]
            eng.wait_ge(t_full[bank], b * T.per + n + 1)
            return Tb[bank], t_out[bank]

        def emptied(eng, b, key):
            bank, n = G[key]
            hold(eng, g_out[bank], b * G.per + n + 2)

        def grid_ready(eng, b, t_):
            for w in (NT - 3, NT - 2, NT - 1):
                emptied(eng, b, ("qkv", t_, w))

        def matrices(n):
            late_ = n >= NPAIR * FIRST_Q
            i = (n + 1) % 3
            made = toep[:, i, :, :, :] if i < 2 else toep_third[late_]
            low = toep_lo[:, i, :, :, :] if i < 2 else (toep_lo_a, toep_lo_b)[late_][:, :, :, :]
            return made, toep_hi[late_][:, n % 2, :, :, :], low

        def tiles_of(m4):
            return [(j, 4 * m4 + j, min(128, NGRID - 128 * (4 * m4 + j))) for j in range(4) if 4 * m4 + j < NTRT]

        def block_rows(u):
            return xn[:, :, :].rearrange("p k (s n) -> p k s n", s=POS)[:, :, :, 32 * u:32 * u + 32]

        def grid_view(w):
            qy, pair = w // 2, w % 2
            py, i0 = (qy + 2) % BLK, (qy + 2) // BLK
            px, j0 = (2, 0) if pair == 0 else (0, 1)
            return grid[:, py, px:px + 2, i0:i0 + NB, j0:j0 + NB]

        block = ctx.enter_context(nc.Block())

        @block.sync
        def _(sp):
            loads = [(con[:, :], D["con"]), (wq[:, :, :, :], D["wq"]), (wp[:, :, :], D["wp"]), (pwt[:, :, :, :], D["pw"]),
                     (gate[:, :, :], D["gate_w"]), (gate_b[:, :], D["gate_b"].to_broadcast([128, NE]))]
            loads += [(bnr[:, i, :], D[k].to_broadcast([128, CH])) for i, k in
                      enumerate(("bn_gamma", "bn_beta", "bn_mean", "bn_var"))]
            loads += [(kt[:, 0:6 * 128], D["zeros_and_ones"])]
            for dst, src in loads:
                sp.dma_start(dst, src).then_inc(w_in, 16)
            assert 16 * len(loads) == W_IN
            for i, first in enumerate([*qe_out, *y1_out]):
                sp.dma_start(prime[:, i, :], D["gate_b"].to_broadcast([128, NE])).then_inc(first, 16)
            def one_image(b, fills):
                def load_x(key):
                    s, n = XT[key]
                    if key[0] == "ln" and key[1] >= 2:
                        emptied(sp, b, ("mu", key[1] - 2))
                    if key[0] == "proj" and key[1] < 2:
                        emptied(sp, b, ("mu", NT - 2 + key[1]))
                    sp.dma_start(xt[s][:, :, :], D["x"][bass.ds(b, 1), :, key[1] * TILE:(key[1] + 1) * TILE]
                                 .rearrange("o (k p) n -> p (o k) n", p=128)).then_inc(xt_in[s], 16)

                def load_dwt(t_):
                    if t_ < 2:
                        hold(sp, toep_done, b * 96 + 1)
                    else:
                        hold(sp, toep_done, b * 96 + 16 * (t_ - 1) + 1)
                    sp.dma_start(dwt[:, t_ % 2, :, :], D["dw"][t_, :, :, :]).then_inc(dwt_in[t_ % 2], 16)

                def regroup(t_, p):
                    if p == 0:
                        grid_ready(sp, b, t_)
                        if t_ == 0:
                            for i in range(2):
                                hold(sp, y1_out[i], b * 64 + 16)
                    for g in (2 * p, 2 * p + 1):
                        hold(sp, conv_done, b * 96 + 16 * t_ + g + 1)
                        sp.dma_start(conv_in[:, g, :, :].rearrange("p i j -> p (i j)").bitcast(f32),
                                     grid[8 * g:8 * g + 8, :, :, :, :].rearrange("p y x i j -> p (y x) (i j)"))\
                            .then_inc(ci_in[g], 16)
                    for i in next(fills, ()):
                        sp.dma_start(D["slots"][i * 512:(i + 1) * 512, :].rearrange("(p r) d -> p r d", p=128),
                                     zero.rearrange("p (o d) -> p o d", o=1).to_broadcast([128, 4, CH])).then_inc(zfill, 16)

                def q_back(t_, p):
                    h = CHUNKS[t_][1]
                    for g in (2 * p, 2 * p + 1):
                        n = NG * t_ + g
                        hold(sp, v_out[(n // 2) % 2], b * 24 + n // 4 + 2)
                        sp.dma_start(qr[2 + h][8 * g:8 * g + 8, :].rearrange("p (s n) -> p s n", s=POS),
                                     qe[:, g % 4, :]).then_inc(qe_out[g % 4], 16)

                load_x(("ln", 0))
                load_x(("ln", 1))
                if isinstance(b, int):
                    hold(sp, zset, 1)
                load_dwt(0)
                load_dwt(1)
                for u in range(2, NT):
                    load_x(("ln", u))
                for p in range(NPAIR):
                    regroup(0, p)
                for t_ in range(1, NCHUNK):
                    sends_q = CHUNKS[t_ - 1][0] == "q"
                    if t_ == FIRST_Q + 1:
                        hold(sp, zfill, 16 * NFILL)
                    if sends_q:
                        for p in range(NPAIR // 2):
                            q_back(t_ - 1, p)
                    for p in range(NPAIR // 2):
                        regroup(t_, p)
                    for p in range(NPAIR // 2, NPAIR):
                        regroup(t_, p)
                        if sends_q:
                            q_back(t_ - 1, p)
                    if t_ + 1 < NCHUNK:
                        load_dwt(t_ + 1)
                for p in range(NPAIR):
                    q_back(NCHUNK - 1, p)
                load_x(("proj", 0))
                load_x(("proj", 1))
                for u in range(NT):
                    emptied(sp, b, ("proj", u, 0))
                    emptied(sp, b, ("proj", u, 1))
                    sp.dma_start(D["y1"][bass.ds(b * NTOK + u * TILE, TILE), :].rearrange("(j p) d -> p j d", p=128),
                                 y1[u % 2]).then_inc(y1_out[u % 2], 16)
                    if u + 2 < NT:
                        load_x(("proj", u + 2))
            one_image(0, iter([(i, i + 1) for i in range(0, NFILL, 2)]))
            with sp.Fori(1, B) as b:
                one_image(b, iter(()))
            for i in range(2):
                hold(sp, y1_out[i], B * 64 + 16)

        @block.gpsimd
        def _(pool):
            for first in [*begin_at_1, k_out, toep_done, carried]:
                pool.sem_inc(first, 1)
            for i, first in enumerate(sc_out):
                pool.dma_start(prime[:, 6 + i, :], D["gate_b"].to_broadcast([128, NE])).then_inc(first, 16)
            nc.gpsimd.memset(zero, 0.0).then_inc(zset, 1)
            nc.gpsimd.memset(grid[:, :, :, :, :], 0.0).then_inc(setup, 1)
            nc.gpsimd.memset(chosen[:, :, :, :].bitcast(f32), 0.0).then_inc(setup, 1)
            nc.gpsimd.memset(mean_w[:, :], 1.0 / CH).then_inc(setup, 1)
            nc.gpsimd.memset(dn[:, :, :], 0.0).then_inc(setup, 1)
            nc.gpsimd.memset(vt[:, :, :, 128:129], 1.0).then_inc(setup, 1)
            nc.gpsimd.memset(eps[:, 0:1], 1e-6).then_inc(setup, 1)
            nc.gpsimd.memset(eps[:, 1:2], 1e-5).then_inc(setup, 1)
            nc.gpsimd.memset(eps[:, 2:3], 1e-15).then_inc(setup, 1)
            hold(pool, w_in, W_IN)
            with pool.Fori(0, B) as b:
                for t_ in range(NCHUNK):
                    hold(pool, dwt_in[t_ % 2], b * 48 + 16 * (t_ // 2) + 16)
                    for g in range(NG):
                        n = NG * t_ + g
                        if n == NG * FIRST_Q + 4:
                            hold(pool, k_full, b * 4 + 4)
                        hold(pool, conv_done, b * 96 + n + 11)
                        nc.gpsimd.tensor_tensor(
                            matrices(n // 2)[0][:, n % 2, :, :].rearrange("p q (c s) -> p q c s", c=8),
                            dwt[:, t_ % 2, g, :].rearrange("p (q o s) -> p q o s", q=4, o=1).to_broadcast([128, 4, 8, POS]),
                            pwt[:, t_, g, :].rearrange("p (o c s) -> p o c s", o=1, s=1).to_broadcast([128, 4, 8, POS]),
                            ALU.mult).then_inc(toep_done, 1)
                hold(pool, zfill, 16 * NFILL)
                for u in range(NT):
                    hold(pool, sidx_done, b * 8 + u + 1)
                    for j in range(4):
                        nc.gpsimd.indirect_dma_start(
                            out=D["slots"], out_offset=bass.IndirectOffsetOnAxis(ap=sidx[:, u % 4, j:j + 1], axis=0),
                            in_=tn[u % 4][:, j, :], in_offset=None,
                            bounds_check=NSLOT - 1, oob_is_err=False).then_inc(sc_out[u % 4], 16)
            for i in range(4):
                hold(pool, sc_out[i], B * 128 + 16)

        @block.tensor
        def _(pe):
            def bank(b, key):
                i, n = G[key]
                pe.wait_ge(g_out[i], b * G.per + n + 1)
                return Gb[i], g_full[i]

            def tbank(b, key):
                i, n = T[key]
                pe.wait_ge(t_out[i], b * T.per + n + 1)
                return Tb[i], t_full[i]

            mm = nc.tensor.matmul
            pe.sem_inc(conv_done, 16)
            pe.wait_ge(w_in, W_IN)
            pe.wait_ge(setup, 8 + 4)
            with pe.Fori(0, B) as b:
                def mu(u):
                    s, n = XT[("ln", u)]
                    pe.wait_ge(xt_in[s], (b * XT.per + n) * 16 + 16)
                    o, done = bank(b, ("mu", u))
                    for k in range(KC):
                        last = mm(o[:, :], mean_w[:, :], xt[s][:, k, :], start=k == 0, stop=k == 1)
                    last.then_inc(done, 1)

                def var(u):
                    pe.wait_ge(sq_done, b * NT + u + 1)
                    if u == 4:
                        pe.wait_ge(v_out[0], b * 24 + 1)
                    for h in range(2):
                        at = 7 - (2 * (u % 4) + h)
                        for k in range(KC):
                            last = mm(Sb[u // 4][0:8, 0:256], c_["row7"][:, at:at + 8], sq[u % 2][:, k, 256 * h:256 * h + 256],
                                      start=u % 4 + h + k == 0, stop=u % 4 + h + k == 5)
                    last.then_inc(ss_done, 1)

                def norm(u):
                    if u % 4 == 0:
                        pe.wait_ge(inv_done, b * 2 + u // 4 + 1)
                    o, done = bank(b, ("norm", u))
                    for h in range(2):
                        r = 2 * (u % 4) + h
                        last = mm(o[:, 256 * h:256 * h + 256], ident[0:8, r:r + 1].to_broadcast([8, 128]), std[u // 4],
                                  start=True, stop=True)
                    last.then_inc(done, 1)

                def ln():
                    layer_norm(dict(mu=mu, var=var, root=nothing, recip=nothing, norm=norm))
                    for u in range(NT - 3, NT):
                        emptied(pe, b, ("norm", u))

                def qkv(t_):
                    if t_:
                        for g in range(8, NG):
                            pe.wait_ge(ci_in[g], b * 96 + 16 * t_)
                    for w in range(NT):
                        o, done = bank(b, ("qkv", t_, w))
                        for k in range(KC):
                            last = mm(o[:, :], wq[:, k, t_, :], xn[:, k, w * TILE:(w + 1) * TILE],
                                      start=k == 0, stop=k == 1)
                        last.then_inc(done, 1)

                def tr(t_):
                    kind, h = CHUNKS[t_]
                    grid_ready(pe, b, t_)

                    def own_vk(m4):
                        i, n = T[("tr", t_, m4)]
                        pe.wait_ge(t_out[i], b * T.per + n + 2)
                        for j, m, n_ in tiles_of(m4):
                            last = mm(Kb[:, 0:129], ktn[0:n_, m, :], vt[0:n_, m4 % 2, j, :], start=m == 0, stop=m == NTRT - 1)
                        if m4 == NTR - 1:
                            last.then_inc(k_full, 1)

                    if kind == "v":
                        pe.wait_ge(k_out, b * 4 + 2 * h + 1)
                    flat = grid[:, :, :, :, :].rearrange("p y x i j -> p (y x i j)")
                    for m4 in range(NTR):
                        o, done = tbank(b, ("tr", t_, m4))
                        for j, m, n_ in tiles_of(m4):
                            last = nc.tensor.transpose(o[0:n_, 128 * j:128 * j + 128], flat[:, 128 * m:128 * m + n_], ident)
                        last.then_inc(done, 1)
                        if kind == "v" and m4:
                            own_vk(m4 - 1)
                    if kind == "v":
                        own_vk(NTR - 1)

                def conv(t_, half):
                    for g in range(8 * half, 8 * half + 8):
                        n = NG * t_ + g
                        i = (n // 2) % 2
                        if g % 2 == 0:
                            pe.wait_ge(in_split, b * 48 + n // 2 + 1)
                            pe.wait_ge(toep_split, b * 48 + n // 2 + 1)
                            pe.wait_ge(v_out[i], b * 24 + n // 4 + 1)
                        o = Vb[i]
                        at = 256 * (g % 2)
                        for q in range(4):
                            y, x = q // 2, q % 2
                            for hw, hx in HALVES:
                                w = matrices(n // 2)[1 + hw]
                                v = (conv_hi[t_ >= FIRST_Q], conv_in)[hx]
                                last = mm(o[:, at:at + 256], w[:, n % 2, q, :], v[:, g, y:y + NB, x:x + NB],
                                          start=q + hw + hx == 0, stop=q + hw == 4)
                        last.then_inc(conv_done, 1)
                        if g % 2 and g > 1 and CHUNKS[t_][0] != "q":
                            turn_conv(t_, g // 2 - 1)

                def turn_conv(t_, p):
                    n = NG * t_ + 2 * p
                    pe.wait_ge(v_out[(n // 2) % 2], b * 24 + n // 4 + 2)
                    o, done = tbank(b, ("ct", t_, p))
                    for i in range(4):
                        last = nc.tensor.transpose(o[:, 128 * i:128 * i + 128],
                                                   qe[:, (2 * p + i // 2) % 4, 128 * (i % 2):128 * (i % 2) + 128], ident)
                    last.then_inc(done, 1)

                def vka(h):
                    pe.wait_ge(k_out, b * 4 + 2 * h + 2)
                    for p in (6, 7):
                        i, n = T[("ct", 2 * h + 1, p)]
                        pe.wait_ge(t_out[i], b * T.per + n + 2)
                    for m in range(32):
                        hf, s = m // POS, m % POS
                        last = mm(Kb[:, 0:129], kta[:, hf, s, :], vta[:, hf, s, :], start=m == 0, stop=m == 31)
                    last.then_inc(k_full, 1)

                def out():
                    pe.wait_ge(k_out, b * 4 + 5)

                def tile_of(c, s):
                    return qr[c].rearrange("p (s n) -> p s n", s=POS)[:, :, 32 * s:32 * s + 32]

                def dens(s):
                    if s >= 2:
                        pe.wait_ge(den_out, b * NT + s - 1)
                    else:
                        pe.wait_ge(v_out[s], b * 24 + 25)
                    for c in range(4):
                        if s == 0 and c >= 2:
                            for i in range(4):
                                pe.wait_ge(qe_out[i], b * 128 + 64 * (c - 1) + 16)
                        last = mm(Vb[s % 2][0:64, :], dn[:, c, :], tile_of(c, s), start=c == 0, stop=c == 3)
                    last.then_inc(den_full, 1)

                def attend(s):
                    for c in range(4):
                        o, done = bank(b, ("num", s, c))
                        mm(o[:, :], vk[:, c, :], tile_of(c, s), start=True, stop=True).then_inc(done, 1)
                        if c == 0:
                            pe.wait_ge(rec_done, b * NT + s + 1)
                        o, done = bank(b, ("inv", s, c))
                        mm(o[:, :], spread[:, c, :], rec[:, s % 2, :], start=True, stop=True).then_inc(done, 1)
                        if 2 <= s < NT - 1 and c:
                            logits_of(s - 2, [c - 1] if c < 3 else [2, 3])

                def proj(s):
                    emptied(pe, b, ("inv", s, 3))
                    sl, n = XT[("proj", s)]
                    pe.wait_ge(xt_in[sl], (b * XT.per + n) * 16 + 16)
                    for i in range(2):
                        o, done = bank(b, ("proj", s, i))
                        for j in range(2):
                            at = (2 * i + j) * 128
                            oo = o[:, 256 * j:256 * j + 256]
                            for c in range(4):
                                mm(oo, ao[s % 2][:, c, at:at + 128], wp[:, c, :], start=c == 0, stop=False)
                            for k in range(KC):
                                last = mm(oo[:, 128 * k:128 * k + 128], xt[sl][:, k, at:at + 128], ident,
                                          start=False, stop=k == 1)
                        last.then_inc(done, 1)

                def turn(s):
                    pe.wait_ge(tn_done, b * NT + s + 1)
                    for k in range(KC):
                        o, done = tbank(b, ("tn", s, k))
                        for j in range(4):
                            last = nc.tensor.transpose(o[:, 128 * j:128 * j + 128], tn[s % 4][:, j, 128 * k:128 * k + 128], ident)
                        last.then_inc(done, 1)

                def logits_of(s, js):
                    if js[0] == 0:
                        for k in range(KC):
                            i, n = T[("tn", s, k)]
                            pe.wait_ge(t_out[i], b * T.per + n + 2)
                        if s:
                            pe.wait_ge(logit_out, b * NT + s)
                    for j in js:
                        for k in range(KC):
                            last = mm(Kb[:, NE * j:NE * j + NE], tnt[:, k, 128 * j:128 * j + 128], gate[:, k, :],
                                      start=k == 0, stop=k == 1)
                    if js[-1] == 3:
                        last.then_inc(logit_full, 1)

                def logit(s):
                    if s + 2 >= NT - 1:
                        logits_of(s, range(4))

                def rank(s):
                    pe.wait_ge(oh_done, b * NT + s + 1)
                    o, done = tbank(b, ("rank", s))
                    mm(o[:, 0:5 * NE], tri, chosen[:, s % 2, :, :], start=True, stop=False)
                    for j in range(4):
                        last = mm(o[:, NE * (j + 1):5 * NE], ones, chosen[:, s % 2, j:j + 1, :].to_broadcast([128, 4 - j, NE]),
                                  start=False, stop=j == 3)
                    last.then_inc(done, 1)

                image(dict(ln=ln, qkv=qkv, tr=tr, prep=nothing, conv=conv, flush=lambda t_: turn_conv(t_, 7), vka=vka, out=out,
                           den=dens, recip=nothing, attend=attend, proj=proj, turn=turn, logit=logit, rank=rank))

        def pairs_ahead(t_, p):
            n = NPAIR * t_ + p
            last = NPAIR * (FIRST_Q if t_ < FIRST_Q else NCHUNK)
            return [n + 1] if n + 1 < last else [], [n + AHEAD] if n + AHEAD < last else []

        def conv_evacuation(eng, b, t_, half, mine, relu, copy, split):
            kind, h = CHUNKS[t_]
            for p in range(4 * half, 4 * half + 4):
                matrices_ahead, inputs_ahead = pairs_ahead(t_, p)
                split(matrices_ahead, [])
                if kind != "q" and p:
                    turned(eng, b, t_, p - 1, mine, copy)
                if p % 2 != mine:
                    split([], inputs_ahead)
                    continue
                g = 2 * p
                n = NG * t_ + 2 * p
                i = (n // 2) % 2
                eng.wait_ge(conv_done, b * 96 + n + 2 + 16)
                if kind != "q" and p >= 2:
                    j, m = T[("ct", t_, p - 2)]
                    eng.wait_ge(t_full[j], b * T.per + m + 1)
                elif kind != "q" and t_ > 0 or t_ == 4 and p < 2:
                    j, m = T[("ct", t_ - 1, 6 + p)]
                    eng.wait_ge(t_full[j], b * T.per + m + 1)
                elif kind != "q":
                    for k in (g % 4, g % 4 + 1):
                        eng.wait_ge(qe_out[k], b * 128 + 16)
                else:
                    for k in (g % 4, g % 4 + 1):
                        eng.wait_ge(qe_out[k], (b * 8 + 4 * h + g // 4) * 16 + 16)
                (copy if kind == "v" else relu)(qe[:, g % 4:g % 4 + 2, :].rearrange("p g n -> p (g n)"), Vb[i][:, :], v_out[i])
                split([], inputs_ahead)

        def turned(eng, b, t_, p, mine, copy):
            if p % 2 != mine:
                return
            if t_ == 0 and p < 2:
                for i in range(4):
                    eng.wait_ge(sc_out[i], b * 128 + 16)
            o, done = tfull(eng, b, ("ct", t_, p))
            dst = kta if CHUNKS[t_][0] == "k" else vta
            for hf in range(2):
                d = dst[:, hf, :, 16 * p:16 * p + 16].rearrange("p s (g c) -> p g c s", g=2)
                copy(d, o[:, :].rearrange("p (g h c s) -> p g h c s", g=2, h=2, c=8)[:, :, hf, :, :], done if hf else None)

        @block.scalar
        def _(act):
            A = nc.scalar.activation
            act.wait_ge(setup, 8)
            act.wait_ge(bn_eps, 1)
            A(bnr[:, 3, :], bnr[:, 3, :], ACT.Sqrt, bias=eps[:, 1:2]).then_inc(bn_sd, 1)
            with act.Fori(0, B) as b:
                def relu(dst, src, done):
                    A(dst, src, ACT.Relu).then_inc(done, 1)

                def copy(dst, src, done):
                    ins = A(dst, src, ACT.Copy)
                    if done:
                        ins.then_inc(done, 1)

                def mu(u):
                    emptied(act, b, ("mu", u))
                    if u >= 2:
                        act.wait_ge(ss_done, b * NT + u - 1)
                    A(sq[u % 2].rearrange("p k (s n) -> p k s n", s=POS), block_rows(u), ACT.Square).then_inc(sq_done, 1)

                def root(half):
                    act.wait_ge(ss_done, b * NT + 4 * half + 4)
                    A(std[half], Sb[half][0:8, 0:256], ACT.Sqrt, bias=eps[0:8, 0:1]).then_inc(root_done, 1)

                def ln():
                    layer_norm(dict(mu=mu, var=nothing, root=root, recip=nothing, norm=nothing))

                def qkv(t_):
                    kind, h = CHUNKS[t_]
                    for w in range(0, NT, 2):
                        o, done = full(act, b, ("qkv", t_, w))
                        ins = A(grid_view(w), o[:, :].rearrange("p (x i j) -> p x i j", x=2, i=NB), ACT.Copy)
                        if kind == "q":
                            ins = A(qr[h][:, w * TILE:(w + 1) * TILE], o[:, :], ACT.Relu)
                        ins.then_inc(done, 1)

                def split(pairs, inputs):
                    for n in pairs:
                        act.wait_ge(toep_done, b * 96 + 2 * n + 3)
                        act.wait_ge(conv_done, b * 96 + 2 * n + 14)
                        made, high, low = matrices(n)
                        A(high, made, ACT.Copy).then_inc(toep_high, 1)
                    for n in inputs:
                        g, t_ = 2 * (n % NPAIR), n // NPAIR
                        for i in range(2):
                            act.wait_ge(ci_in[g + i], b * 96 + 16 * (t_ + 1))
                        A(conv_hi[t_ >= FIRST_Q][:, g:g + 2, :, :], conv_in[:, g:g + 2, :, :].bitcast(f32), ACT.Copy)\
                            .then_inc(in_high, 1)

                def prep(t_):
                    if t_ == FIRST_Q:
                        act.wait_ge(k_full, b * 4 + 4)
                    split([NPAIR * t_], range(NPAIR * t_, NPAIR * t_ + AHEAD))

                def tr(t_):
                    for m4 in range(0, NTR, 2):
                        o, done = tfull(act, b, ("tr", t_, m4))
                        o = o[:, :].rearrange("p (j c) -> p j c", j=4)
                        n, rows = len(tiles_of(m4)), tiles_of(m4)[-1][2]
                        if CHUNKS[t_][0] == "k":
                            relu(ktn[0:rows, 4 * m4:4 * m4 + n, :], o[0:rows, 0:n, :], done)
                        else:
                            copy(vt[0:rows, m4 % 2, 0:n, 0:128], o[0:rows, 0:n, :], done)

                def dens(s):
                    act.wait_ge(den_full, b * NT + s + 1)
                    if s >= 2:
                        full(act, b, ("inv", s - 2, 3))
                    A(den[s % 2], Vb[s % 2][0:64, :], ACT.Identity, bias=eps[0:64, 2:3]).then_inc(den_out, 1)

                def attend(s):
                    for c in range(4):
                        if c >= 2:
                            emptied(act, b, ("inv", s, c - 2))
                        elif s:
                            emptied(act, b, ("inv", s - 1, c + 2))
                        o, done = full(act, b, ("num", s, c))
                        A(num[c % 2], o[:, :], ACT.Copy).then_inc(done, 1)

                def proj(s):
                    act.wait_ge(var_done, b * NT + s + 1)
                    A(stat[:, s % 2, :, 8:9], stat[:, s % 2, :, 7:8], ACT.Sqrt, bias=eps[:, 1:2]).then_inc(sd_done, 1)

                def turn(s):
                    for k in range(KC):
                        o, done = tfull(act, b, ("tn", s, k))
                        A(tnt[:, k, :], o[:, :], ACT.Copy).then_inc(done, 1)

                image(dict(ln=ln, qkv=qkv, tr=tr, prep=prep, out=nothing, vka=nothing, den=dens, attend=attend, proj=proj,
                           turn=turn, logit=nothing, recip=nothing, rank=nothing, flush=lambda t_: turned(act, b, t_, 7, 0, copy),
                           conv=lambda t_, half: conv_evacuation(act, b, t_, half, 0, relu, copy, split)))

        @block.vector
        def _(dve):
            V = nc.vector
            here = [0]

            def link0(ins):
                here[0] += 1
                ins.then_inc(chain0, 1)
                dve.wait_ge(chain0, here[0])

            dve.wait_ge(w_in, W_IN)
            dve.wait_ge(setup, 8)
            dve.sem_inc(bn_eps, 1)
            dve.wait_ge(bn_sd, 1)
            link0(V.reciprocal(bnr[:, 3, :], bnr[:, 3, :]))
            link0(V.tensor_tensor(bnr[:, 0, :], bnr[:, 0, :], bnr[:, 3, :], ALU.mult))
            link0(V.tensor_tensor(bnr[:, 2, :], bnr[:, 2, :], bnr[:, 0, :], ALU.mult))
            V.tensor_tensor(bias[:, :], bnr[:, 1, :], bnr[:, 2, :], ALU.subtract).then_inc(setup, 1)
            V.tensor_tensor(wp[:, :, :], wp[:, :, :], bnr[:, 0:1, :].to_broadcast([128, 4, CH]), ALU.mult).then_inc(setup, 1)
            V.tensor_copy(carry[:, :], c_["carry0"]).then_inc(setup, 1)
            V.tensor_copy(zeros_and_ones[:, :, :], kt[:, 0:6 * 128].rearrange("p (c m) -> p c m", c=6)).then_inc(setup, 1)
            dve.wait_ge(setup, 12)
            with dve.Fori(0, B) as b:
                here = [0]

                def link(ins):
                    here[0] += 1
                    ins.then_inc(chain, 1)
                    dve.wait_ge(chain, b * LINKS + here[0])

                def relu(dst, src, done):
                    V.tensor_scalar_max(dst, src, 0.0).then_inc(done, 1)

                def copy(dst, src, done):
                    ins = V.tensor_copy(dst, src)
                    if done:
                        ins.then_inc(done, 1)

                def mu(u):
                    s, n = XT[("ln", u)]
                    dve.wait_ge(xt_in[s], (b * XT.per + n) * 16 + 16)
                    o, done = full(dve, b, ("mu", u))
                    for k in range(KC):
                        for i in range(2):
                            src = [a[:, 256 * i:256 * i + 256].rearrange("p (q j x) -> p q x j", q=4, x=4)
                                   for a in (xt[s][:, k, :], o)]
                            dst = xn[:, k, :].rearrange("p (q x i j) -> p q x i j", q=4, x=4, i=NB)
                            ins = V.tensor_tensor(dst[:, :, :, 2 * u + i, :], src[0], src[1], ALU.subtract)
                    ins.then_inc(done, 1)

                def inverse(half):
                    dve.wait_ge(root_done, b * 2 + half + 1)
                    V.reciprocal(std[half], std[half]).then_inc(inv_done, 1)

                def norm(u):
                    o, done = full(dve, b, ("norm", u))
                    V.tensor_tensor(block_rows(u), block_rows(u), o[:, :].rearrange("p (o s n) -> p o s n", o=1, s=POS)
                                    .to_broadcast([128, KC, POS, 2 * NB]), ALU.mult).then_inc(done, 1)

                def ln():
                    layer_norm(dict(mu=mu, var=nothing, root=nothing, recip=inverse, norm=norm))

                def qkv(t_):
                    kind, h = CHUNKS[t_]
                    for w in range(1, NT, 2):
                        o, done = full(dve, b, ("qkv", t_, w))
                        ins = V.tensor_copy(grid_view(w), o[:, :].rearrange("p (x i j) -> p x i j", x=2, i=NB))
                        if kind == "q":
                            ins = V.tensor_scalar_max(qr[h][:, w * TILE:(w + 1) * TILE], o[:, :], 0.0)
                        ins.then_inc(done, 1)

                def kv(c):
                    h, conv = c % 2, c // 2
                    dve.wait_ge(k_full, b * 4 + 2 * h + conv + 1)
                    V.tensor_tensor(vk[:, c, :], Kb[:, 0:128], c_["gmask"], ALU.mult)
                    V.tensor_scalar(dn[:, c, 16 * c:16 * c + 16], c_["gm16"], Kb[:, 128:129], None, ALU.mult)\
                        .then_inc(k_out, 1)

                def split(pairs, inputs):
                    for n in pairs:
                        dve.wait_ge(toep_high, b * 48 + n + 1)
                        made, high, low = matrices(n)
                        V.tensor_tensor(low, made, high, ALU.subtract).then_inc(toep_split, 1)
                    for n in inputs:
                        g, t_ = 2 * (n % NPAIR), n // NPAIR
                        dve.wait_ge(in_high, b * 48 + n + 1)
                        V.tensor_tensor(conv_in[:, g:g + 2, :, :], conv_in[:, g:g + 2, :, :].bitcast(f32),
                                        conv_hi[t_ >= FIRST_Q][:, g:g + 2, :, :], ALU.subtract).then_inc(in_split, 1)

                def prep(t_):
                    split([NPAIR * t_], range(NPAIR * t_, NPAIR * t_ + AHEAD))

                def tr(t_):
                    for m4 in range(1, NTR, 2):
                        o, done = tfull(dve, b, ("tr", t_, m4))
                        o = o[:, :].rearrange("p (j c) -> p j c", j=4)
                        n, rows = len(tiles_of(m4)), tiles_of(m4)[-1][2]
                        if CHUNKS[t_][0] == "k":
                            relu(ktn[0:rows, 4 * m4:4 * m4 + n, :], o[0:rows, 0:n, :], done)
                        else:
                            copy(vt[0:rows, m4 % 2, 0:n, 0:128], o[0:rows, 0:n, :], done)
                    if CHUNKS[t_][0] == "v":
                        kv(CHUNKS[t_][1])
                        V.memset(vta[:, :, :, 128:129], 1.0)

                def recip(s):
                    dve.wait_ge(den_out, b * NT + s + 1)
                    link(V.reciprocal(den[s % 2], den[s % 2]))
                    link(V.tensor_copy(rec[0:64, s % 2, :], den[s % 2]))
                    V.tensor_tensor(rec[64:128, s % 2, :], den[s % 2], rec[0:64, s % 2, :], ALU.subtract).then_inc(rec_done, 1)

                def attend(s):
                    for c in range(4):
                        o, done = full(dve, b, ("inv", s, c))
                        emptied(dve, b, ("num", s, c))
                        for i in range(2):
                            src = [a.rearrange("p (q x i j) -> p q x i j", q=4, x=4, i=2)[:, :, :, i, :]
                                   for a in (num[c % 2], o[:, :])]
                            dst = ao[s % 2][:, c, 256 * i:256 * i + 256].rearrange("p (q j x) -> p q x j", q=4, x=4)
                            ins = V.tensor_tensor(dst, src[0], src[1], ALU.mult)
                        ins.then_inc(done, 1)

                def proj(s):
                    dve.wait_ge(y1_out[s % 2], (b * 4 + s // 2) * 16 + 16)
                    for i in range(2):
                        o, done = full(dve, b, ("proj", s, i))
                        V.tensor_tensor(y1[s % 2][:, 2 * i:2 * i + 2, :], o[:, :].rearrange("p (j d) -> p j d", j=2),
                                        bias[:, :].rearrange("p (o d) -> p o d", o=1).to_broadcast([128, 2, CH]),
                                        ALU.add).then_inc(done, 1)
                    st = stat[:, s % 2, :, :]
                    emptied(dve, b, ("proj", s, 0))
                    emptied(dve, b, ("proj", s, 1))
                    for j in range(4):
                        ins = V.bn_stats(st[:, j, 0:6], y1[s % 2][:, j, :])
                    link(ins)
                    dve.nop(nofuse=True)
                    for j in range(4):
                        ins = V.bn_aggr(st[:, j, 6:8], st[:, j, 0:6])
                    ins.then_inc(var_done, 1)
                    dve.wait_ge(sd_done, b * NT + s + 1)
                    link(V.reciprocal(st[:, :, 14:15], st[:, :, 8:9]))
                    dve.wait_ge(sc_out[s % 4], (b * 2 + s // 4) * 64 + 16)
                    for j in range(4):
                        ins = V.tensor_scalar(tn[s % 4][:, j, :], y1[s % 2][:, j, :], st[:, j, 6:7], st[:, j, 14:15],
                                              ALU.subtract, ALU.mult)
                    ins.then_inc(tn_done, 1)

                def logit(s):
                    dve.wait_ge(logit_full, b * NT + s + 1)
                    st, sm = stat[:, s % 2, :, :], small[:, s % 2, :, :]
                    oh, lg, cand = chosen[:, s % 2, 0:4, :], sm[:, :, 8:16], sm[:, :, 16:24]
                    d = dlog[:, bass.ds(b * 32 + 4 * s, 4), :]
                    over4 = lambda a: a.rearrange("p (o e) -> p o e", o=1).to_broadcast([128, 4, NE])
                    V.tensor_tensor(lg, Kb[:, 0:32].rearrange("p (j e) -> p j e", j=4), over4(gate_b[:, :]),
                                    ALU.add).then_inc(logit_out, 1)
                    dve.wait_ge(logit_out, b * NT + s + 1)
                    link(V.tensor_reduce(st[:, :, 9:10], lg, AX.X, ALU.max))
                    link(V.tensor_tensor(d, lg, st[:, :, 9:10].to_broadcast([128, 4, NE]), ALU.subtract))
                    link(V.tensor_scalar(cand, d, 0.0, None, ALU.is_ge))
                    link(V.tensor_tensor(cand, cand, over4(c_["rev"]), ALU.mult))
                    link(V.tensor_reduce(st[:, :, 10:11], cand, AX.X, ALU.max))
                    V.tensor_tensor(oh, over4(c_["rev"]), st[:, :, 10:11].to_broadcast([128, 4, NE]),
                                    ALU.is_equal).then_inc(oh_done, 1)

                def rank(s):
                    o, done = tfull(dve, b, ("rank", s))
                    dve.wait_ge(oh_done, b * NT + s + 1)
                    st, sm = stat[:, s % 2, :, :], small[:, s % 2, :, :]
                    oh, pos = chosen[:, s % 2, 0:4, :], sm[:, :, 16:24]
                    at = bass.ds(b * 32 + 4 * s, 4)
                    dve.wait_ge(carried, b * NT + s + 1)
                    link(V.tensor_tensor(pos, o[:, 0:32].rearrange("p (j e) -> p j e", j=4),
                                         carry[:, :].rearrange("p (o e) -> p o e", o=1).to_broadcast([128, 4, NE]), ALU.add))
                    V.tensor_tensor(carry[:, :], carry[:, :], o[:, 32:32 + NE], ALU.add).then_inc(carried, 1)
                    link(V.tensor_tensor(pos, pos, oh, ALU.mult))
                    link(V.tensor_reduce(st[:, :, 11:12], pos, AX.X, ALU.add))
                    link(V.tensor_scalar(st[:, :, 12:13], st[:, :, 10:11], float(-CAP), float(NE * CAP + CAP - 1),
                                         ALU.mult, ALU.add))
                    dve.wait_ge(carried, b * NT + s + 2)
                    dve.sem_inc(done, 1)
                    kp = kept[:, at].rearrange("p (j o) -> p j o", o=1)
                    link(V.tensor_tensor(kp, st[:, :, 11:12], st[:, :, 12:13], ALU.is_le))
                    V.tensor_tensor(gidx[:, at].rearrange("p (j o) -> p j o", o=1), st[:, :, 11:12], st[:, :, 12:13], ALU.min)
                    link(V.tensor_scalar(st[:, :, 13:14], kp, -float(NSLOT), float(NSLOT), ALU.mult, ALU.add))
                    V.tensor_tensor(sidx[:, s % 4, :].rearrange("p (j o) -> p j o", o=1), st[:, :, 11:12], st[:, :, 13:14],
                                    ALU.add).then_inc(sidx_done, 1)

                image(dict(ln=ln, qkv=qkv, tr=tr, prep=prep, out=nothing, vka=lambda h: kv(2 + h), den=nothing, recip=recip,
                           attend=attend, proj=proj, turn=nothing, logit=logit, rank=rank, flush=lambda t_: turned(dve, b, t_, 7, 1, copy),
                           conv=lambda t_, half: conv_evacuation(dve, b, t_, half, 1, relu, copy, split)))
                assert here[0] == LINKS, here[0]


def experts(nc, D):
    f32, f32r = mybir.dt.float32, mybir.dt.float32r
    ALU, ACT = mybir.AluOpType, mybir.ActivationFunctionType
    PER = 2 * NSB
    SECOND_LOAD = 4
    with ExitStack() as ctx:
        def sb(name, shape, dt=f32):
            return ctx.enter_context(nc.sbuf_tensor(name, shape, dt))

        def sem(name):
            return ctx.enter_context(nc.semaphore(name))

        w1s = sb("w1s", [128, KC, FF])
        w2s = sb("w2s", [128, FT, CH])
        w1 = [[sb(f"w1_{i}{h}", [128, KC, FF], f32r) for h in range(2)] for i in range(2)]
        w2 = [[sb(f"w2_{i}{h}", [128, FT, CH], f32r) for h in range(2)] for i in range(2)]
        b1 = [sb(f"b1_{i}", [128, FT]) for i in range(2)]
        b2 = [sb(f"b2_{i}", [128, CH]) for i in range(2)]
        rows = [sb(f"rows{i}", [128, 4, CH]) for i in range(2)]
        rowt = [[sb(f"rowt{i}{h}", [128, KC, TILE], f32r) for h in range(2)] for i in range(2)]
        act_out = sb("act_out", [128, 4, TILE])
        hid = [[sb(f"hid{i}{h}", [128, FT, TILE], f32r) for h in range(2)] for i in range(2)]
        yr = [sb(f"yr{i}", [128, 4, CH]) for i in range(2)]
        ident = sb("ident2", [128, 128])
        prime = sb("prime2", [128, 2, NE])
        Rb = [ctx.enter_context(nc.psum_tensor(f"R{i}", [128, 512], f32)) for i in range(2)]
        Hb = [ctx.enter_context(nc.psum_tensor(f"H{i}", [128, 512], f32)) for i in range(4)]
        Yb = [ctx.enter_context(nc.psum_tensor(f"Y{i}", [128, 512], f32)) for i in range(2)]
        id_in = sem("id_in")
        w_in = [sem(f"ew_in{i}") for i in range(2)]
        w_split = sem("w_split")
        w_hi = sem("w_hi")
        rows_in = [sem(f"rows_in{i}") for i in range(2)]
        r_full = [sem(f"r_full{i}") for i in range(2)]
        r_hi = sem("r_hi")
        r_out = [sem(f"r_out{i}") for i in range(2)]
        h_full = [sem(f"h_full{i}") for i in range(4)]
        h_out = [sem(f"h_out{i}") for i in range(4)]
        h_split = sem("h_split")
        y_full = [sem(f"y_full{i}") for i in range(2)]
        y_out = [sem(f"y_out{i}") for i in range(2)]
        stored = [sem(f"stored{i}") for i in range(2)]
        block = ctx.enter_context(nc.Block())

        def slots(ap, n):
            return ap[bass.ds(n * TILE, TILE), :].rearrange("(p j) d -> p j d", j=4)

        @block.sync
        def _(sp):
            sp.dma_start(ident[:, :], D["con"][:, CON["ident"][0]:CON["ident"][1]]).then_inc(id_in, 16)
            with sp.Fori(0, NE // 2) as ep:
                def weights(par):
                    e = bass.ds(ep * 2 + par, 1)
                    hold(sp, y_full[1], ep * PER + 1 + NSB * par)
                    hold(sp, w_split, ep * 4 + 2 * par + 1)
                    sp.dma_start(w1s[:, :, :], D["w1"][e, :, :].rearrange("o (k p) f -> p (o k) f", p=128)).then_inc(w_in[0], 16)
                    sp.dma_start(b1[par][:, :], D["b1"][e, :, :].rearrange("o p f -> p (o f)")).then_inc(w_in[0], 16)
                    sp.dma_start(w2s[:, :, :], D["w2"][e, :, :].rearrange("o (k p) d -> p (o k) d", p=128)).then_inc(w_in[1], 16)
                    sp.dma_start(b2[par][:, :], D["b2"][e, :].to_broadcast([128, CH])).then_inc(w_in[1], 16)

                for m in range(PER):
                    if m == 0:
                        weights(0)
                    if m == SECOND_LOAD:
                        weights(1)
                    hold(sp, r_full[1], ep * PER + m + 1)
                    sp.dma_start(rows[m % 2][:, :, :], slots(D["slots"], ep * PER + m)).then_inc(rows_in[m % 2], 16)

        @block.gpsimd
        def _(pool):
            for first in [*r_out, *h_out, *y_out, w_split]:
                pool.sem_inc(first, 1)
            pool.sem_inc(h_split, 4)
            pool.sem_inc(r_full[1], 2)
            pool.sem_inc(y_full[1], NSB + 1)
            for i in range(2):
                pool.dma_start(prime[:, i, :], D["gate_b"].to_broadcast([128, NE])).then_inc(stored[i], 16)
            with pool.Fori(0, NE // 2) as ep:
                for m in range(PER):
                    for i in range(2):
                        hold(pool, y_out[i], ep * PER + m + 2)
                    pool.dma_start(slots(D["ybuf"], ep * PER + m), yr[m % 2][:, :, :]).then_inc(stored[m % 2], 16)
            for i in range(2):
                hold(pool, stored[i], 16 * NE * NSB // 2 + 16)

        @block.tensor
        def _(pe):
            mm = nc.tensor.matmul
            pe.wait_ge(id_in, 16)
            with pe.Fori(0, NE // 2) as ep:
                def turn(m):
                    pe.wait_ge(rows_in[m % 2], (ep * NSB + m // 2 + 1) * 16)
                    for k in range(KC):
                        pe.wait_ge(r_out[k], ep * PER + m + 1)
                        for j in range(4):
                            last = nc.tensor.transpose(Rb[k][:, 128 * j:128 * j + 128], rows[m % 2][:, j, 128 * k:128 * k + 128],
                                                       ident[:, :])
                        last.then_inc(r_full[k], 1)

                def first(m):
                    par, s = m // NSB, m % 2
                    if m % NSB == 0:
                        pe.wait_ge(w_split, ep * 4 + 2 * par + 2)
                    for k in range(KC):
                        pe.wait_ge(r_out[k], ep * PER + m + 2)
                    for f in range(FT):
                        pe.wait_ge(h_out[f % 4], 2 * (ep * PER + m) + f // 4 + 1)
                        for k in range(KC):
                            for hw, hx in HALVES:
                                last = mm(Hb[f % 4][:, :], w1[par][hw][:, k, 128 * f:128 * f + 128], rowt[s][hx][:, k, :],
                                          start=k + hw + hx == 0, stop=k + hw == 2)
                        last.then_inc(h_full[f % 4], 1)

                def second(m):
                    par, s = m // NSB, m % 2
                    if m % NSB == 0:
                        pe.wait_ge(w_split, ep * 4 + 2 * par + 3)
                    pe.wait_ge(h_split, (ep * PER + m) * FT + FT + 4)
                    for i in range(2):
                        pe.wait_ge(y_out[i], ep * PER + m + 1)
                        for j in range(2 * i, 2 * i + 2):
                            for f in range(FT):
                                for hh, hw in HALVES:
                                    last = mm(Yb[i][:, 256 * (j % 2):256 * (j % 2) + 256],
                                              hid[s][hh][:, f, 128 * j:128 * j + 128], w2[par][hw][:, f, :],
                                              start=f + hh + hw == 0, stop=f + hh == FT)
                        last.then_inc(y_full[i], 1)

                turn(0)
                for m in range(PER):
                    first(m)
                    if m + 1 < PER:
                        turn(m + 1)
                    if m:
                        second(m - 1)
                second(PER - 1)

        @block.scalar
        def _(act):
            A = nc.scalar.activation
            with act.Fori(0, NE // 2) as ep:
                def turn(m):
                    for k in range(KC):
                        act.wait_ge(r_full[k], ep * PER + m + 1 + 2 * k)
                        A(rowt[m % 2][0][:, k, :], Rb[k][:, :], ACT.Copy).then_inc(r_hi, 1)

                turn(0)
                for m in range(PER):
                    par = m // NSB
                    for f in range(FT):
                        act.wait_ge(h_full[f % 4], 2 * (ep * PER + m) + f // 4 + 1)
                        act.wait_ge(h_split, (ep * PER + m) * FT + f + 1)
                        A(act_out[:, f % 4, :], Hb[f % 4][:, :], ACT.Relu, bias=b1[par][:, f:f + 1])
                        A(hid[m % 2][0][:, f, :], Hb[f % 4][:, :], ACT.Relu, bias=b1[par][:, f:f + 1]).then_inc(h_out[f % 4], 1)
                    if m + 1 < PER:
                        turn(m + 1)

        @block.vector
        def _(dve):
            V = nc.vector
            with dve.Fori(0, NE // 2) as ep:
                def split(par, layer):
                    src, dst = ((w1s, w1[par]), (w2s, w2[par]))[layer]
                    dve.wait_ge(w_in[layer], (ep * 4 + 2 * par + 2) * 16)
                    V.tensor_copy(dst[0][:, :, :], src[:, :, :]).then_inc(w_hi, 1)
                    dve.wait_ge(w_hi, ep * 4 + 2 * par + layer + 1)
                    V.tensor_tensor(dst[1][:, :, :], src[:, :, :], dst[0][:, :, :], ALU.subtract).then_inc(w_split, 1)

                def turn(m):
                    for k in range(KC):
                        dve.wait_ge(r_hi, (ep * PER + m) * KC + k + 1)
                        V.tensor_tensor(rowt[m % 2][1][:, k, :], Rb[k][:, :], rowt[m % 2][0][:, k, :], ALU.subtract)\
                            .then_inc(r_out[k], 1)

                def biased(m):
                    par, s = m // NSB, m % 2
                    dve.wait_ge(stored[s], (ep * NSB + m // 2) * 16 + 16)
                    for i in range(2):
                        dve.wait_ge(y_full[i], ep * PER + m + 1 + (NSB + 1) * i)
                        V.tensor_tensor(yr[s][:, 2 * i:2 * i + 2, :], Yb[i][:, :].rearrange("p (j d) -> p j d", j=2),
                                        b2[par][:, :].rearrange("p (o d) -> p o d", o=1).to_broadcast([128, 2, CH]),
                                        ALU.add).then_inc(y_out[i], 1)

                split(0, 0)
                turn(0)
                split(0, 1)
                for m in range(PER):
                    for f in range(FT):
                        dve.wait_ge(h_out[f % 4], 2 * (ep * PER + m) + f // 4 + 2)
                        V.tensor_tensor(hid[m % 2][1][:, f, :], act_out[:, f % 4, :], hid[m % 2][0][:, f, :], ALU.subtract)\
                            .then_inc(h_split, 1)
                    if m + 1 < PER:
                        turn(m + 1)
                    if m == SECOND_LOAD + 1:
                        split(1, 0)
                        split(1, 1)
                    if m:
                        biased(m - 1)
                biased(PER - 1)


def combine(nc, keep, D, out):
    f32, f32r, u32 = mybir.dt.float32, mybir.dt.float32r, mybir.dt.uint32
    ALU, ACT, AX = mybir.AluOpType, mybir.ActivationFunctionType, mybir.AxisListType
    dlog, kept, gidx = keep
    with ExitStack() as ctx:
        def sb(name, shape, dt=f32):
            return ctx.enter_context(nc.sbuf_tensor(name, shape, dt))

        def sem(name):
            return ctx.enter_context(nc.semaphore(name))

        NS = 4
        yg = [sb(f"yg{i}", [128, 4, CH]) for i in range(NS)]
        yl = [sb(f"yl{i}", [128, 4, CH]) for i in range(NS)]
        v = [sb(f"v{i}", [128, 4, CH]) for i in range(2)]
        mag = [sb(f"mag{i}", [128, 4, CH]) for i in range(2)]
        lim = [sb(f"lim{i}", [128, 4, CH]) for i in range(2)]
        clip = [sb(f"clip{i}", [128, 4, CH], f32r) for i in range(2)]
        zt = [sb(f"zt{i}", [128, KC, TILE]) for i in range(2)]
        pick = sb("pick", [128, NS, 4], u32)
        wsel = sb("wsel", [128, NS, 4])
        wgt = sb("wgt", [128, TOKENS // 128])
        ident = sb("ident3", [128, 128])
        ident_r = sb("ident3r", [128, 128], f32r)
        prime = sb("prime3", [128, 2, NE])
        Pb = [ctx.enter_context(nc.psum_tensor(f"P{i}", [128, 512], f32)) for i in range(4)]
        id_in, id_copied = sem("id_in3"), sem("id_copied")
        exp_done, chain3, w_done = sem("exp_done"), sem("chain3"), sem("w_done")
        yl_in = [sem(f"yl_in{i}") for i in range(NS)]
        yg_in = [sem(f"yg_in{i}") for i in range(NS)]
        picked = sem("picked")
        v_done, mag_done, z_done = sem("v_done"), sem("mag_done"), sem("z_done")
        p_full = [sem(f"p_full{i}") for i in range(4)]
        p_out = [sem(f"p_out{i}") for i in range(4)]
        o_out = [sem(f"o_out{i}") for i in range(2)]
        block = ctx.enter_context(nc.Block())

        @block.sync
        def _(sp):
            sp.dma_start(ident[:, :], D["con"][:, CON["ident"][0]:CON["ident"][1]]).then_inc(id_in, 16)
            for i in range(2):
                sp.dma_start(prime[:, i, :], D["gate_b"].to_broadcast([128, NE])).then_inc(o_out[i], 16)
            with sp.Fori(0, B) as b:
                def load(u):
                    hold(sp, p_full[2 * (u % 2) + 1], b * 4 + u // 2 + 1)
                    sp.dma_start(yl[u % NS][:, :, :], D["y1"][bass.ds(b * NTOK + u * TILE, TILE), :]
                                 .rearrange("(j p) d -> p j d", p=128)).then_inc(yl_in[u % NS], 16)

                for u in range(NS - 1):
                    load(u)
                for u in range(NT):
                    if u + NS - 1 < NT:
                        load(u + NS - 1)
                    for k in range(KC):
                        hold(sp, p_out[2 * (u % 2) + k], b * 4 + u // 2 + 2)
                    sp.dma_start(out[bass.ds(b, 1), :, u * TILE:(u + 1) * TILE].rearrange("o (k p) n -> p (o k) n", p=128),
                                 zt[u % 2][:, :, :]).then_inc(o_out[u % 2], 16)
            for i in range(2):
                hold(sp, o_out[i], 16 * QUADS // 2 + 16)

        @block.gpsimd
        def _(pool):
            for first in p_out:
                pool.sem_inc(first, 1)
            for first in p_full:
                pool.sem_inc(first, 2)
            for first in (z_done, v_done):
                pool.sem_inc(first, NS)
            with pool.Fori(0, B) as b:
                for u in range(NT):
                    s = u % NS
                    hold(pool, v_done, b * NT + u + 1)
                    nc.gpsimd.tensor_copy(pick[:, s, :], gidx[:, bass.ds(b * 32 + 4 * u, 4)]).then_inc(picked, 1)
                    hold(pool, picked, b * NT + u + 1)
                    for j in range(4):
                        nc.gpsimd.indirect_dma_start(
                            out=yg[s][:, j, :], out_offset=None, in_=D["ybuf"],
                            in_offset=bass.IndirectOffsetOnAxis(ap=pick[:, s, j:j + 1], axis=0),
                            bounds_check=NSLOT - 1, oob_is_err=False).then_inc(yg_in[s], 16)

        @block.tensor
        def _(pe):
            pe.wait_ge(id_in, 16)
            pe.wait_ge(id_copied, 1)
            with pe.Fori(0, B) as b:
                for u in range(NT):
                    pe.wait_ge(yl_in[u % NS], (b * 2 + u // NS + 1) * 16)
                    pe.wait_ge(z_done, b * NT + u + 1 + NS)
                    for k in range(KC):
                        i = 2 * (u % 2) + k
                        pe.wait_ge(p_out[i], b * 4 + u // 2 + 1)
                        for j in range(4):
                            for n, part in enumerate((yl[u % NS], lim[u % 2], clip[u % 2])):
                                last = nc.tensor.matmul(Pb[i][:, 128 * j:128 * j + 128], part[:, j, 128 * k:128 * k + 128],
                                                        (ident, ident_r)[n == 2][:, :], start=n == 0, stop=n == 2)
                        last.then_inc(p_full[i], 1)

        @block.scalar
        def _(act):
            A = nc.scalar.activation
            A(dlog[:, :, :], dlog[:, :, :], ACT.Exp).then_inc(exp_done, 1)
            act.wait_ge(w_done, 1)
            with act.Fori(0, B) as b:
                for u in range(NT + 1):
                    if u < NT:
                        s = u % NS
                        act.wait_ge(yg_in[s], (b * 2 + u // NS + 1) * 64)
                        act.wait_ge(z_done, b * NT + u + 3)
                        for j in range(4):
                            ins = A(v[u % 2][:, j, :], yg[s][:, j, :], ACT.Copy, scale=wgt[:, bass.ds(b * 32 + 4 * u + j, 1)])
                        ins.then_inc(v_done, 1)
                        act.wait_ge(v_done, b * NT + u + 1 + NS)
                        A(mag[u % 2][:, :, :], v[u % 2][:, :, :], ACT.Abs).then_inc(mag_done, 1)
                    if u:
                        w = u - 1
                        i = 2 * (w % 2)
                        act.wait_ge(p_full[i], b * 4 + w // 2 + 3)
                        act.wait_ge(o_out[w % 2], (b * 4 + w // 2) * 16 + 16)
                        A(zt[w % 2][:, 0, :], Pb[i][:, :], ACT.Copy).then_inc(p_out[i], 1)

        @block.vector
        def _(dve):
            V = nc.vector
            dve.wait_ge(id_in, 16)
            V.tensor_copy(ident_r[:, :], ident[:, :]).then_inc(id_copied, 1)
            dve.wait_ge(exp_done, 1)
            V.tensor_reduce(wgt[:, :].rearrange("p (n o) -> p n o", o=1), dlog[:, :, :], AX.X, ALU.add).then_inc(chain3, 1)
            dve.wait_ge(chain3, 1)
            V.reciprocal(wgt[:, :], wgt[:, :]).then_inc(chain3, 1)
            dve.wait_ge(chain3, 2)
            V.tensor_tensor(wgt[:, :], wgt[:, :], kept[:, :], ALU.mult).then_inc(w_done, 1)
            with dve.Fori(0, B) as b:
                here = [2]

                def link(ins):
                    here[0] += 1
                    ins.then_inc(chain3, 1)
                    dve.wait_ge(chain3, b * LINKS3 + here[0])

                for u in range(NT + 1):
                    if u < NT:
                        s = u % 2
                        flat = lambda a: a[:, :, :].rearrange("p j d -> p (j d)")
                        vv, mm_, ll, cc = flat(v[s]), flat(mag[s]), flat(lim[s]), flat(clip[s])
                        dve.wait_ge(mag_done, b * NT + u + 1)
                        dve.wait_ge(p_full[2 * s + 1], b * 4 + u // 2 + 2)
                        V.tensor_scalar(ll, vv, FMAX, -FMAX, ALU.min, ALU.max)
                        link(V.tensor_scalar(cc, vv, 1e4, -1e4, ALU.min, ALU.max))
                        V.scalar_tensor_tensor(ll, mm_, FMAX, ll, ALU.is_le, ALU.mult)
                        V.scalar_tensor_tensor(cc, mm_, FMAX, cc, ALU.is_gt, ALU.mult)\
                            .then_inc(z_done, 1)
                    if u:
                        w = u - 1
                        i = 2 * (w % 2) + 1
                        dve.wait_ge(p_full[i], b * 4 + w // 2 + 3)
                        dve.wait_ge(o_out[w % 2], (b * 4 + w // 2) * 16 + 16)
                        V.tensor_copy(zt[w % 2][:, 1, :], Pb[i][:, :]).then_inc(p_out[i], 1)
                assert here[0] == 2 + LINKS3, here[0]


W_IN = 16 * 11
LINKS = NT * 15
LINKS3 = NT


def metaformer(nc, D, out):
    f32, u32 = mybir.dt.float32, mybir.dt.uint32
    D["slots"] = nc.dram_tensor("slots", (NSLOT, CH), f32, kind="Internal").ap()
    D["ybuf"] = nc.dram_tensor("ybuf", (NSLOT, CH), f32, kind="Internal").ap()
    D["y1"] = nc.dram_tensor("y1", (TOKENS, CH), f32, kind="Internal").ap()
    with ExitStack() as ctx:
        keep = (ctx.enter_context(nc.sbuf_tensor("dlog", [128, TOKENS // 128, NE], f32)),
                ctx.enter_context(nc.sbuf_tensor("kept", [128, TOKENS // 128], f32)),
                ctx.enter_context(nc.sbuf_tensor("gidx", [128, TOKENS // 128], u32)))
        mixer_and_dispatch(nc, keep, D)
        experts(nc, D)
        combine(nc, keep, D, out)


def constants():
    import numpy as np
    con = np.zeros((128, NCON), np.float32)
    p = np.arange(128)
    con[:, slice(*CON["ident"])] = np.eye(128)
    con[:, slice(*CON["gmask"])] = p[:, None] // 8 == p[None, :] // 8
    con[:, slice(*CON["gm16"])] = p[:, None] // 8 == np.arange(16)[None, :]
    con[:, slice(*CON["carry0"])] = np.arange(NE)[None, :] * CAP - 1
    con[:, CON["row7"][0] + 7] = 1.0 / CH
    con[:, slice(*CON["rev"])] = NE - np.arange(NE)[None, :]
    return con


def zeros_and_ones():
    import numpy as np
    p, w = np.arange(128), np.zeros((128, 6, 128), np.float32)
    for c in range(4):
        w[16 * c + p // 8, c, p] = w[64 + 16 * c + p // 8, c, p] = 1.0
    w[:, 4] = p[:, None] <= p[None, :]
    w[:, 5] = 1.0
    return w.reshape(128, 6 * 128)


def lay_out(x, w_qkv, w_dw, w_pw, w_proj, gate_w, b1):
    import numpy as np
    ch = np.array([[24 * (16 * h + g) + 8 * "qkv".index(kind) + c for g in range(NG) for c in range(8)] for kind, h in CHUNKS])
    wq = np.asarray(w_qkv).reshape(768, CH)[ch]
    wq = wq.transpose(2, 0, 1).reshape(KC, 128, NCHUNK, 128).transpose(1, 0, 2, 3)
    wp = np.asarray(w_proj).reshape(CH, 512).T.reshape(4, 128, CH).transpose(1, 0, 2)
    pad = np.zeros((768, 11, 11), np.float32)
    pad[:, 3:8, 3:8] = np.asarray(w_dw).reshape(768, 5, 5)
    py, qa, qq = np.arange(4), np.arange(2), np.arange(4)
    idx = 4 * qa[None, :, None] + py[:, None, None] - qq[None, None, :] + 3
    dw = pad[ch][:, :, idx][:, :, :, :, :, idx]
    dw = dw.reshape(NCHUNK, NG, 8, 4, 2, 4, 4, 2, 4).transpose(0, 2, 3, 6, 1, 4, 7, 5, 8)
    dw = dw.reshape(NCHUNK, 128, NG, 64)
    pw = np.asarray(w_pw).reshape(768, 8)[ch].reshape(NCHUNK, NG, 8, 8)
    pw = np.broadcast_to(pw.transpose(3, 0, 1, 2)[:, None], (8, POS, NCHUNK, NG, 8)).reshape(128, NCHUNK, NG, 8)
    gw = np.asarray(gate_w).reshape(KC, 128, NE).transpose(1, 0, 2)
    return dict(x=np.asarray(x).reshape(B, CH, NTOK), wq=wq, wp=wp, dw=dw, pw=pw, gate_w=gw,
                b1=np.asarray(b1).reshape(NE, FT, 128).transpose(0, 2, 1))


def kernel(**inputs):
    import numpy as np
    import concourse.bacc as bacc
    from concourse.bass_utils import run_bass_kernel_spmd

    i = inputs
    arrays = lay_out(i["x"], i["L0_conv_w_qkv"], i["L0_conv_w_dw"], i["L0_conv_w_pw"], i["L0_conv_w_proj"],
                     i["L0_ffn_gate_w"], i["L0_ffn_b1"])
    for name in ("bn_gamma", "bn_beta", "bn_mean", "bn_var"):
        arrays[name] = np.asarray(i["L0_conv_" + name]).reshape(1, CH)
    arrays["gate_b"] = np.asarray(i["L0_ffn_gate_b"]).reshape(1, NE)
    arrays["w1"], arrays["w2"], arrays["b2"] = (np.asarray(i["L0_ffn_" + n]) for n in ("w1", "w2", "b2"))
    arrays["con"], arrays["zeros_and_ones"] = constants(), zeros_and_ones()
    arrays = {"in_" + k: np.ascontiguousarray(v) for k, v in arrays.items()}

    nc = bacc.Bacc("TRN2", target_bir_lowering=False, num_devices=1)
    D = {k[3:]: nc.dram_tensor(k, v.shape, mybir.dt.from_np(v.dtype), kind="ExternalInput").ap() for k, v in arrays.items()}
    out = nc.dram_tensor("out", (B, CH, NTOK), mybir.dt.float32, kind="ExternalOutput").ap()
    metaformer(nc, D, out)
    r = run_bass_kernel_spmd(nc, [arrays], core_ids=[0])
    return np.asarray(r.results[0]["out"]).reshape(B, CH, HW, HW)
```
